# Optimizing a Trainium2 kernel written in Bass

```python
import numpy as np
import jax
import jax.numpy as jnp

def _softmax(x, axis=-1):
    return jax.nn.softmax(x, axis=axis)

def _gelu(x):
    return jax.nn.gelu(x, approximate=True)

def _silu(x):
    return jax.nn.silu(x)

def _sigmoid(x):
    return jax.nn.sigmoid(x)

def _layernorm(x, axis=-1, eps=1e-05):
    m = jnp.mean(x, axis=axis, keepdims=True)
    v = jnp.var(x, axis=axis, keepdims=True)
    return (x - m) / jnp.sqrt(v + eps)

def _scatter_add(tgt, idx, src, axis=0):
    return tgt.at[idx].add(src)

def _segment_sum(src, seg, n):
    return jax.ops.segment_sum(src, seg, n)
kernel_name = 'mk_sandwich_d2_jaxref_r8_ef102c'

def setup_inputs(seed: int=0):
    np.random.seed(seed)
    _w = jnp.asarray

    def _L0_attn_setup():
        import jax, jax.numpy as jnp
        import numpy as np
        B, T, D = (4, 256, 128)
        H = 4
        K = D // H
        V = D // H
        M = 64
        GATE_LOGIT_NORMALIZER = 8.0
        NORM_EPS = 1e-05

        def _swish(x):
            return x * jax.nn.sigmoid(x)

        def _gsa_recurrence(q, k, v, s, g, scale):
            b, t, h, dk = q.shape
            dv = v.shape[-1]
            m = s.shape[-1]

            def step(carry, inp):
                hk, hv = carry
                q_t, k_t, v_t, s_t, g_t = inp
                ge = jnp.exp(g_t)
                hk = hk * ge[:, :, None, :] + k_t[..., :, None] * s_t[..., None, :]
                logits = jnp.einsum('bhk,bhkm->bhm', q_t * scale, hk)
                p = jax.nn.softmax(logits, axis=-1)
                hv = hv * ge[..., :, None] + s_t[..., :, None] * v_t[..., None, :]
                o_t = jnp.einsum('bhm,bhmv->bhv', p, hv)
                return ((hk, hv), o_t)
            init = (jnp.zeros((b, h, dk, m), q.dtype), jnp.zeros((b, h, m, dv), q.dtype))
            xs = tuple((jnp.moveaxis(a, 1, 0) for a in (q, k, v, s, g)))
            _, o = jax.lax.scan(step, init, xs)
            return jnp.moveaxis(o, 0, 1)
        key = jax.random.key(seed)
        ks = jax.random.split(key, 6)
        sc = lambda n: 1.0 / np.sqrt(n)
        return {'x': jax.random.normal(ks[0], (B, T, D), jnp.float32), 'Wq': jax.random.normal(ks[1], (D, H * K), jnp.float32) * sc(D), 'Wk': jax.random.normal(ks[2], (D, H * K), jnp.float32) * sc(D), 'Wv': jax.random.normal(ks[3], (D, H * V), jnp.float32) * sc(D), 'Wf': jax.random.normal(ks[4], (D, H * M), jnp.float32) * sc(D), 'g_norm_w': jnp.ones((V,), jnp.float32), 'Wo': jax.random.normal(ks[5], (H * V, D), jnp.float32) * sc(H * V)}
    _L0_attn_in = _L0_attn_setup()

    def _L0_ffn_setup():
        import jax, jax.numpy as jnp
        import numpy as np
        from jax import lax
        D = 128
        H = 176
        E = 8
        K = 2
        ROUTER_SCALE = 1.0

        def _expert(x, w1, b1, w3, b3, w2, b2):
            h = jax.nn.silu((x @ w1 + b1) * (x @ w3 + b3))
            return h @ w2 + b2
        key = jax.random.key(seed)
        ks = jax.random.split(key, 16)
        s = 0.02
        inp = {'x': jax.random.normal(ks[0], (2, 256, D), dtype=jnp.float32), 'gate_w': jax.random.normal(ks[1], (E, D), dtype=jnp.float32) * s, 'gate_b': jax.random.normal(ks[2], (E,), dtype=jnp.float32) * s, 'w1': jax.random.normal(ks[3], (E, D, H), dtype=jnp.float32) * s, 'b1': jax.random.normal(ks[4], (E, H), dtype=jnp.float32) * s, 'w3': jax.random.normal(ks[5], (E, D, H), dtype=jnp.float32) * s, 'b3': jax.random.normal(ks[6], (E, H), dtype=jnp.float32) * s, 'w2': jax.random.normal(ks[7], (E, H, D), dtype=jnp.float32) * s, 'b2': jax.random.normal(ks[8], (E, D), dtype=jnp.float32) * s, 'sw1': jax.random.normal(ks[9], (D, H), dtype=jnp.float32) * s, 'sb1': jax.random.normal(ks[10], (H,), dtype=jnp.float32) * s, 'sw3': jax.random.normal(ks[11], (D, H), dtype=jnp.float32) * s, 'sb3': jax.random.normal(ks[12], (H,), dtype=jnp.float32) * s, 'sw2': jax.random.normal(ks[13], (H, D), dtype=jnp.float32) * s, 'sb2': jax.random.normal(ks[14], (D,), dtype=jnp.float32) * s}
        return inp
    _L0_ffn_in = _L0_ffn_setup()

    def _L1_attn_setup():
        import jax, jax.numpy as jnp
        import numpy as np
        EMBED_DIM = 128
        NUM_HEADS = 16
        QKV_DIM = EMBED_DIM // NUM_HEADS
        BATCH = 4
        SEQ_LEN = 256
        key = jax.random.key(seed)
        k_x, k_wqkv, k_wout = jax.random.split(key, 3)
        scale_in = 1.0 / np.sqrt(EMBED_DIM)
        X = jax.random.normal(k_x, (BATCH, SEQ_LEN, EMBED_DIM), dtype=jnp.float32)
        W_qkv = jax.random.normal(k_wqkv, (EMBED_DIM, 3 * EMBED_DIM), dtype=jnp.float32) * scale_in
        b_qkv = jnp.zeros((3 * EMBED_DIM,), dtype=jnp.float32)
        W_out = jax.random.normal(k_wout, (EMBED_DIM, EMBED_DIM), dtype=jnp.float32) * scale_in
        b_out = jnp.zeros((EMBED_DIM,), dtype=jnp.float32)
        return {'X': X, 'W_qkv': W_qkv, 'b_qkv': b_qkv, 'W_out': W_out, 'b_out': b_out}
    _L1_attn_in = _L1_attn_setup()

    def _L1_ffn_setup():
        import jax, jax.numpy as jnp
        import numpy as np
        DIM = 128

        def _reference_tuple_inner(x, W_r, W_k, W_v, mu_r, mu_k):
            B, T, C = x.shape
            x_prev = jnp.concatenate([jnp.zeros((B, 1, C), x.dtype), x[:, :-1, :]], axis=1)
            xr = mu_r * x + (1.0 - mu_r) * x_prev
            xk = mu_k * x + (1.0 - mu_k) * x_prev
            r = jax.nn.sigmoid(jnp.einsum('btc,dc->btd', xr, W_r))
            k = jnp.einsum('btc,dc->btd', xk, W_k)
            k_act = jnp.square(jax.nn.relu(k))
            out = r * jnp.einsum('btc,dc->btd', k_act, W_v)
            new_state = x[:, -1, :]
            return (out, new_state)
        key = jax.random.key(seed)
        ks = jax.random.split(key, 6)
        B, T, C = (8, 256, DIM)
        x = jax.random.normal(ks[0], (B, T, C), dtype=jnp.float32)
        s = 1.0 / np.sqrt(C)
        W_r = jax.random.uniform(ks[1], (C, C), jnp.float32, -s, s)
        W_k = jax.random.uniform(ks[2], (C, C), jnp.float32, -s, s)
        W_v = jax.random.uniform(ks[3], (C, C), jnp.float32, -s, s)
        mu_r = jax.random.uniform(ks[4], (C,), jnp.float32)
        mu_k = jax.random.uniform(ks[5], (C,), jnp.float32)
        return {'x': x, 'W_r': W_r, 'W_k': W_k, 'W_v': W_v, 'mu_r': mu_r, 'mu_k': mu_k}
    _L1_ffn_in = _L1_ffn_setup()
    _d = {'L0_attn_x': _L0_attn_in['x'], 'L0_attn_Wq': _L0_attn_in['Wq'], 'L0_attn_Wk': _L0_attn_in['Wk'], 'L0_attn_Wv': _L0_attn_in['Wv'], 'L0_attn_Wf': _L0_attn_in['Wf'], 'L0_attn_g_norm_w': _L0_attn_in['g_norm_w'], 'L0_attn_Wo': _L0_attn_in['Wo'], 'L0_ffn_gate_w': _L0_ffn_in['gate_w'], 'L0_ffn_gate_b': _L0_ffn_in['gate_b'], 'L0_ffn_w1': _L0_ffn_in['w1'], 'L0_ffn_b1': _L0_ffn_in['b1'], 'L0_ffn_w3': _L0_ffn_in['w3'], 'L0_ffn_b3': _L0_ffn_in['b3'], 'L0_ffn_w2': _L0_ffn_in['w2'], 'L0_ffn_b2': _L0_ffn_in['b2'], 'L0_ffn_sw1': _L0_ffn_in['sw1'], 'L0_ffn_sb1': _L0_ffn_in['sb1'], 'L0_ffn_sw3': _L0_ffn_in['sw3'], 'L0_ffn_sb3': _L0_ffn_in['sb3'], 'L0_ffn_sw2': _L0_ffn_in['sw2'], 'L0_ffn_sb2': _L0_ffn_in['sb2'], 'L1_attn_W_qkv': _L1_attn_in['W_qkv'], 'L1_attn_b_qkv': _L1_attn_in['b_qkv'], 'L1_attn_W_out': _L1_attn_in['W_out'], 'L1_attn_b_out': _L1_attn_in['b_out'], 'L1_ffn_W_r': _L1_ffn_in['W_r'], 'L1_ffn_W_k': _L1_ffn_in['W_k'], 'L1_ffn_W_v': _L1_ffn_in['W_v'], 'L1_ffn_mu_r': _L1_ffn_in['mu_r'], 'L1_ffn_mu_k': _L1_ffn_in['mu_k']}
    _x0 = _d['L0_attn_x']
    _d['L0_attn_x'] = jax.random.normal(jax.random.fold_in(jax.random.key(seed), 1), (16, 512, 128), dtype=_x0.dtype)
    del _x0
    return _d

def reference(L0_attn_x, L0_attn_Wq, L0_attn_Wk, L0_attn_Wv, L0_attn_Wf, L0_attn_g_norm_w, L0_attn_Wo, L0_ffn_gate_w, L0_ffn_gate_b, L0_ffn_w1, L0_ffn_b1, L0_ffn_w3, L0_ffn_b3, L0_ffn_w2, L0_ffn_b2, L0_ffn_sw1, L0_ffn_sb1, L0_ffn_sw3, L0_ffn_sb3, L0_ffn_sw2, L0_ffn_sb2, L1_attn_W_qkv, L1_attn_b_qkv, L1_attn_W_out, L1_attn_b_out, L1_ffn_W_r, L1_ffn_W_k, L1_ffn_W_v, L1_ffn_mu_r, L1_ffn_mu_k):

    def _L0_attn_ref(x, Wq, Wk, Wv, Wf, g_norm_w, Wo):
        import jax, jax.numpy as jnp
        import numpy as np
        B, T, D = (4, 256, 128)
        H = 4
        K = D // H
        V = D // H
        M = 64
        GATE_LOGIT_NORMALIZER = 8.0
        NORM_EPS = 1e-05

        def _swish(x):
            return x * jax.nn.sigmoid(x)

        def _gsa_recurrence(q, k, v, s, g, scale):
            b, t, h, dk = q.shape
            dv = v.shape[-1]
            m = s.shape[-1]

            def step(carry, inp):
                hk, hv = carry
                q_t, k_t, v_t, s_t, g_t = inp
                ge = jnp.exp(g_t)
                hk = hk * ge[:, :, None, :] + k_t[..., :, None] * s_t[..., None, :]
                logits = jnp.einsum('bhk,bhkm->bhm', q_t * scale, hk)
                p = jax.nn.softmax(logits, axis=-1)
                hv = hv * ge[..., :, None] + s_t[..., :, None] * v_t[..., None, :]
                o_t = jnp.einsum('bhm,bhmv->bhv', p, hv)
                return ((hk, hv), o_t)
            init = (jnp.zeros((b, h, dk, m), q.dtype), jnp.zeros((b, h, m, dv), q.dtype))
            xs = tuple((jnp.moveaxis(a, 1, 0) for a in (q, k, v, s, g)))
            _, o = jax.lax.scan(step, init, xs)
            return jnp.moveaxis(o, 0, 1)
        b, t, d = x.shape
        q = _swish((x @ Wq).reshape(b, t, H, K))
        k = _swish((x @ Wk).reshape(b, t, H, K))
        v = (x @ Wv).reshape(b, t, H, V)
        f = jax.nn.log_sigmoid((x @ Wf).reshape(b, t, H, M)) / GATE_LOGIT_NORMALIZER
        s = 1.0 - jnp.exp(f)
        o = _gsa_recurrence(q, k, v, s, f, scale=K ** (-0.5))
        o = o * jax.lax.rsqrt(jnp.mean(o * o, axis=-1, keepdims=True) + NORM_EPS) * g_norm_w
        return o.reshape(b, t, H * V) @ Wo

    def _L0_ffn_ref(x, gate_w, gate_b, w1, b1, w3, b3, w2, b2, sw1, sb1, sw3, sb3, sw2, sb2):
        import jax, jax.numpy as jnp
        import numpy as np
        from jax import lax
        D = 128
        H = 176
        E = 8
        K = 2
        ROUTER_SCALE = 1.0

        def _expert(x, w1, b1, w3, b3, w2, b2):
            h = jax.nn.silu((x @ w1 + b1) * (x @ w3 + b3))
            return h @ w2 + b2
        shape = x.shape
        xf = x.reshape(-1, D)
        T = xf.shape[0]
        scores = jax.nn.softmax(xf @ gate_w.T, axis=-1)
        biased = scores + gate_b
        _, idx = lax.top_k(biased, K)
        w = jnp.take_along_axis(scores, idx, axis=-1) * ROUTER_SCALE
        rw = jnp.zeros((T, E), dtype=xf.dtype).at[jnp.arange(T)[:, None], idx].add(w)
        h = jax.nn.silu((jnp.einsum('td,edh->teh', xf, w1) + b1) * (jnp.einsum('td,edh->teh', xf, w3) + b3))
        oe = jnp.einsum('teh,ehd->ted', h, w2) + b2
        y = jnp.einsum('te,ted->td', rw, oe)
        z = _expert(xf, sw1, sb1, sw3, sb3, sw2, sb2)
        return (y + z).reshape(shape)

    def _L1_attn_ref(X, W_qkv, b_qkv, W_out, b_out):
        import jax, jax.numpy as jnp
        import numpy as np
        EMBED_DIM = 128
        NUM_HEADS = 16
        QKV_DIM = EMBED_DIM // NUM_HEADS
        BATCH = 4
        SEQ_LEN = 256
        B, S, E = X.shape
        qkv = (jnp.einsum('bse,ef->bsf', X, W_qkv) + b_qkv).reshape(B, S, NUM_HEADS, 3 * QKV_DIM)
        q, k, v = jnp.split(qkv, 3, axis=-1)
        attn = jnp.einsum('bqhd,bkhd->bhqk', q, k) / jnp.sqrt(jnp.float32(QKV_DIM)).astype(X.dtype)
        attn = jax.nn.softmax(attn, axis=-1)
        out = jnp.einsum('bhqk,bkhd->bqhd', attn, v).reshape(B, S, NUM_HEADS * QKV_DIM)
        out = jnp.einsum('bse,ef->bsf', out, W_out) + b_out
        return out

    def _L1_ffn_ref(x, W_r, W_k, W_v, mu_r, mu_k):
        import jax, jax.numpy as jnp
        import numpy as np
        DIM = 128

        def _reference_tuple_inner(x, W_r, W_k, W_v, mu_r, mu_k):
            B, T, C = x.shape
            x_prev = jnp.concatenate([jnp.zeros((B, 1, C), x.dtype), x[:, :-1, :]], axis=1)
            xr = mu_r * x + (1.0 - mu_r) * x_prev
            xk = mu_k * x + (1.0 - mu_k) * x_prev
            r = jax.nn.sigmoid(jnp.einsum('btc,dc->btd', xr, W_r))
            k = jnp.einsum('btc,dc->btd', xk, W_k)
            k_act = jnp.square(jax.nn.relu(k))
            out = r * jnp.einsum('btc,dc->btd', k_act, W_v)
            new_state = x[:, -1, :]
            return (out, new_state)
        return _reference_tuple_inner(x, W_r, W_k, W_v, mu_r, mu_k)[0]
    x = L0_attn_x
    x = x + _layernorm(_L0_attn_ref(_layernorm(x, axis=-1), L0_attn_Wq, L0_attn_Wk, L0_attn_Wv, L0_attn_Wf, L0_attn_g_norm_w, L0_attn_Wo), axis=-1)
    x = x + _layernorm(_L0_ffn_ref(_layernorm(x, axis=-1), L0_ffn_gate_w, L0_ffn_gate_b, L0_ffn_w1, L0_ffn_b1, L0_ffn_w3, L0_ffn_b3, L0_ffn_w2, L0_ffn_b2, L0_ffn_sw1, L0_ffn_sb1, L0_ffn_sw3, L0_ffn_sb3, L0_ffn_sw2, L0_ffn_sb2), axis=-1)
    x = x + _layernorm(_L1_attn_ref(_layernorm(x, axis=-1), L1_attn_W_qkv, L1_attn_b_qkv, L1_attn_W_out, L1_attn_b_out), axis=-1)
    x = x + _layernorm(_L1_ffn_ref(_layernorm(x, axis=-1), L1_ffn_W_r, L1_ffn_W_k, L1_ffn_W_v, L1_ffn_mu_r, L1_ffn_mu_k), axis=-1)
    return x

_drawn_inputs = setup_inputs


def setup_inputs(seed=0):
    import zlib

    import numpy as np

    out = dict(_drawn_inputs(seed))
    spreads = {'L0_attn_g_norm_w': (1.0, 0.2), 'L1_attn_b_qkv': (0.0, 0.1), 'L1_attn_b_out': (0.0, 0.1)}
    factors = {'L0_attn_Wq': 6.57,
     'L0_attn_Wk': 6.031,
     'L0_ffn_b1': 8.0,
     'L0_ffn_b3': 8.0,
     'L0_ffn_sb1': 3.819,
     'L0_ffn_sb3': 4.261}
    for name, (base, spread) in spreads.items():
        noise = np.random.default_rng([zlib.crc32(name.encode()), seed]).standard_normal(out[name].shape)
        drawn = base * np.exp(spread * noise) if base else spread * noise
        out[name] = jnp.asarray(drawn.astype(out[name].dtype))
    for name, factor in factors.items():
        out[name] = (out[name] * factor).astype(out[name].dtype)
    return out
```

```python
from contextlib import ExitStack

import concourse.bass as bass
from concourse import mybir

ALU = mybir.AluOpType
ACT = mybir.ActivationFunctionType
AX = mybir.AxisListType
F32 = mybir.dt.float32
BF16 = mybir.dt.bfloat16

P = 128
D = 128
SEQ = 512
TILES = SEQ // P
EPS = 1e-5


class LayerSemaphores:

    def __init__(self, nc):
        self.nc, self.held = nc, []

    def get(self, name):
        self.held.append(self.nc.alloc_semaphore(name))
        return self.held[-1]

    def __enter__(self):
        return self

    def __exit__(self, *_):
        self.nc.clear_and_free_semaphores(self.held)
        self.nc.all_engine_barrier()


class Common:
    pass


def group_loop(eng, groups, body):
    with eng.Fori(0, groups // 2 - 1) as i:
        for parity in range(2):
            body(2 * i + parity, parity, False)
    for parity in range(2):
        body(groups - 2 + parity, parity, parity == 1)


def ln_stats(dve, c, source, bufs, link):
    for j in range(TILES):
        ins = dve.bn_stats(bufs.stats[:, j, :], source(j))
    link(ins)
    dve.memset(c.spare[:, :], 0.0)
    for j in range(TILES):
        ins = dve.bn_aggr(bufs.meanvar[:, j, :], bufs.stats[:, j, :])
    link(ins)
    return dve.tensor_scalar(bufs.vareps[:, :], bufs.meanvar[:, :, 1], EPS, None, ALU.add)


def build_common(nc, ctx, x_in):
    c = Common()
    c.nc = nc
    c.groups = x_in.shape[0]
    c.x_res = ctx.enter_context(nc.sbuf_tensor("x_res", [P, c.groups * TILES, D], F32))
    c.ident = ctx.enter_context(nc.sbuf_tensor("ident", [P, P], F32))
    c.neg_half = ctx.enter_context(nc.sbuf_tensor("neg_half", [P, TILES], F32))
    c.zero = ctx.enter_context(nc.sbuf_tensor("zero", [P, 1], F32))
    c.spare = ctx.enter_context(nc.sbuf_tensor("spare", [P, 1], F32))
    c.loaded_first = ctx.enter_context(nc.semaphore("x_first_loaded"))
    c.loaded_rest = ctx.enter_context(nc.semaphore("x_rest_loaded"))
    c.consts = ctx.enter_context(nc.semaphore("consts_ready"))
    c.ident_zero = ctx.enter_context(nc.semaphore("ident_zeroed"))
    tokens = x_in.rearrange("b (j p) d -> p (b j) d", p=P)
    first = 2 * TILES
    with nc.Block() as block:
        @block.sync
        def _(sp):
            sp.dma_start(c.x_res[:, 0:first, :], tokens[:, 0:first, :]).then_inc(c.loaded_first, 16)
            sp.dma_start(c.x_res[:, first:, :], tokens[:, first:, :]).then_inc(c.loaded_rest, 16)

        @block.gpsimd
        def _(pool):
            pool.memset(c.neg_half[:, :], -0.5).then_inc(c.consts, 1)
            pool.memset(c.zero[:, :], 0.0).then_inc(c.consts, 1)
            pool.memset(c.ident[:, :], 0.0).then_inc(c.ident_zero, 1)
            pool.wait_ge(c.ident_zero, 1)
            pool.affine_select(out=c.ident[:, :], in_=c.ident[:, :], compare_op=ALU.not_equal, fill=1.0,
                               base=0, pattern=[[-1, P]], channel_multiplier=1).then_inc(c.consts, 1)
    return c


def tile_of(c, g, j):
    return c.x_res[:, bass.ds(g * TILES + j, 1), :].rearrange("p a d -> p (a d)")


def group_of(c, g):
    return c.x_res[:, bass.ds(g * TILES, TILES), :]


class LnBufs:
    def __init__(self, sb, name):
        self.stats = sb(name + "_stats", [P, TILES, 6], F32)
        self.meanvar = sb(name + "_meanvar", [P, TILES, 2], F32)
        self.vareps = sb(name + "_vareps", [P, TILES], F32)
        self.rstd = sb(name + "_rstd", [P, TILES], F32)


def channel_mix(c, W_r, W_k, W_v, mu_r, mu_k, out):
    nc = c.nc
    G = c.groups
    with ExitStack() as ctx:
        semaphores = ctx.enter_context(LayerSemaphores(nc))

        def sb(name, shape, dt):
            return ctx.enter_context(nc.sbuf_tensor("cm_" + name, shape, dt))

        def sem(name):
            return semaphores.get("cm_" + name)

        def bank(name):
            return ctx.enter_context(nc.psum_tensor("cm_" + name, [P, 512], F32))

        w_raw = sb("w_raw", [P, 3, D], F32)
        w_t = sb("w_t", [P, 3, D], F32)
        mu = sb("mu", [P, 2], F32)
        one_minus_mu = sb("one_minus_mu", [P, 2], F32)
        pre, post = LnBufs(sb, "pre"), LnBufs(sb, "post")
        xn = sb("xn", [P, 2, TILES, D], F32)
        xn_t = sb("xn_t", [P, 2, SEQ + 1], F32)
        scaled = sb("scaled", [P, 2, 2, SEQ], F32)
        mixed = sb("mixed", [P, 2, 2, SEQ], F32)
        k_relu = sb("k_relu", [P, SEQ], F32)
        k_act = sb("k_act", [P, 2, SEQ], F32)
        r_sb = sb("r_sb", [P, 2, SEQ], F32)
        y = sb("y", [P, TILES, D], F32)
        yn = sb("yn", [P, TILES, D], F32)
        xn_ps = [bank(f"xn_ps{i}") for i in range(2)]
        r_ps = [bank(f"r_ps{i}") for i in range(2)]
        k_ps = bank("k_ps")
        v_ps = [bank(f"v_ps{i}") for i in range(2)]
        w_ps = bank("w_ps")

        w_loaded, w_turned, w_ready = sem("w_loaded"), sem("w_turned"), sem("w_ready")
        mu_loaded, mu_ready = sem("mu_loaded"), sem("mu_ready")
        edge_zeroed = sem("edge_zeroed")
        pre_var, pre_rstd = sem("pre_var"), sem("pre_rstd")
        post_var, post_rstd = sem("post_var"), sem("post_rstd")
        xn_ready, xn_turned = sem("xn_ready"), sem("xn_turned")
        xn_t_ready, scaled_ready, mixed_ready = sem("xn_t_ready"), sem("scaled_ready"), sem("mixed_ready")
        k_done, k_relu_ready, k_act_ready = sem("k_done"), sem("k_relu_ready"), sem("k_act_ready")
        r_done, r_ready, v_done = sem("r_done"), sem("r_ready"), sem("v_done")
        y_ready = sem("y_ready")
        x_done, stored = sem("x_done"), sem("stored")
        chain = sem("dve_chain")
        LINKS = 6

        block = ctx.enter_context(nc.Block())
        out_tokens = out.rearrange("b (j p) d -> b p j d", p=P)

        @block.sync
        def _(sp):
            for n, w in enumerate((W_r, W_k, W_v)):
                sp.dma_start(w_raw[:, n, :], w).then_inc(w_loaded, 16)
            for n, m in enumerate((mu_r, mu_k)):
                sp.dma_start(mu[:, n:n + 1], m.rearrange("(p a) -> p a", a=1)).then_inc(mu_loaded, 16)
            with sp.Fori(0, G) as g:
                sp.wait_ge(x_done, g + 1)
                sp.dma_start(out_tokens[bass.ds(g, 1), :, :, :].rearrange("b p j d -> (b p) j d"),
                             group_of(c, g)).then_inc(stored, 16)
            sp.wait_ge(stored, 16 * G)

        @block.gpsimd
        def _(pool):
            def body(g, parity, last):
                if not last:
                    pool.wait_ge(pre_var, g + 2)
                    pool.tensor_tensor(pre.rstd[:, :], pre.vareps[:, :], c.neg_half[:, :],
                                       ALU.pow).then_inc(pre_rstd, 1)
                pool.wait_ge(post_var, g + 1)
                pool.tensor_tensor(post.rstd[:, :], post.vareps[:, :], c.neg_half[:, :],
                                   ALU.pow).then_inc(post_rstd, 1)

            pool.wait_ge(pre_var, 1)
            pool.tensor_tensor(pre.rstd[:, :], pre.vareps[:, :], c.neg_half[:, :], ALU.pow).then_inc(pre_rstd, 1)
            group_loop(pool, G, body)

        @block.scalar
        def _(act):
            act.wait_ge(w_turned, 1)
            act.copy(w_t[:, :, :].rearrange("p n d -> p (n d)"), w_ps[:, 0:3 * D]).then_inc(w_ready, 1)
            act.wait_ge(mu_loaded, 32)
            act.activation(one_minus_mu[:, :], mu[:, :], ACT.Copy, bias=1.0, scale=-1.0).then_inc(mu_ready, 1)

            def body(g, parity, last):
                act.wait_ge(xn_turned, g + 1)
                if isinstance(g, int) and g < 2:
                    pass
                act.wait_ge(mixed_ready, 2 * g)
                act.copy(xn_t[:, parity, 1:SEQ + 1], xn_ps[parity][:, :]).then_inc(xn_t_ready, 1)
                for n in range(2):
                    act.activation(scaled[:, parity, n, :], xn_ps[parity][:, :], ACT.Copy,
                                   scale=mu[:, n:n + 1]).then_inc(scaled_ready, 1)
                act.wait_ge(k_done, g + 1)
                act.wait_ge(k_act_ready, g)
                act.activation(k_relu[:, :], k_ps[:, :], ACT.Relu).then_inc(k_relu_ready, 1)
                act.wait_ge(r_done, g + 1)
                act.wait_ge(y_ready, g)
                act.activation(r_sb[:, parity, :], r_ps[parity][:, :], ACT.Sigmoid).then_inc(r_ready, 1)

            group_loop(act, G, body)

        @block.tensor
        def _(pe):
            pe.wait_ge(c.consts, 3)
            pe.wait_ge(w_loaded, 48)
            for n in range(3):
                mm = pe.transpose(w_ps[:, n * D:(n + 1) * D], w_raw[:, n, :], c.ident[:, :])
            mm.then_inc(w_turned, 1)

            def turn(g, parity):
                pe.wait_ge(xn_ready, g + 1)
                pe.wait_ge(scaled_ready, 2 * g)
                for j in range(TILES):
                    mm = pe.transpose(xn_ps[parity][:, j * P:(j + 1) * P], xn[:, parity, j, :], c.ident[:, :])
                mm.then_inc(xn_turned, 1)

            turn(0, 0)
            pe.wait_ge(w_ready, 1)

            def body(g, parity, last):
                pe.wait_ge(mixed_ready, 2 * g + 2)
                pe.wait_ge(k_act_ready, g)
                pe.matmul(k_ps[:, :], w_t[:, 1, :], mixed[:, parity, 1, :], start=True, stop=True).then_inc(k_done, 1)
                pe.wait_ge(y_ready, g)
                for j in range(TILES):
                    mm = pe.matmul(r_ps[parity][:, j * P:(j + 1) * P], mixed[:, parity, 0, j * P:(j + 1) * P],
                                   w_t[:, 0, :], start=True, stop=True)
                mm.then_inc(r_done, 1)
                if not last:
                    turn(g + 1, 1 - parity)
                pe.wait_ge(k_act_ready, g + 1)
                for j in range(TILES):
                    mm = pe.matmul(v_ps[parity][:, j * P:(j + 1) * P], k_act[:, parity, j * P:(j + 1) * P],
                                   w_t[:, 2, :], start=True, stop=True)
                mm.then_inc(v_done, 1)

            group_loop(pe, G, body)

        @block.vector
        def _(dve):
            state = {"base": 0, "k": 0}

            def link(ins):
                ins.then_inc(chain, 1)
                state["k"] += 1
                dve.wait_ge(chain, state["base"] + state["k"])

            def pre_norm(g, parity):
                ln_stats(dve, c, lambda j: tile_of(c, g, j), pre, link).then_inc(pre_var, 1)
                dve.wait_ge(pre_rstd, g + 1)
                dve.wait_ge(xn_turned, g)
                for j in range(TILES):
                    ins = dve.tensor_scalar(xn[:, parity, j, :], tile_of(c, g, j), pre.meanvar[:, j, 0:1],
                                            pre.rstd[:, j:j + 1], ALU.subtract, ALU.mult)
                ins.then_inc(xn_ready, 1)

            dve.memset(xn_t[:, :, 0:1], 0.0).then_inc(edge_zeroed, 1)
            dve.wait_ge(edge_zeroed, 1)
            dve.wait_ge(c.loaded_first, 16)
            dve.wait_ge(c.loaded_rest, 16)
            dve.wait_ge(mu_ready, 1)
            pre_norm(0, 0)
            first_links = state["k"]

            def body(g, parity, last):
                state["base"], state["k"] = first_links + g * LINKS, 0
                dve.wait_ge(xn_t_ready, g + 1)
                dve.wait_ge(v_done, g)
                for n in (1, 0):
                    dve.wait_ge(scaled_ready, 2 * g + n + 1)
                    dve.scalar_tensor_tensor(out=mixed[:, parity, n, :], in0=xn_t[:, parity, 0:SEQ],
                                             scalar=one_minus_mu[:, n:n + 1], in1=scaled[:, parity, n, :],
                                             op0=ALU.mult, op1=ALU.add).then_inc(mixed_ready, 1)
                dve.wait_ge(k_relu_ready, g + 1)
                dve.scalar_tensor_tensor(out=k_act[:, parity, :], in0=k_ps[:, :], scalar=0.0, in1=k_relu[:, :],
                                         op0=ALU.max, op1=ALU.mult).then_inc(k_act_ready, 1)
                if not last:
                    pre_norm(g + 1, 1 - parity)
                dve.wait_ge(v_done, g + 1)
                dve.wait_ge(r_ready, g + 1)
                ins = dve.tensor_tensor(y[:, :, :].rearrange("p j d -> p (j d)"), r_sb[:, parity, :],
                                        v_ps[parity][:, :], ALU.mult)
                ins.then_inc(y_ready, 1)
                dve.wait_ge(y_ready, g + 1)
                ln_stats(dve, c, lambda j: y[:, j, :], post, link).then_inc(post_var, 1)
                dve.wait_ge(post_rstd, g + 1)
                for j in range(TILES):
                    ins = dve.tensor_scalar(yn[:, j, :], y[:, j, :], post.meanvar[:, j, 0:1],
                                            post.rstd[:, j:j + 1], ALU.subtract, ALU.mult)
                link(ins)
                ins = dve.tensor_tensor(group_of(c, g), group_of(c, g), yn[:, :, :], ALU.add)
                ins.then_inc(x_done, 1)
                dve.wait_ge(x_done, g + 1)
                if last:
                    return
                while state["k"] < LINKS:
                    link(dve.tensor_copy(post.stats[:, 0, 0:1], post.stats[:, 0, 0:1]))
                assert state["k"] == LINKS, state["k"]

            group_loop(dve, G, body)


def softmax_attention(c, W_qkv, b_qkv, W_out, b_out, scratch):
    nc = c.nc
    G = c.groups
    H = 16
    DH = D // H
    QUADS = H // 4
    HALF = H // 2
    PARTS = 3
    ROWS = PARTS * PARTS * DH
    ROWS_MAX = ROWS + PARTS
    VW = DH + 1
    SCALE = float(DH) ** -0.5
    A_N = H * TILES
    B_N = H * TILES // 2

    with ExitStack() as ctx:
        semaphores = ctx.enter_context(LayerSemaphores(nc))

        def sb(name, shape, dt):
            return ctx.enter_context(nc.sbuf_tensor("sa_" + name, shape, dt))

        def sem(name):
            return semaphores.get("sa_" + name)

        def bank(name, n=1):
            return ctx.enter_context(nc.psum_tensor("sa_" + name, [P, 512 * n], F32))

        w_raw = sb("w_raw", [P, 3 * D], F32)
        w_q, w_k, w_v = (sb(n, [P, D], F32) for n in ("w_q", "w_k", "w_v"))
        w_o = sb("w_o", [P, D], F32)
        bias_qk = sb("bias_qk", [P, 2], F32)
        bias_v = sb("bias_v", [P, 3 * D], F32)
        bias_o = sb("bias_o", [P, D], F32)
        pre, post = LnBufs(sb, "pre"), LnBufs(sb, "post")
        xn = sb("xn", [P, TILES, D], F32)
        xn_t = sb("xn_t", [P, 2, SEQ], F32)
        qk = sb("qk", [P, 2, SEQ], F32)
        rest = sb("rest", [P, 2, SEQ], F32)
        parts = sb("parts", [P, 2, PARTS, SEQ], BF16)
        q_rows = sb("q_rows", [ROWS_MAX, 2, H, SEQ], BF16)
        k_rows = sb("k_rows", [ROWS_MAX, 2, H, SEQ], BF16)
        v_one = sb("v_one", [P, 2, TILES, H, VW], F32)
        maxima = sb("maxima", [P, 2, A_N], F32)
        neg_max = sb("neg_max", [32, D], F32)
        max_rest = sb("max_rest", [32, D], F32)
        max_parts = sb("max_parts", [32, PARTS, D], BF16)
        probs = sb("probs", [P, 8, TILES, SEQ], F32)
        o_t = sb("o_t", [P, 2, SEQ], F32)
        rsum = sb("rsum", [P, TILES, 4], F32)
        attn = sb("attn", [P, TILES, H, DH], F32)
        attn_t = sb("attn_t", [P, SEQ], F32)
        y = sb("y", [P, TILES, D], F32)

        a_ps = [bank(f"a_ps{i}") for i in range(2)]
        b_ps = [bank(f"b_ps{i}", 2) for i in range(2)]
        o_ps = bank("o_ps")
        small = bank("small")

        w_loaded, w_ready, bias_ready = sem("w_loaded"), sem("w_ready"), sem("bias_ready")
        edges_set, o_cleared = sem("edges_set"), sem("o_cleared")
        pre_var, pre_rstd = sem("pre_var"), sem("pre_rstd")
        post_var, post_rstd = sem("post_var"), sem("post_rstd")
        xn_ready = sem("xn_ready")
        filled = {n: sem(n + "_filled") for n in ("xt", "q", "k", "v", "mx", "ot", "at", "y")}
        taken = {n: sem(n + "_taken") for n in ("xt", "q", "k", "v", "mx", "ot", "at", "y")}
        per_seq = {"xt": 1, "q": 1, "k": 1, "v": 1, "mx": 2, "ot": QUADS, "at": 1, "y": 1}
        split = sem("split_steps")
        max_split = sem("max_split_steps")
        parts_stored, max_stored = sem("parts_stored"), sem("max_stored")
        rows_loaded = [[sem(f"rows_loaded{i}{n}") for n in range(2)] for i in range(2)]
        max_loaded = sem("max_loaded")
        a_filled, a_taken = sem("a_filled"), sem("a_taken")
        b_filled, exp_done = sem("b_filled"), sem("exp_done")
        pv_done, o_taken = sem("pv_done"), sem("o_taken")
        x_done = sem("x_done")
        chain = sem("dve_chain")

        parts_dram, max_dram = scratch
        block = ctx.enter_context(nc.Block())

        @block.sync
        def _(sp):
            sp.dma_start(w_raw[:, :], W_qkv).then_inc(w_loaded, 16)
            sp.dma_start(w_o[:, :], W_out).then_inc(w_loaded, 16)
            per_head = b_qkv.rearrange("(h c d) -> c d h", h=H, c=3)
            for n in range(2):
                for d in range(DH):
                    sp.dma_start(bias_qk[d * H:(d + 1) * H, n:n + 1],
                                 per_head[n, d, :].rearrange("(h a) -> h a", a=1),
                                 allow_slow_non_contiguous=True).then_inc(w_loaded, 16)
            sp.dma_start(bias_v[:, :], b_qkv.partition_broadcast(P)).then_inc(w_loaded, 16)
            sp.dma_start(bias_o[:, :], b_out.partition_broadcast(P)).then_inc(w_loaded, 16)

            def value(v):
                return v if isinstance(v, int) else sp.snap(v)

            def values_of_parts(g, parity):
                return value(48 * (g - parity)), value(4 * (g + 1)), value(32 * (g + 1))

            def store_parts(parity, again, loads, splits):
                if again:
                    for half in range(2):
                        sp.wait_ge(rows_loaded[parity][half], loads)
                sp.wait_ge(split, splits)
                for n in range(2):
                    sp.dma_start(parts_dram[parity, n].rearrange("i c t -> c i t"), parts[:, n, :, :])\
                      .then_inc(parts_stored, 16)

            def load_rows(parity, half, stores, reads):
                if stores is not None:
                    sp.wait_ge(parts_stored, stores)
                if reads is not None:
                    sp.wait_ge(b_filled, reads)
                heads = slice(half * HALF, (half + 1) * HALF)
                q_src, k_src = (parts_dram[parity, n].rearrange("i (d h) t -> i d h t", h=H) for n in range(2))
                for i in range(PARTS):
                    sp.dma_start(q_rows[i * PARTS * DH:(i + 1) * PARTS * DH, parity, heads, :],
                                 q_src.rearrange("i d h t -> (i d) h t")[:, heads, :])\
                      .then_inc(rows_loaded[parity][half], 16)
                    sp.dma_start(k_rows[i * PARTS * DH:(i + 1) * PARTS * DH, parity, heads, :],
                                 k_src[i][:, heads, :].unsqueeze(0).broadcast_to([PARTS, DH, HALF, SEQ]))\
                      .then_inc(rows_loaded[parity][half], 16)

            def values_of_max(n):
                return value(4 * n + 4), value(16 * n - 16), value(16 * n + 16)

            def load_max(parity, half, again, splits, loads, stores):
                sp.wait_ge(max_split, splits)
                if again:
                    sp.wait_ge(max_loaded, loads)
                sp.dma_start(max_dram[half].rearrange("i a t -> a i t"), max_parts[:, :, :]).then_inc(max_stored, 16)
                sp.wait_ge(max_stored, stores)
                sp.dma_start(q_rows[ROWS:ROWS_MAX, parity, half * HALF:(half + 1) * HALF, :],
                             max_dram[half].rearrange("i (h q) t -> i h (q t)", q=TILES)).then_inc(max_loaded, 16)

            sp.wait_ge(edges_set, 2)
            for g in range(2):
                store_parts(g, False, 0, 4 * (g + 1))
                for half in range(2):
                    load_rows(g, half, 32 * (g + 1) if half == 0 else None, None)
            load_max(0, 0, False, *values_of_max(0))

            def body(g, parity, ok):
                reads = [value(B_N * g + B_N // 2 * (half + 1)) for half in range(2)]
                loads, splits, stores = values_of_parts(g + 2, parity)
                max_now, max_next = values_of_max(2 * g + 1), values_of_max(2 * g + 2)
                if ok(0):
                    load_max(parity, 1, not isinstance(g, int) or g > 0, *max_now)
                if ok(2):
                    store_parts(parity, True, loads, splits)
                    load_rows(parity, 0, stores, reads[0])
                if ok(1):
                    load_max(1 - parity, 0, True, *max_next)
                if ok(2):
                    load_rows(parity, 1, None, reads[1])

            turns(sp, G, body)

        @block.gpsimd
        def _(pool):
            def rstd(bufs, var, done, g):
                pool.wait_ge(var, g + 1)
                pool.tensor_tensor(bufs.rstd[:, :], bufs.vareps[:, :], c.neg_half[:, :], ALU.pow).then_inc(done, 1)

            def zeros(*shape):
                return c.zero[:, :].unsqueeze(1).broadcast_to([P, *shape])

            def split_qk(g):
                pool.wait_ge(taken["q"], g + 1)
                pool.wait_ge(taken["k"], g + 1)
                if not (isinstance(g, int) and g == 0):
                    pool.wait_ge(parts_stored, 32 * g)
                pool.tensor_tensor(parts[:, :, 0, :], qk[:, :, :], zeros(2, SEQ), ALU.add).then_inc(split, 1)
                pool.wait_ge(split, 4 * g + 1)
                pool.tensor_tensor(rest[:, :, :], qk[:, :, :], parts[:, :, 0, :], ALU.subtract).then_inc(split, 1)
                pool.wait_ge(split, 4 * g + 2)
                pool.tensor_tensor(parts[:, :, 1, :], rest[:, :, :], zeros(2, SEQ), ALU.add).then_inc(split, 1)
                pool.wait_ge(split, 4 * g + 3)
                pool.tensor_tensor(parts[:, :, 2, :], rest[:, :, :], parts[:, :, 1, :], ALU.subtract).then_inc(split, 1)

            def split_max(g, half):
                n = 2 * g + half
                pool.wait_ge(taken["mx"], n + 1)
                if not (isinstance(n, int) and n == 0):
                    pool.wait_ge(max_stored, 16 * n)
                pool.tensor_tensor(max_parts[:, 0, :], neg_max[:, :], c.zero[0:32, :].broadcast_to([32, D]), ALU.add).then_inc(max_split, 1)
                pool.wait_ge(max_split, 4 * n + 1)
                pool.tensor_tensor(max_rest[:, :], neg_max[:, :], max_parts[:, 0, :], ALU.subtract).then_inc(max_split, 1)
                pool.wait_ge(max_split, 4 * n + 2)
                pool.tensor_tensor(max_parts[:, 1, :], max_rest[:, :], c.zero[0:32, :].broadcast_to([32, D]), ALU.add).then_inc(max_split, 1)
                pool.wait_ge(max_split, 4 * n + 3)
                pool.tensor_tensor(max_parts[:, 2, :], max_rest[:, :], max_parts[:, 1, :], ALU.subtract).then_inc(max_split, 1)

            pool.wait_ge(c.consts, 3)
            pool.memset(v_one[:, :, :, :, DH:VW], 1.0).then_inc(edges_set, 1)
            pool.wait_ge(edges_set, 1)
            pool.memset(k_rows[64:ROWS_MAX, :, :, :], 1.0).then_inc(edges_set, 1)
            pool.wait_ge(edges_set, 2)
            for g in range(2):
                rstd(pre, pre_var, pre_rstd, g)
                split_qk(g)
            split_max(0, 0)

            def body(g, parity, ok):
                if ok(0):
                    split_max(g, 1)
                if ok(2):
                    rstd(pre, pre_var, pre_rstd, g + 2)
                    split_qk(g + 2)
                if ok(-1):
                    rstd(post, post_var, post_rstd, g - 1)
                if ok(1):
                    split_max(g + 1, 0)

            turns(pool, G, body)

        @block.scalar
        def _(act):
            act.wait_ge(w_loaded, 16 * 20)
            act.mul(bias_qk[:, 0:1], bias_qk[:, 0:1], SCALE).then_inc(bias_ready, 1)
            act.wait_ge(bias_ready, 1)

            def copy_xt(g, parity):
                act.wait_ge(filled["xt"], g + 1)
                if not (isinstance(g, int) and g < 2):
                    act.wait_ge(filled["v"], g - 1)
                act.copy(xn_t[:, parity, :], small[:, :]).then_inc(taken["xt"], 1)

            def copy_qk(g, n):
                name = "qk"[n]
                act.wait_ge(filled[name], g + 1)
                if not (isinstance(g, int) and g == 0):
                    act.wait_ge(split, 4 * g)
                act.activation(qk[:, n, :], small[:, :], ACT.Identity, bias=bias_qk[:, n:n + 1],
                               scale=SCALE if n == 0 else 1.0).then_inc(taken[name], 1)

            def exps(g, parity, h, n):
                act.wait_ge(b_filled, B_N * g + 2 * h + n + 1)
                if h % 4 == 0 and n == 0:
                    wait_past(act, pv_done, g, QUADS, h // 4 - 1)
                act.activation(probs[:, h % 8, 2 * n:2 * n + 2, :].rearrange("p a t -> p (a t)"),
                               b_ps[n][:, :], ACT.Exp).then_inc(exp_done, 1)

            def take_o(g, quad):
                act.wait_ge(pv_done, QUADS * g + quad + 1)
                wait_past(act, filled["ot"], g, QUADS, quad - 1)
                act.copy(o_t[:, quad % 2, :], o_ps[:, :]).then_inc(o_taken, 1)

            for g in range(2):
                copy_xt(g, g)
                copy_qk(g, 0)
                copy_qk(g, 1)

            def body(g, parity, ok):
                for s in range(H):
                    if ok(0):
                        exps(g, parity, s, 0)
                    if s == 3 and ok(2):
                        copy_xt(g + 2, parity)
                    if s == 3 and ok(-1):
                        take_o(g - 1, 3)
                    if s == 5 and ok(2):
                        copy_qk(g + 2, 0)
                    if s == 6 and ok(2):
                        copy_qk(g + 2, 1)
                    if s == 7 and ok(-1):
                        act.wait_ge(filled["at"], g)
                        wait_past(act, filled["y"], g, 1, -1)
                        act.copy(attn_t[:, :], small[:, :]).then_inc(taken["at"], 1)
                    if s in (7, 11, 15) and ok(0):
                        take_o(g, s // 4 - 1)
                    if ok(0):
                        exps(g, parity, s, 1)

            turns(act, G, body)

        @block.tensor
        def _(pe):
            last = [None, None]

            def small_free():
                if last[0] is not None:
                    pe.wait_ge(taken[last[0]], last[1])

            def use(name, ins, g, n=0):
                ins.then_inc(filled[name], 1)
                last[:] = [name, g * per_seq[name] + n + 1]

            def turn_x(g, parity):
                pe.wait_ge(xn_ready, g + 1)
                small_free()
                for j in range(TILES):
                    mm = pe.transpose(small[:, j * P:(j + 1) * P], xn[:, j, :], c.ident[:, :])
                use("xt", mm, g)

            def project_qk(g, parity, n):
                pe.wait_ge(taken["xt"], g + 1)
                small_free()
                use("qk"[n], pe.matmul(small[:, :], (w_q, w_k)[n][:, :], xn_t[:, parity, :], start=True, stop=True), g)

            def project_v(g, parity):
                pe.wait_ge(taken["xt"], g + 1)
                small_free()
                for j in range(TILES):
                    mm = pe.matmul(small[:, j * P:(j + 1) * P], xn_t[:, parity, j * P:(j + 1) * P], w_v[:, :],
                                   start=True, stop=True)
                use("v", mm, g)

            def turn_max(g, parity, half):
                pe.wait_ge(a_taken, A_N * g + A_N // 2 * (half + 1))
                small_free()
                use("mx", pe.transpose(small[0:32, 0:P], maxima[:, parity, 32 * half:32 * half + 32], c.ident[:, :]),
                    g, half)

            def pass_a(g, parity, h, j):
                if h % HALF == 0 and j == 0:
                    pe.wait_ge(rows_loaded[parity][h // HALF], 48 * (g - parity) + 96)
                wait_past(pe, a_taken, g, A_N, h * TILES + j - 1)
                pe.matmul(a_ps[j % 2][:, :], q_rows[0:ROWS, parity, h, j * P:(j + 1) * P],
                          k_rows[0:ROWS, parity, h, :], start=True, stop=True).then_inc(a_filled, 1)

            def pass_b(g, parity, h, n):
                if h % HALF == 0 and n == 0:
                    pe.wait_ge(max_loaded, 32 * g + 16 * (h // HALF) + 16)
                wait_past(pe, exp_done, g, B_N, 2 * h + n - 1)
                for a in range(2):
                    kb = 2 * n + a
                    mm = pe.matmul(b_ps[n][:, a * 512:(a + 1) * 512], k_rows[:, parity, h, kb * P:(kb + 1) * P],
                                   q_rows[:, parity, h, :], start=True, stop=True)
                mm.then_inc(b_filled, 1)

            def values(g, parity, quad, kb):
                if kb == 0:
                    if quad == 0:
                        pe.wait_ge(taken["v"], g + 1)
                    pe.wait_ge(exp_done, B_N * g + 8 * quad + 8)
                    wait_past(pe, o_taken, g, QUADS, quad)
                for n in range(4):
                    h = 4 * quad + n
                    mm = pe.matmul(o_ps[32 * n:32 * n + VW, :], v_one[:, parity, kb, h, :],
                                   probs[:, h % 8, kb, :], start=(kb == 0), stop=(kb == TILES - 1))
                if kb == TILES - 1:
                    mm.then_inc(pv_done, 1)

            def turn_o(g, quad):
                pe.wait_ge(o_taken, QUADS * g + quad + 1)
                small_free()
                for j in range(TILES):
                    mm = pe.transpose(small[:, j * P:(j + 1) * P], o_t[:, quad % 2, j * P:(j + 1) * P], c.ident[:, :])
                use("ot", mm, g, quad)

            def turn_attn(g):
                pe.wait_ge(taken["ot"], QUADS * g + QUADS)
                small_free()
                for j in range(TILES):
                    mm = pe.transpose(small[:, j * P:(j + 1) * P], attn[:, j, :, :].rearrange("p h d -> p (h d)"),
                                      c.ident[:, :])
                use("at", mm, g)

            def project_out(g):
                pe.wait_ge(taken["at"], g + 1)
                small_free()
                for j in range(TILES):
                    mm = pe.matmul(small[:, j * P:(j + 1) * P], attn_t[:, j * P:(j + 1) * P], w_o[:, :],
                                   start=True, stop=True)
                use("y", mm, g)

            pe.wait_ge(w_ready, 3)
            pe.wait_ge(edges_set, 2)
            pe.wait_ge(o_cleared, 1)
            for g in range(2):
                turn_x(g, g)
                project_qk(g, g, 0)
                project_qk(g, g, 1)
            project_v(0, 0)
            for h in range(H):
                for j in range(TILES):
                    pass_a(0, 0, h, j)
            turn_max(0, 0, 0)

            def body(g, parity, ok):
                if not isinstance(g, int) or g > 0:
                    last[:] = ["ot", QUADS * (g - 1) + 3]
                for s in range(H):
                    if ok(1):
                        pass_a(g + 1, 1 - parity, s, 0)
                    if ok(0):
                        pass_b(g, parity, s, 0)
                    if ok(1):
                        pass_a(g + 1, 1 - parity, s, 1)
                    if s < 4 and ok(-1):
                        values(g - 1, 1 - parity, 3, s)
                    if s >= 4 and ok(0):
                        values(g, parity, s // 4 - 1, s % 4)
                    if ok(1):
                        pass_a(g + 1, 1 - parity, s, 2)
                    if ok(0):
                        pass_b(g, parity, s, 1)
                    if ok(1):
                        pass_a(g + 1, 1 - parity, s, 3)
                    if s == 0 and ok(0):
                        turn_max(g, parity, 1)
                    if s == 2 and ok(2):
                        turn_x(g + 2, parity)
                    if s == 3 and ok(-1):
                        turn_o(g - 1, 3)
                    if s == 4 and ok(2):
                        project_qk(g + 2, parity, 0)
                    if s == 5 and ok(2):
                        project_qk(g + 2, parity, 1)
                    if s == 6 and ok(-1):
                        turn_attn(g - 1)
                    if s == 8 and ok(-1):
                        project_out(g - 1)
                    if s == 9 and ok(1):
                        turn_max(g + 1, 1 - parity, 0)
                    if s == 10 and ok(1):
                        project_v(g + 1, 1 - parity)
                    if s in (7, 11, 15) and ok(0):
                        turn_o(g, s // 4 - 1)

            turns(pe, G, body)

        @block.vector
        def _(dve):
            links = [0, 0]

            def link(ins):
                ins.then_inc(chain, 1)
                links[1] += 1
                dve.wait_ge(chain, links[0] + links[1])

            def norm_in(g):
                for j in range(TILES):
                    ins = dve.bn_stats(pre.stats[:, j, :], tile_of(c, g, j))
                link(ins)
                dve.memset(c.spare[:, :], 0.0)
                for j in range(TILES):
                    ins = dve.bn_aggr(pre.meanvar[:, j, :], pre.stats[:, j, :])
                link(ins)
                dve.tensor_scalar(pre.vareps[:, :], pre.meanvar[:, :, 1], EPS, None, ALU.add).then_inc(pre_var, 1)

            def scale_in(g):
                dve.wait_ge(pre_rstd, g + 1)
                if not (isinstance(g, int) and g == 0):
                    dve.wait_ge(filled["xt"], g)
                for j in range(TILES):
                    ins = dve.tensor_scalar(xn[:, j, :], tile_of(c, g, j), pre.meanvar[:, j, 0:1],
                                            pre.rstd[:, j:j + 1], ALU.subtract, ALU.mult)
                ins.then_inc(xn_ready, 1)

            def take_max(g, half):
                dve.wait_ge(filled["mx"], 2 * g + half + 1)
                n = 2 * g + half
                if not (isinstance(n, int) and n == 0):
                    dve.wait_ge(max_split, 4 * n)
                dve.tensor_scalar(neg_max[:, :], small[0:32, 0:P], -1.0, None, ALU.mult).then_inc(taken["mx"], 1)

            def take_v(g, parity):
                dve.wait_ge(filled["v"], g + 1)
                wait_past(dve, pv_done, g, QUADS, -QUADS)
                bias = bias_v[:, :].rearrange("p (h c d) -> p h c d", h=H, c=3)[:, :, 2, :]
                dve.tensor_tensor(v_one[:, parity, :, :, 0:DH],
                                  small[:, :].rearrange("p (j h d) -> p j h d", j=TILES, h=H),
                                  bias.unsqueeze(1).broadcast_to([P, TILES, H, DH]), ALU.add).then_inc(taken["v"], 1)

            def maxima_of(g, parity, h, j):
                at = h * TILES + j
                dve.wait_ge(a_filled, A_N * g + at + 1)
                if at == 0:
                    wait_past(dve, filled["mx"], g, 2, -2)
                dve.tensor_reduce(maxima[:, parity, at:at + 1], a_ps[j % 2][:, :], AX.X, ALU.max)\
                   .then_inc(a_taken, 1)

            def take_attn(g, quad):
                dve.wait_ge(filled["ot"], QUADS * g + quad + 1)
                if quad == 0:
                    wait_past(dve, filled["at"], g, 1, 0)
                o = small[:, :].rearrange("p (j n d) -> p j n d", j=TILES, n=4)
                link(dve.reciprocal(rsum[:, :, :], o[:, :, :, DH]))
                dve.tensor_tensor(attn[:, :, 4 * quad:4 * quad + 4, :], o[:, :, :, 0:DH],
                                  rsum[:, :, :].unsqueeze(3).broadcast_to([P, TILES, 4, DH]), ALU.mult)\
                   .then_inc(taken["ot"], 1)

            def add_out_bias(g):
                dve.wait_ge(filled["y"], g + 1)
                dve.tensor_tensor(y[:, :, :], small[:, :].rearrange("p (j d) -> p j d", j=TILES),
                                  bias_o[:, :].unsqueeze(1).broadcast_to([P, TILES, D]), ALU.add).then_inc(taken["y"], 1)
                dve.wait_ge(taken["y"], g + 1)
                for j in range(TILES):
                    ins = dve.bn_stats(post.stats[:, j, :], y[:, j, :])
                link(ins)
                dve.memset(c.spare[:, :], 0.0)
                for j in range(TILES):
                    ins = dve.bn_aggr(post.meanvar[:, j, :], post.stats[:, j, :])
                link(ins)
                dve.tensor_scalar(post.vareps[:, :], post.meanvar[:, :, 1], EPS, None, ALU.add).then_inc(post_var, 1)

            def norm_out(g):
                dve.wait_ge(post_rstd, g + 1)
                for j in range(TILES):
                    ins = dve.tensor_scalar(y[:, j, :], y[:, j, :], post.meanvar[:, j, 0:1],
                                            post.rstd[:, j:j + 1], ALU.subtract, ALU.mult)
                link(ins)
                dve.tensor_tensor(group_of(c, g), group_of(c, g), y[:, :, :], ALU.add).then_inc(x_done, 1)

            dve.wait_ge(c.loaded_first, 16)
            dve.wait_ge(c.loaded_rest, 16)
            dve.wait_ge(w_loaded, 16 * 20)
            w_heads = w_raw[:, :].rearrange("p (h c d) -> p c h d", h=H, c=3)
            for n, w in enumerate((w_q, w_k)):
                dve.tensor_copy(w[:, :].rearrange("p (d h) -> p h d", d=DH), w_heads[:, n]).then_inc(w_ready, 1)
            dve.tensor_copy(w_v[:, :].rearrange("p (h d) -> p h d", h=H), w_heads[:, 2]).then_inc(w_ready, 1)
            dve.memset(o_ps[:, :], 0.0).then_inc(o_cleared, 1)
            for g in range(2):
                norm_in(g)
                scale_in(g)
            take_v(0, 0)
            for h in range(H):
                for j in range(TILES):
                    maxima_of(0, 0, h, j)
            take_max(0, 0)

            per_turn = 9
            loop_base = []

            def body(g, parity, ok):
                if not isinstance(g, int):
                    if not loop_base:
                        loop_base.append(links[0] + links[1])
                    links[:] = [loop_base[0] + per_turn * (g - 2), 0]
                elif g == G - 2 and loop_base:
                    links[:] = [loop_base[0] + per_turn * (G - 4), 0]
                for s in range(H):
                    if ok(1):
                        maxima_of(g + 1, 1 - parity, s, 0)
                    if s == 1 and ok(0):
                        take_max(g, 1)
                    if s == 4 and ok(-1):
                        take_attn(g - 1, 3)
                    if s in (8, 12) and ok(0):
                        take_attn(g, s // 4 - 2)
                    if s == 9 and ok(-1):
                        add_out_bias(g - 1)
                    if s == 10 and ok(1):
                        take_max(g + 1, 0)
                    if s == 11 and ok(1):
                        take_v(g + 1, 1 - parity)
                    if s == 0 and ok(-1):
                        take_attn(g - 1, 2)
                    if ok(1):
                        maxima_of(g + 1, 1 - parity, s, 1)
                    if s == 0 and ok(2):
                        norm_in(g + 2)
                    if ok(1):
                        maxima_of(g + 1, 1 - parity, s, 2)
                    if s == 1 and ok(2):
                        scale_in(g + 2)
                    if s == 13 and ok(-1):
                        norm_out(g - 1)
                    if ok(1):
                        maxima_of(g + 1, 1 - parity, s, 3)
                if not isinstance(g, int):
                    assert links[1] == per_turn, links[1]

            turns(dve, G, body)


def turns(eng, groups, body):
    def fixed(g):
        body(g, g % 2, lambda d: 0 <= g + d < groups)
    fixed(0)
    fixed(1)
    with eng.Fori(1, groups // 2 - 1) as i:
        for parity in range(2):
            body(2 * i + parity, parity, lambda d: True)
    for g in range(groups - 2, groups + 1):
        fixed(g)


def wait_past(eng, semaphore, g, n, at):
    if isinstance(g, int) and n * g + at <= 0:
        return
    eng.wait_ge(semaphore, g * n + at)


class Chain:

    def __init__(self, eng, semaphore, groups, per_turn):
        self.eng, self.semaphore, self.groups, self.per_turn = eng, semaphore, groups, per_turn
        self.base, self.n, self.loop_base = 0, 0, None

    def turn(self, g):
        if not isinstance(g, int):
            if self.loop_base is None:
                self.loop_base = self.base + self.n
            else:
                assert self.n == self.per_turn, self.n
            self.base, self.n = self.loop_base + self.per_turn * (g - 2), 0
        elif g == self.groups - 2 and self.loop_base is not None:
            self.base, self.n = self.loop_base + self.per_turn * (self.groups - 4), 0

    def link(self, ins):
        ins.then_inc(self.semaphore, 1)
        self.n += 1
        self.eng.wait_ge(self.semaphore, self.base + self.n)


def mixture_of_experts(c, gate_w, gate_b, w1, b1, w3, b3, w2, b2, sw1, sb1, sw3, sb3, sw2, sb2):
    nc = c.nc
    G = c.groups
    E, _, HID = w1.shape
    N_E = E + 1
    PARTS = 3
    CHUNKS = -(-N_E * HID // P)
    ROUTED = E * HID // P
    LAST = N_E * HID - (CHUNKS - 1) * P
    assert E * HID % P == 0 and CHUNKS == ROUTED + 2
    size = [P] * (CHUNKS - 1) + [LAST]

    with ExitStack() as ctx:
        semaphores = ctx.enter_context(LayerSemaphores(nc))

        def sb(name, shape, dt):
            return ctx.enter_context(nc.sbuf_tensor("me_" + name, shape, dt))

        def sem(name):
            return semaphores.get("me_" + name)

        def bank(name):
            return ctx.enter_context(nc.psum_tensor("me_" + name, [P, 512], F32))

        up = [sb(f"w_up{n}", [P, N_E * HID], F32) for n in range(2)]
        up_bias = [sb(f"b_up{n}", [P, CHUNKS], F32) for n in range(2)]
        down = sb("w_down", [P, CHUNKS, D], F32)
        down_bias = sb("b_down", [PARTS * N_E, D], F32)
        gate_raw = sb("gate_raw", [E, D], F32)
        gate_t = sb("gate_t", [P, E], F32)
        gate_bias = sb("gate_bias", [P, E], F32)
        one_hot0 = sb("one_hot0", [N_E, N_E * HID], BF16)
        one_hot = sb("one_hot", [PARTS * N_E, N_E * HID], BF16)
        ident_bf = sb("ident_bf", [P, P], BF16)
        iota = sb("iota", [P, TILES, E], F32)
        euler = sb("euler", [P, TILES, E], F32)
        pre, post = LnBufs(sb, "pre"), LnBufs(sb, "post")
        xn = sb("xn", [P, TILES, D], F32)
        xn_t = sb("xn_t", [P, 2, SEQ], F32)
        top = sb("top", [P, TILES], F32)
        shifted = sb("shifted", [P, TILES, E], F32)
        expd = sb("expd", [P, TILES, E], F32)
        total = sb("total", [P, TILES], F32)
        inverse = sb("inverse", [P, TILES], F32)
        score = sb("score", [P, TILES, E], F32)
        biased = sb("biased", [P, 2, TILES, E], F32)
        place = sb("place", [P, TILES, E], F32)
        chosen = sb("chosen", [P, 2, TILES, E], F32)
        weight = sb("weight", [P, TILES, N_E], F32)
        w_rest = sb("w_rest", [P, TILES, N_E], F32)
        w_parts = sb("w_parts", [P, TILES, PARTS * N_E], BF16)
        wt_bf = sb("wt_bf", [PARTS * N_E, 2, SEQ], BF16)
        wt_f = sb("wt_f", [PARTS * N_E, 2, SEQ], F32)
        first = sb("first", [P, 2, SEQ], F32)
        both = sb("both", [P, 2, SEQ], F32)
        act_out = sb("act_out", [P, 2, SEQ], F32)
        hidden = sb("hidden", [P, CHUNKS, SEQ], F32)
        y = sb("y", [P, TILES, D], F32)

        up_ps = [[bank(f"up{n}_ps{i}") for i in range(2)] for n in range(2)]
        wb_ps = [bank(f"wb_ps{i}") for i in range(2)]
        y_ps = bank("y_ps")
        small = bank("small")
        small_bf = small[:, :].bitcast(BF16)

        loaded, hot_zero, hot_ready, hot_spread = sem("loaded"), sem("hot_steps"), sem("hot_ready"), sem("hot_spread")
        ones_set, gate_turned, gate_ready = sem("ones_set"), sem("gate_turned"), sem("gate_ready")
        pre_var, pre_rstd = sem("pre_var"), sem("pre_rstd")
        post_var, post_rstd = sem("post_var"), sem("post_rstd")
        xn_ready, xn_turned, xn_t_ready = sem("xn_ready"), sem("xn_turned"), sem("xn_t_ready")
        logits_done, logits_read = sem("logits_done"), sem("logits_read")
        shifted_ready, exp_ready = sem("shifted_ready"), sem("exp_ready")
        parts_ready, wt_turned, wt_ready = sem("parts_ready"), sem("wt_turned"), sem("wt_ready")
        up_done = [sem(f"up{n}_done") for n in range(2)]
        wb_done = sem("wb_done")
        first_ready, both_ready, act_ready, hidden_ready = (sem(n) for n in ("first_ready", "both_ready", "act_ready",
                                                                             "hidden_ready"))
        down_done, y_ready, x_done = sem("down_done"), sem("y_ready"), sem("x_done")
        dve_chain = sem("dve_chain")
        N_LOADS = 17

        block = ctx.enter_context(nc.Block())

        @block.sync
        def _(sp):
            for n, (w, sw, b, s_b) in enumerate(((w1, sw1, b1, sb1), (w3, sw3, b3, sb3))):
                sp.dma_start(up[n][:, 0:E * HID].rearrange("p (e h) -> p e h", e=E),
                             w.rearrange("e d h -> d e h")).then_inc(loaded, 16)
                sp.dma_start(up[n][:, E * HID:N_E * HID], sw).then_inc(loaded, 16)
                sp.dma_start(up_bias[n][:, 0:ROUTED], b.rearrange("e h -> (e h)").rearrange("(c p) -> p c", p=P),
                             allow_slow_non_contiguous=True).then_inc(loaded, 16)
                sp.dma_start(up_bias[n][:, ROUTED:ROUTED + 1], s_b[0:P].rearrange("(p a) -> p a", a=1)).then_inc(loaded, 16)
                sp.dma_start(up_bias[n][0:LAST, ROUTED + 1:CHUNKS], s_b[P:HID].rearrange("(p a) -> p a", a=1))\
                  .then_inc(loaded, 16)
            sp.dma_start(down[:, 0:ROUTED, :], w2.rearrange("e h d -> (e h) d").rearrange("(c p) d -> p c d", p=P))\
              .then_inc(loaded, 16)
            sp.dma_start(down[:, ROUTED, :], sw2[0:P, :]).then_inc(loaded, 16)
            sp.dma_start(down[0:LAST, ROUTED + 1, :], sw2[P:HID, :]).then_inc(loaded, 16)
            sp.dma_start(gate_raw[:, :], gate_w).then_inc(loaded, 16)
            sp.dma_start(gate_bias[:, :], gate_b.partition_broadcast(P)).then_inc(loaded, 16)
            for n in range(PARTS):
                sp.dma_start(down_bias[n * N_E:n * N_E + E, :], b2).then_inc(loaded, 16)
                sp.dma_start(down_bias[n * N_E + E:(n + 1) * N_E, :], sb2.rearrange("(a d) -> a d", a=1)).then_inc(loaded, 16)
            sp.wait_ge(hot_ready, 1)
            for n in range(PARTS):
                sp.dma_start(one_hot[n * N_E:(n + 1) * N_E, :], one_hot0[:, :]).then_inc(hot_spread, 16)

        @block.gpsimd
        def _(pool):
            steps = [0]

            def step(ins):
                ins.then_inc(hot_zero, 1)
                steps[0] += 1
                pool.wait_ge(hot_zero, steps[0])

            step(pool.memset(one_hot0[:, :], 1.0))
            step(pool.affine_select(out=one_hot0[:, :], in_=one_hot0[:, :], compare_op=ALU.is_ge, fill=0.0, base=0,
                                    pattern=[[1, N_E * HID]], channel_multiplier=-HID))
            pool.affine_select(out=one_hot0[:, :], in_=one_hot0[:, :], compare_op=ALU.is_ge, fill=0.0,
                               base=HID - 1, pattern=[[-1, N_E * HID]], channel_multiplier=HID).then_inc(hot_ready, 1)
            pool.wait_ge(hot_ready, 1)
            step(pool.memset(euler[:, :, :], 2.718281828459045))
            step(pool.memset(weight[:, :, E:N_E], 1.0))
            pool.iota(iota[:, :, :], pattern=[[0, TILES], [1, E]], base=0, channel_multiplier=0,
                      allow_small_or_imprecise_dtypes=True).then_inc(ones_set, 1)
            pool.wait_ge(ones_set, 1)

            def rstd(bufs, var, done, g):
                pool.wait_ge(var, g + 1)
                pool.tensor_tensor(bufs.rstd[:, :], bufs.vareps[:, :], c.neg_half[:, :], ALU.pow).then_inc(done, 1)

            def exps(g):
                pool.wait_ge(shifted_ready, g + 1)
                pool.tensor_tensor(expd[:, :, :], euler[:, :, :], shifted[:, :, :], ALU.pow).then_inc(exp_ready, 1)

            rstd(pre, pre_var, pre_rstd, 0)
            exps(0)

            def body(g, parity, ok):
                if ok(1):
                    rstd(pre, pre_var, pre_rstd, g + 1)
                if ok(-1):
                    rstd(post, post_var, post_rstd, g - 1)
                if ok(1):
                    exps(g + 1)

            turns(pool, G, body)

        @block.scalar
        def _(act):
            act.wait_ge(gate_turned, 1)
            act.copy(gate_t[:, :], small[:, 0:E]).then_inc(gate_ready, 1)
            act.wait_ge(loaded, 16 * (N_LOADS + 4))

            def copy_xt(g, parity):
                act.wait_ge(xn_turned, g + 1)
                wait_past(act, up_done[1], g, CHUNKS, -CHUNKS)
                act.copy(xn_t[:, parity, :], small[:, :]).then_inc(xn_t_ready, 1)

            def copy_wt(g, parity):
                act.wait_ge(wt_turned, g + 1)
                wait_past(act, wb_done, g, CHUNKS, -CHUNKS)
                act.copy(wt_bf[:, parity, :], small_bf[0:PARTS * N_E, 0:SEQ]).then_inc(wt_ready, 1)
                act.copy(wt_f[:, parity, :], small_bf[0:PARTS * N_E, 0:SEQ]).then_inc(wt_ready, 1)

            def add_bias(g, parity, n):
                b = (parity + n) % 2
                act.wait_ge(up_done[0], CHUNKS * g + n + 1)
                wait_past(act, both_ready, g, CHUNKS, n - 1)
                act.activation(first[0:size[n], b, :], up_ps[0][b][0:size[n], :], ACT.Identity,
                               bias=up_bias[0][0:size[n], n:n + 1]).then_inc(first_ready, 1)

            def silu(g, parity, n):
                b = (parity + n) % 2
                act.wait_ge(both_ready, CHUNKS * g + n + 1)
                wait_past(act, hidden_ready, g, CHUNKS, n - 1)
                act.activation(act_out[0:size[n], b, :], both[0:size[n], b, :], ACT.Silu).then_inc(act_ready, 1)

            copy_xt(0, 0)
            copy_wt(0, 0)

            def body(g, parity, ok):
                for n in range(CHUNKS):
                    if ok(0):
                        add_bias(g, parity, n)
                    if n == 0 and ok(-1):
                        silu(g - 1, 1 - parity, CHUNKS - 1)
                    if n > 0 and ok(0):
                        silu(g, parity, n - 1)
                    if n == 2 and ok(-1):
                        act.wait_ge(down_done, CHUNKS * g)
                        wait_past(act, x_done, g, 1, -1)
                        act.copy(y[:, :, :].rearrange("p j d -> p (j d)"), y_ps[:, :]).then_inc(y_ready, 1)
                    if n == 4 and ok(1):
                        copy_xt(g + 1, 1 - parity)
                    if n == 10 and ok(1):
                        copy_wt(g + 1, 1 - parity)

            turns(act, G, body)

        @block.tensor
        def _(pe):
            pe.wait_ge(c.consts, 3)
            pe.wait_ge(loaded, 16 * (N_LOADS + 4))
            pe.transpose(small[:, 0:E], gate_raw[:, :], c.ident[0:E, 0:E]).then_inc(gate_turned, 1)
            pe.wait_ge(gate_ready, 1)
            pe.wait_ge(hot_spread, 48)

            def turn_x(g):
                pe.wait_ge(xn_ready, g + 1)
                wait_past(pe, wt_ready, g, 2, 0)
                for j in range(TILES):
                    mm = pe.transpose(small[:, j * P:(j + 1) * P], xn[:, j, :], c.ident[:, :])
                mm.then_inc(xn_turned, 1)

            def logits(g, parity):
                pe.wait_ge(xn_t_ready, g + 1)
                for j in range(TILES):
                    mm = pe.matmul(small[:, j * E:(j + 1) * E], xn_t[:, parity, j * P:(j + 1) * P], gate_t[:, :],
                                   start=True, stop=True)
                mm.then_inc(logits_done, 1)

            def turn_weights(g):
                pe.wait_ge(parts_ready, g + 1)
                for j in range(TILES):
                    mm = pe.transpose(small_bf[0:PARTS * N_E, j * P:(j + 1) * P], w_parts[:, j, :], ident_bf[:, :])
                mm.then_inc(wt_turned, 1)

            def up_products(g, parity, n):
                b = (parity + n) % 2
                cols = slice(n * P, n * P + size[n])
                for k, used in ((0, first_ready), (1, both_ready)):
                    wait_past(pe, used, g, CHUNKS, n - 1)
                    pe.matmul(up_ps[k][b][0:size[n], :], up[k][:, cols], xn_t[:, parity, :], start=True, stop=True)\
                      .then_inc(up_done[k], 1)
                wait_past(pe, hidden_ready, g, CHUNKS, n - 1)
                pe.matmul(wb_ps[b][0:size[n], :], one_hot[:, cols], wt_bf[:, parity, :], start=True, stop=True)\
                  .then_inc(wb_done, 1)

            def down_product(g, parity, n):
                pe.wait_ge(hidden_ready, CHUNKS * g + n + 1)
                if n == 0:
                    wait_past(pe, y_ready, g, 1, 0)
                    for j in range(TILES):
                        pe.matmul(y_ps[:, j * D:(j + 1) * D], wt_f[:, parity, j * P:(j + 1) * P], down_bias[:, :],
                                  start=(j == 0), stop=False, skip_group_check=True)
                for j in range(TILES):
                    mm = pe.matmul(y_ps[:, j * D:(j + 1) * D], hidden[0:size[n], n, j * P:(j + 1) * P],
                                   down[0:size[n], n, :], start=False, stop=(n == CHUNKS - 1), skip_group_check=True)
                mm.then_inc(down_done, 1)

            turn_x(0)
            logits(0, 0)
            turn_weights(0)
            pe.wait_ge(wt_ready, 2)

            def body(g, parity, ok):
                if ok(0):
                    wait_past(pe, wt_ready, g, 2, 2)
                for n in range(CHUNKS):
                    if ok(0):
                        up_products(g, parity, n)
                    if n < 2 and ok(-1):
                        down_product(g - 1, 1 - parity, CHUNKS - 2 + n)
                    if n >= 2 and ok(0):
                        down_product(g, parity, n - 2)
                    if n == 3 and ok(1):
                        turn_x(g + 1)
                    if n == 5 and ok(1):
                        logits(g + 1, 1 - parity)
                    if n == 9 and ok(1):
                        turn_weights(g + 1)

            turns(pe, G, body)

        @block.vector
        def _(dve):
            chain = Chain(dve, dve_chain, G, 26)
            link = chain.link

            def norm_in(g):
                ln_stats(dve, c, lambda j: tile_of(c, g, j), pre, link).then_inc(pre_var, 1)

            def scale_in(g):
                dve.wait_ge(pre_rstd, g + 1)
                wait_past(dve, xn_turned, g, 1, 0)
                for j in range(TILES):
                    ins = dve.tensor_scalar(xn[:, j, :], tile_of(c, g, j), pre.meanvar[:, j, 0:1],
                                            pre.rstd[:, j:j + 1], ALU.subtract, ALU.mult)
                ins.then_inc(xn_ready, 1)

            def over(t):
                return t.unsqueeze(2).broadcast_to([P, TILES, E])

            def route_shift(g):
                dve.wait_ge(logits_done, g + 1)
                logit = small[:, 0:TILES * E].rearrange("p (j e) -> p j e", j=TILES)
                link(dve.tensor_reduce(top[:, :], logit, AX.X, ALU.max))
                dve.tensor_tensor(shifted[:, :, :], logit, over(top[:, :]), ALU.subtract).then_inc(shifted_ready, 1)

            def route(g):
                dve.wait_ge(exp_ready, g + 1)
                link(dve.tensor_reduce(total[:, :], expd[:, :, :], AX.X, ALU.add))
                link(dve.reciprocal(inverse[:, :], total[:, :]))
                link(dve.tensor_tensor(score[:, :, :], expd[:, :, :], over(inverse[:, :]), ALU.mult))
                link(dve.tensor_tensor(biased[:, 0], score[:, :, :],
                                       gate_bias[:, :].unsqueeze(1).broadcast_to([P, TILES, E]), ALU.add))
                for n in range(2):
                    link(dve.tensor_reduce(top[:, :], biased[:, n], AX.X, ALU.max))
                    link(dve.tensor_tensor(place[:, :, :], biased[:, n], over(top[:, :]), ALU.is_lt))
                    flat = place[:, :, :].rearrange("p j e -> p (j e)")
                    link(dve.scalar_tensor_tensor(out=flat, in0=flat, scalar=float(E),
                                                  in1=iota[:, :, :].rearrange("p j e -> p (j e)"),
                                                  op0=ALU.mult, op1=ALU.add))
                    link(dve.tensor_reduce(top[:, :], place[:, :, :], AX.X, ALU.min))
                    link(dve.tensor_tensor(chosen[:, n], iota[:, :, :], over(top[:, :]), ALU.is_equal))
                    if n == 0:
                        link(dve.scalar_tensor_tensor(out=biased[:, 1].rearrange("p j e -> p (j e)"),
                                                      in0=chosen[:, 0].rearrange("p j e -> p (j e)"), scalar=-1e30,
                                                      in1=biased[:, 0].rearrange("p j e -> p (j e)"),
                                                      op0=ALU.mult, op1=ALU.add))
                link(dve.tensor_tensor(place[:, :, :], chosen[:, 0], chosen[:, 1], ALU.add))
                link(dve.tensor_tensor(weight[:, :, 0:E], score[:, :, :], place[:, :, :], ALU.mult))

            def split_weights(g):
                wait_past(dve, wt_turned, g, 1, 0)
                parts = [w_parts[:, :, n * N_E:(n + 1) * N_E] for n in range(PARTS)]
                link(dve.tensor_scalar(parts[0], weight[:, :, :], 0.0, None, ALU.add))
                link(dve.tensor_tensor(w_rest[:, :, :], weight[:, :, :], parts[0], ALU.subtract))
                link(dve.tensor_scalar(parts[1], w_rest[:, :, :], 0.0, None, ALU.add))
                dve.tensor_tensor(parts[2], w_rest[:, :, :], parts[1], ALU.subtract).then_inc(parts_ready, 1)

            def multiply(g, parity, n):
                b = (parity + n) % 2
                dve.wait_ge(up_done[1], CHUNKS * g + n + 1)
                dve.wait_ge(first_ready, CHUNKS * g + n + 1)
                wait_past(dve, act_ready, g, CHUNKS, n - 1)
                dve.scalar_tensor_tensor(out=both[0:size[n], b, :], in0=up_ps[1][b][0:size[n], :],
                                         scalar=up_bias[1][0:size[n], n:n + 1], in1=first[0:size[n], b, :],
                                         op0=ALU.add, op1=ALU.mult).then_inc(both_ready, 1)

            def weigh(g, parity, n):
                b = (parity + n) % 2
                dve.wait_ge(act_ready, CHUNKS * g + n + 1)
                dve.wait_ge(wb_done, CHUNKS * g + n + 1)
                wait_past(dve, down_done, g, CHUNKS, n + 1 - CHUNKS)
                dve.tensor_tensor(hidden[0:size[n], n, :], act_out[0:size[n], b, :], wb_ps[b][0:size[n], :],
                                  ALU.mult).then_inc(hidden_ready, 1)

            def norm_out(g):
                dve.wait_ge(y_ready, g + 1)
                ln_stats(dve, c, lambda j: y[:, j, :], post, link).then_inc(post_var, 1)

            def add_out(g):
                dve.wait_ge(post_rstd, g + 1)
                for j in range(TILES):
                    ins = dve.tensor_scalar(y[:, j, :], y[:, j, :], post.meanvar[:, j, 0:1],
                                            post.rstd[:, j:j + 1], ALU.subtract, ALU.mult)
                link(ins)
                dve.tensor_tensor(group_of(c, g), group_of(c, g), y[:, :, :], ALU.add).then_inc(x_done, 1)

            dve.wait_ge(c.loaded_first, 16)
            dve.wait_ge(c.loaded_rest, 16)
            dve.wait_ge(loaded, 16 * (N_LOADS + 4))
            dve.wait_ge(ones_set, 1)
            dve.wait_ge(c.consts, 3)
            link(dve.tensor_copy(ident_bf[:, :], c.ident[:, :]))
            norm_in(0)
            scale_in(0)
            route_shift(0)
            route(0)
            split_weights(0)

            def body(g, parity, ok):
                chain.turn(g)
                for n in range(CHUNKS):
                    if ok(0):
                        multiply(g, parity, n)
                    if n == 0 and ok(-1):
                        weigh(g - 1, 1 - parity, CHUNKS - 1)
                    if n > 0 and ok(0):
                        weigh(g, parity, n - 1)
                    if n == 1 and ok(1):
                        norm_in(g + 1)
                    if n == 2 and ok(1):
                        scale_in(g + 1)
                    if n == 3 and ok(-1):
                        norm_out(g - 1)
                    if n == 4 and ok(-1):
                        add_out(g - 1)
                    if n == 6 and ok(1):
                        route_shift(g + 1)
                    if n == 7 and ok(1):
                        route(g + 1)
                    if n == 8 and ok(1):
                        split_weights(g + 1)

            turns(dve, G, body)


def gated_slots(c, Wq, Wk, Wv, Wf, g_norm_w, Wo):
    nc = c.nc
    G = c.groups
    H = 4
    HK = D // H
    M = Wf.shape[1] // H
    SLOTS = H * M
    PAIRS = SLOTS // P
    CH = 64
    PER_TILE = P // CH
    CHUNKS = SEQ // CH
    QSCALE = -float(HK) ** -0.5
    NORM = 8.0
    assert M == 64 and HK == 32 and PAIRS == 2 and PER_TILE == 2

    STEPS = (
        "A0 U0 xt A1 H1 L0 U1 q k H2 A2 U2 pt0 H3 L1 kt A3 B0 U3 vf0 H4 o0 pt1 U4 H5 L2 B1 G0 o1 U5 H6 "
        "pt2 vf1 U6 H7 L3 B2 G1 o2 D pt3 Dt B3 st0 o3 st1").split()

    def step_of(name):
        head = name.rstrip("0123456789")
        return head, int(name[len(head):] or 0)

    with ExitStack() as ctx:
        semaphores = ctx.enter_context(LayerSemaphores(nc))

        def sb(name, shape, dt=F32):
            return ctx.enter_context(nc.sbuf_tensor("gs_" + name, shape, dt))

        def sem(name):
            return semaphores.get("gs_" + name)

        w_q, w_k, w_o = sb("w_q", [P, D]), sb("w_k", [P, D]), sb("w_o", [P, D])
        w_vf = sb("w_vf", [P, D + SLOTS])
        norm_w = sb("norm_w", [P, 1])
        causal = sb("causal", [P, P])
        causal_q = sb("causal_q", [P, P])
        sum_from_mid = sb("sum_from_mid", [P, P])
        early = sb("early", [P, P])
        between = sb("between", [P, TILES, CHUNKS - 1])
        own_head = sb("own_head", [P, 2, 2 * HK])
        neg_half = sb("neg_half", [P, TILES * H])
        pre, post = LnBufs(sb, "pre"), LnBufs(sb, "post")
        xn = sb("xn", [P, TILES, D])
        xn_t = sb("xn_t", [P, SEQ])
        q_t = sb("q_t", [P, 2, SEQ])
        q_own = sb("q_own", [P, 2, TILES, H, P])
        k_t = sb("k_t", [P, 2, SEQ])
        kv = sb("kv", [P, 2, TILES, 2, D])
        abs_z = sb("abs_z", [P, 2, SLOTS])
        exp_z = sb("exp_z", [P, 2, SLOTS])
        log_z = sb("log_z", [P, 2, SLOTS])
        gate_log = sb("gate_log", [P, TILES, SLOTS])
        gate = sb("gate", [P, TILES, SLOTS])
        keep = sb("keep", [P, 2, TILES, SLOTS])
        unkeep = sb("unkeep", [P, TILES, SLOTS])
        write = sb("write", [P, 2, TILES, SLOTS])
        write_t = sb("write_t", [P, 2, TILES, PAIRS, P])
        decay_rows = sb("decay_rows", [CHUNKS - 1, SLOTS])
        decay = sb("decay", [P, 2, PAIRS, CHUNKS - 1])
        added = sb("added", [P, PAIRS, 2, 2 * HK])
        state = sb("state", [P, CHUNKS, PAIRS, 2, D])
        state_k = sb("state_k", [P, CHUNKS, SLOTS])
        a_sb = sb("a_sb", [P, TILES, H, P])
        logit = sb("logit", [P, TILES, SLOTS])
        expd = sb("expd", [P, TILES, SLOTS])
        p_keep = sb("p_keep", [P, TILES, SLOTS])
        p_t = sb("p_t", [P, TILES, PAIRS, P])
        p_own = sb("p_own", [P, TILES, PAIRS, 2, P])
        b_sb = sb("b_sb", [P, TILES, H, P])
        top = sb("top", [P, H])
        total = sb("total", [P, TILES * H])
        inverse = sb("inverse", [P, TILES * H])
        o_sb = sb("o_sb", [P, TILES * H, HK])
        o_sq = sb("o_sq", [P, TILES * H, HK])
        o_var = sb("o_var", [P, TILES * H])
        o_rstd = sb("o_rstd", [P, TILES * H])
        on = sb("on", [P, TILES * H, HK])
        on_t = sb("on_t", [P, SEQ])
        y = sb("y", [P, TILES, D])

        banks = {n: ctx.enter_context(nc.psum_tensor("gs_" + n, [P, 512], F32))
                 for n in ("prep0", "prep1", "a", "b", "l", "pt", "state_ps", "o_ps")}

        per_seq = {"xt": 1, "q": 1, "k": 1, "kt": 1, "vf": TILES, "G": 2, "D": 1, "Dt": 1, "st": 2, "A": TILES,
                   "L": TILES, "pt": TILES, "B": TILES, "U": CHUNKS - 1, "H": CHUNKS - 1, "o": 1, "ont": 1, "y": 1}
        filled = {n: sem(n + "_filled") for n in per_seq}
        taken = {n: sem(n + "_taken") for n in per_seq}
        loaded, masks, wo_ready = sem("loaded"), sem("mask_steps"), sem("wo_ready")
        consts_ready = sem("consts_ready")
        pre_var, pre_rstd, xn_ready = sem("pre_var"), sem("pre_rstd"), sem("xn_ready")
        post_var, post_rstd, x_done = sem("post_var"), sem("post_rstd"), sem("x_done")
        act_steps = sem("act_steps")
        gate_log_ready, write_ready = sem("gate_log_ready"), sem("write_ready")
        shifted_ready, exp_done, p_ready = sem("shifted_ready"), sem("exp_done"), sem("p_ready")
        state_ready = sem("state_ready")
        own_zero, q_own_ready, p_own_ready = sem("own_zero"), sem("q_own_ready"), sem("p_own_ready")
        o_var_ready, o_rstd_ready, on_ready = sem("o_var_ready"), sem("o_rstd_ready"), sem("on_ready")
        dve_chain = sem("dve_chain")
        LOADS = 10

        block = ctx.enter_context(nc.Block())

        @block.sync
        def _(sp):
            sp.dma_start(w_q[:, :], Wq).then_inc(loaded, 16)
            sp.dma_start(w_k[:, :], Wk).then_inc(loaded, 16)
            sp.dma_start(w_vf[:, 0:D], Wv).then_inc(loaded, 16)
            sp.dma_start(w_vf[:, D:], Wf).then_inc(loaded, 16)
            sp.dma_start(w_o[:, :], Wo).then_inc(loaded, 16)
            for h in range(H):
                sp.dma_start(norm_w[h * HK:(h + 1) * HK, :], g_norm_w.rearrange("(p a) -> p a", a=1)).then_inc(loaded, 16)
            sp.wait_ge(loaded, 16 * (LOADS - 1))

        @block.gpsimd
        def _(pool):
            def rstd(bufs, var, done, g):
                pool.wait_ge(var, g + 1)
                pool.tensor_tensor(bufs.rstd[:, :], bufs.vareps[:, :], c.neg_half[:, :], ALU.pow).then_inc(done, 1)

            pool.memset(causal[:, :], 1.0).then_inc(masks, 1)
            pool.wait_ge(masks, 1)
            pool.affine_select(out=causal[:, :], in_=causal[:, :], compare_op=ALU.is_ge, fill=0.0, base=0,
                               pattern=[[1, P]], channel_multiplier=-1).then_inc(masks, 1)
            pool.wait_ge(masks, 2)
            pool.wait_ge(c.consts, 3)
            pool.memset(q_own[:, :, :, :, :], 0.0).then_inc(own_zero, 1)
            pool.memset(p_own[:, :, :, :, :], 0.0).then_inc(own_zero, 1)
            pool.wait_ge(own_zero, 2)
            rstd(pre, pre_var, pre_rstd, 0)

            def spread_q(g, parity):
                pool.wait_ge(taken["q"], g + 1)
                wait_past(pool, filled["A"], g, TILES, -TILES)
                for h in range(H):
                    rows = slice(h * HK, (h + 1) * HK)
                    pool.tensor_tensor(q_own[rows, parity, :, h, :],
                                       q_t[rows, parity, :].rearrange("p (j t) -> p j t", j=TILES),
                                       c.zero[rows, :].unsqueeze(2).broadcast_to([HK, TILES, P]), ALU.add)\
                        .then_inc(q_own_ready, 1)
                    pool.wait_ge(q_own_ready, H * g + h + 1)

            def spread_p(g, n):
                pool.wait_ge(taken["pt"], TILES * g + n + 1)
                wait_past(pool, filled["B"], g, TILES, n - TILES + 1)
                for i in range(2):
                    rows = slice(i * M, (i + 1) * M)
                    pool.tensor_tensor(p_own[rows, n, :, i, :], p_t[rows, n, :, :],
                                       c.zero[rows, :].unsqueeze(2).broadcast_to([M, PAIRS, P]), ALU.add)\
                        .then_inc(p_own_ready, 1)
                    pool.wait_ge(p_own_ready, 2 * (TILES * g + n) + i + 1)

            spread_q(0, 0)

            def body(g, parity, ok):
                if ok(-1):
                    pool.wait_ge(o_var_ready, g)
                    pool.tensor_tensor(o_rstd[:, :], o_var[:, :], neg_half[:, :], ALU.pow).then_inc(o_rstd_ready, 1)
                if ok(1):
                    rstd(pre, pre_var, pre_rstd, g + 1)
                if ok(-1):
                    rstd(post, post_var, post_rstd, g - 1)
                for name in STEPS:
                    name, n = step_of(name)
                    if name == "q" and ok(1):
                        spread_q(g + 1, 1 - parity)
                    if name == "pt" and ok(0):
                        spread_p(g, n)

            turns(pool, G, body)

        @block.scalar
        def _(act):
            act.wait_ge(loaded, 16 * (LOADS - 1))

            def take(name, g, n, out, in_, func=ACT.Copy, scale=1.0, inc=True):
                act.wait_ge(filled[name], per_seq[name] * g + n + 1)
                ins = act.activation(out, in_, func, scale=scale)
                if inc:
                    ins.then_inc(taken[name], 1)

            def prepare(name, n, g, parity):
                if name == "xt":
                    wait_past(act, filled["vf"], g, TILES, 0)
                    take("xt", g, 0, xn_t[:, :], banks["prep0"][:, :])
                if name == "q":
                    wait_past(act, filled["L"], g, TILES, -TILES)
                    take("q", g, 0, q_t[:, parity, :], banks["prep1"][:, :], ACT.Silu)
                if name == "k":
                    wait_past(act, filled["A"], g, TILES, -TILES)
                    take("k", g, 0, k_t[:, parity, :], banks["prep0"][:, :], ACT.Silu)
                if name == "kt":
                    wait_past(act, filled["o"], g, 1, -1)
                    take("kt", g, 0, kv[:, parity, :, 0, :],
                         banks["prep1"][:, :].rearrange("p (j d) -> p j d", j=TILES))
                if name == "vf":
                    for a in range(2):
                        j = 2 * n + a
                        bank = banks[f"prep{a}"]
                        act.wait_ge(filled["vf"], TILES * g + j + 1)
                        if a == 0:
                            wait_past(act, gate_log_ready, g, TILES, 2 * n)
                        act.activation(kv[:, parity, j, 1, :], bank[:, 0:D], ACT.Copy, scale=-1.0)
                        ins = act.activation(abs_z[:, a, :], bank[:, D:D + SLOTS], ACT.Abs)
                    at = (2 * g + n) * 4
                    ins.then_inc(act_steps, 1)
                    act.wait_ge(act_steps, at + 1)
                    act.activation(exp_z[:, :, :], abs_z[:, :, :], ACT.Exp, scale=-1.0).then_inc(act_steps, 1)
                    act.wait_ge(act_steps, at + 2)
                    act.activation(log_z[:, :, :], exp_z[:, :, :], ACT.Ln, bias=1.0).then_inc(act_steps, 1)
                    act.wait_ge(gate_log_ready, TILES * g + 2 * n + 2)
                    wait_past(act, write_ready, g, 2, n - 1)
                    act.activation(gate[:, 2 * n:2 * n + 2, :], gate_log[:, 2 * n:2 * n + 2, :], ACT.Exp,
                                   scale=1.0 / NORM).then_inc(act_steps, 1)
                if name == "G":
                    tiles = slice(2 * n, 2 * n + 2)
                    bank = banks[f"prep{n}"][:, :].rearrange("p (j m) -> p j m", j=2)
                    wait_past(act, p_ready, g, TILES, -TILES)
                    wait_past(act, write_ready, g, 2, n - 1)
                    take("G", g, n, keep[:, parity, tiles, :], bank, ACT.Exp, inc=False)
                    take("G", g, n, unkeep[:, tiles, :], bank, ACT.Exp, scale=-1.0)
                if name == "D":
                    wait_past(act, filled["Dt"], g, 1, 0)
                    take("D", g, 0, decay_rows[:, :], banks["prep0"][0:CHUNKS - 1, 0:SLOTS], ACT.Exp)
                if name == "st":
                    wait_past(act, filled["B"], g, TILES, -TILES)
                    take("st", g, n, write_t[:, parity, 2 * n:2 * n + 2, :, :],
                         banks[f"prep{n}"][:, :].rearrange("p (j a t) -> p j a t", j=2, a=PAIRS))

            def main(name, n, g, parity):
                if name == "H":
                    wait_past(act, filled["L"], g, TILES, 0)
                    take("H", g, n - 1, state_k[:, n, :], banks["state_ps"][:, 0:SLOTS], scale=QSCALE)
                if name == "L":
                    act.wait_ge(shifted_ready, TILES * g + n + 1)
                    wait_past(act, p_ready, g, TILES, n - TILES + 1)
                    act.activation(expd[:, n, :], logit[:, n, :], ACT.Exp).then_inc(exp_done, 1)
                if name == "pt":
                    wait_past(act, filled["o"], g, 1, 0)
                    take("pt", g, n, p_t[:, n, :, :], banks["pt"][:, 0:SLOTS].rearrange("p (a t) -> p a t", a=PAIRS))

            for name in STEPS:
                prepare(*step_of(name), 0, 0)

            def body(g, parity, ok):
                if ok(-1):
                    wait_past(act, filled["y"], g, 1, -1)
                    take("ont", g - 1, 0, on_t[:, :], banks["pt"][:, :])
                    wait_past(act, x_done, g, 1, -1)
                    take("y", g - 1, 0, y[:, :, :].rearrange("p j d -> p (j d)"), banks["l"][:, :])
                for name in STEPS:
                    if ok(1):
                        prepare(*step_of(name), g + 1, 1 - parity)
                    if ok(0):
                        main(*step_of(name), g, parity)

            turns(act, G, body)

        @block.tensor
        def _(pe):
            last = {n: None for n in banks}

            def claim(bank):
                if last[bank] is not None:
                    name, count = last[bank]
                    if not (isinstance(count, int) and count <= 0):
                        pe.wait_ge(taken[name], count)
                return banks[bank]

            def done(bank, ins, name, g, n=0):
                ins.then_inc(filled[name], 1)
                last[bank] = (name, per_seq[name] * g + n + 1)

            def prepare(name, n, g, parity):
                if name == "xt":
                    pe.wait_ge(xn_ready, g + 1)
                    ps = claim("prep0")
                    for j in range(TILES):
                        mm = pe.transpose(ps[:, j * P:(j + 1) * P], xn[:, j, :], c.ident[:, :])
                    done("prep0", mm, "xt", g)
                if name in ("q", "k"):
                    bank, w = ("prep1", w_q) if name == "q" else ("prep0", w_k)
                    pe.wait_ge(taken["xt"], g + 1)
                    ps = claim(bank)
                    done(bank, pe.matmul(ps[:, :], w[:, :], xn_t[:, :], start=True, stop=True), name, g)
                if name == "kt":
                    pe.wait_ge(taken["k"], g + 1)
                    ps = claim("prep1")
                    for j in range(TILES):
                        mm = pe.transpose(ps[:, j * P:(j + 1) * P], k_t[:, parity, j * P:(j + 1) * P], c.ident[:, :])
                    done("prep1", mm, "kt", g)
                if name == "vf":
                    for a in range(2):
                        j, bank = 2 * n + a, f"prep{a}"
                        ps = claim(bank)
                        done(bank, pe.matmul(ps[:, 0:D + SLOTS], xn_t[:, j * P:(j + 1) * P], w_vf[:, :],
                                             start=True, stop=True), "vf", g, j)
                if name == "G":
                    bank = f"prep{n}"
                    pe.wait_ge(gate_log_ready, TILES * g + 2 * n + 2)
                    ps = claim(bank)
                    for a in range(2):
                        mm = pe.matmul(ps[:, a * SLOTS:(a + 1) * SLOTS], sum_from_mid[:, :], gate_log[:, 2 * n + a, :],
                                       start=True, stop=True)
                    done(bank, mm, "G", g, n)
                if name == "D":
                    pe.wait_ge(gate_log_ready, TILES * g + TILES)
                    ps = claim("prep0")
                    for j in range(TILES):
                        mm = pe.matmul(ps[0:CHUNKS - 1, 0:SLOTS], between[:, j, :], gate_log[:, j, :],
                                       start=(j == 0), stop=(j == TILES - 1))
                    done("prep0", mm, "D", g)
                if name == "Dt":
                    pe.wait_ge(taken["D"], g + 1)
                    ps = claim("prep1")
                    for a in range(PAIRS):
                        mm = pe.matmul(ps[:, a * 8:a * 8 + CHUNKS - 1], decay_rows[:, a * P:(a + 1) * P],
                                       c.ident[0:CHUNKS - 1, 0:CHUNKS - 1], start=True, stop=True)
                    done("prep1", mm, "Dt", g)
                if name == "st":
                    bank = f"prep{n}"
                    pe.wait_ge(write_ready, 2 * g + n + 1)
                    ps = claim(bank)
                    for a in range(2):
                        for b in range(PAIRS):
                            at = (a * PAIRS + b) * P
                            mm = pe.transpose(ps[:, at:at + P], write[:, parity, 2 * n + a, b * P:(b + 1) * P],
                                              c.ident[:, :])
                    done(bank, mm, "st", g, n)

            def main(name, n, g, parity):
                tok = slice(n * P, (n + 1) * P)
                if name == "A":
                    pe.wait_ge(q_own_ready, H * (g + 1))
                    ps = claim("a")
                    mm = pe.matmul(ps[:, :], k_t[:, parity, tok], q_own[:, parity, n, :, :], start=True, stop=True)
                    done("a", mm, "A", g, n)
                if name == "U":
                    ps = claim("state_ps")
                    j, rows = n // 2, slice(CH * (n % 2), CH * (n % 2) + CH)
                    for a in range(PAIRS):
                        mm = pe.matmul(ps[:, a * P:(a + 1) * P], write[rows, parity, j, a * P:(a + 1) * P],
                                       kv[rows, parity, j, :, 2 * HK * a:2 * HK * (a + 1)], start=True, stop=True)
                    done("state_ps", mm, "U", g, n)
                if name == "H":
                    pe.wait_ge(state_ready, (CHUNKS - 1) * g + n)
                    ps = claim("state_ps")
                    for a in range(PAIRS):
                        mm = pe.transpose(ps[:, a * P:(a + 1) * P], state[:, n, a, 0, :], c.ident[:, :])
                    done("state_ps", mm, "H", g, n - 1)
                if name == "L":
                    pe.wait_ge(taken["A"], TILES * g + n + 1)
                    ps = claim("l")
                    for h in range(H):
                        mm = pe.matmul(ps[:, h * M:(h + 1) * M], a_sb[:, n, h, :], write[:, parity, n, h * M:(h + 1) * M],
                                       start=(h == 0), stop=False, skip_group_check=True)
                    for i in range(PER_TILE):
                        ch = PER_TILE * n + i
                        if ch == 0:
                            continue
                        pe.wait_ge(taken["H"], (CHUNKS - 1) * g + ch)
                        mm = pe.matmul(ps[CH * i:CH * i + CH, 0:SLOTS], q_t[:, parity, CH * ch:CH * ch + CH],
                                       state_k[:, ch, :], start=False, stop=True, skip_group_check=True)
                    done("l", mm, "L", g, n)
                if name == "pt":
                    pe.wait_ge(p_ready, TILES * g + n + 1)
                    ps = claim("pt")
                    for a in range(PAIRS):
                        mm = pe.transpose(ps[:, a * P:(a + 1) * P], p_keep[:, n, a * P:(a + 1) * P], c.ident[:, :])
                    done("pt", mm, "pt", g, n)
                if name == "B":
                    pe.wait_ge(p_own_ready, 2 * (TILES * g + n) + 2)
                    pe.wait_ge(taken["st"], 2 * g + n // 2 + 1)
                    ps = claim("b")
                    for a in range(PAIRS):
                        mm = pe.matmul(ps[:, 2 * a * P:2 * (a + 1) * P], write_t[:, parity, n, a, :],
                                       p_own[:, n, a, :, :], start=True, stop=True)
                    done("b", mm, "B", g, n)
                if name == "o":
                    pe.wait_ge(taken["B"], TILES * g + n + 1)
                    ps = claim("o_ps") if n == 0 else banks["o_ps"]
                    for h in range(H):
                        mm = pe.matmul(ps[:, n * D + h * HK:n * D + (h + 1) * HK], b_sb[:, n, h, :],
                                       kv[:, parity, n, 1, h * HK:(h + 1) * HK],
                                       start=(h == 0), stop=False, skip_group_check=True)
                    for i in range(PER_TILE):
                        ch = PER_TILE * n + i
                        if ch == 0:
                            continue
                        for a in range(PAIRS):
                            mm = pe.matmul(ps[CH * i:CH * i + CH, n * D:(n + 1) * D],
                                           p_t[:, n, a, CH * i:CH * i + CH], state[:, ch, a, 1, :],
                                           start=False, stop=(a == PAIRS - 1), skip_group_check=True)
                    if n == TILES - 1:
                        done("o_ps", mm, "o", g)

            pe.wait_ge(c.consts, 3)
            pe.wait_ge(loaded, 16 * (LOADS - 1))
            pe.wait_ge(consts_ready, 1)
            pe.wait_ge(wo_ready, 1)
            for name in STEPS:
                prepare(*step_of(name), 0, 0)

            def body(g, parity, ok):
                if not isinstance(g, int) or g >= 2:
                    last.update(prep0=("st", 2 * g + 1), prep1=("st", 2 * g + 2), a=("A", TILES * g),
                                b=("B", TILES * g), l=("L", TILES * g), pt=("pt", TILES * g),
                                state_ps=("H", (CHUNKS - 1) * g), o_ps=("o", g - 1))
                if ok(-1):
                    pe.wait_ge(on_ready, g)
                    ps = claim("pt")
                    for j in range(TILES):
                        mm = pe.transpose(ps[:, j * P:(j + 1) * P],
                                          on[:, :, :].rearrange("p (j h) d -> p j (h d)", j=TILES)[:, j, :], c.ident[:, :])
                    done("pt", mm, "ont", g - 1)
                    pe.wait_ge(taken["ont"], g)
                    ps = claim("l")
                    for j in range(TILES):
                        mm = pe.matmul(ps[:, j * D:(j + 1) * D], on_t[:, j * P:(j + 1) * P], w_o[:, :],
                                       start=True, stop=True)
                    done("l", mm, "y", g - 1)
                for name in STEPS:
                    if ok(1):
                        prepare(*step_of(name), g + 1, 1 - parity)
                    if ok(0):
                        main(*step_of(name), g, parity)

            turns(pe, G, body)

        @block.vector
        def _(dve):
            chain = Chain(dve, dve_chain, G, 12)
            link = chain.link

            def norm_in(g):
                ln_stats(dve, c, lambda j: tile_of(c, g, j), pre, link).then_inc(pre_var, 1)

            def scale_in(g):
                dve.wait_ge(pre_rstd, g + 1)
                wait_past(dve, filled["xt"], g, 1, 0)
                for j in range(TILES):
                    ins = dve.tensor_scalar(xn[:, j, :], tile_of(c, g, j), pre.meanvar[:, j, 0:1],
                                            pre.rstd[:, j:j + 1], ALU.subtract, ALU.mult)
                ins.then_inc(xn_ready, 1)

            def prepare(name, n, g, parity):
                if name == "vf":
                    dve.wait_ge(act_steps, (2 * g + n) * 4 + 3)
                    wait_past(dve, filled["D"], g, 1, 0)
                    for a in range(2):
                        dve.scalar_tensor_tensor(out=gate_log[:, 2 * n + a, :], in0=banks[f"prep{a}"][:, D:D + SLOTS],
                                                 scalar=0.0, in1=log_z[:, a, :], op0=ALU.min, op1=ALU.subtract)\
                           .then_inc(gate_log_ready, 1)
                        dve.wait_ge(gate_log_ready, TILES * g + 2 * n + a + 1)
                        dve.sem_inc(taken["vf"], 1)
                if name == "G":
                    dve.wait_ge(taken["G"], 2 * g + n + 1)
                    dve.wait_ge(act_steps, (2 * g + n) * 4 + 4)
                    wait_past(dve, filled["L"], g, TILES, -TILES)
                    tiles = slice(2 * n, 2 * n + 2)
                    dve.scalar_tensor_tensor(out=write[:, parity, tiles, :], in0=gate[:, tiles, :], scalar=1.0,
                                             in1=unkeep[:, tiles, :], op0=ALU.subtract, op1=ALU.mult)\
                       .then_inc(write_ready, 1)
                if name == "Dt":
                    dve.wait_ge(filled["Dt"], g + 1)
                    dve.tensor_copy(decay[:, parity, :, :], banks["prep1"][:, 0:16]
                                    .rearrange("p (a i) -> p a i", a=PAIRS)[:, :, 0:CHUNKS - 1]).then_inc(taken["Dt"], 1)

            def main(name, n, g, parity):
                def over(t):
                    return t.unsqueeze(2).broadcast_to([P, H, M])

                def heads(t):
                    return t.rearrange("p (h m) -> p h m", h=H)

                if name == "A":
                    dve.wait_ge(filled["A"], TILES * g + n + 1)
                    wait_past(dve, filled["L"], g, TILES, n - TILES + 1)
                    dve.tensor_tensor(a_sb[:, n, :, :], banks["a"][:, :].rearrange("p (h t) -> p h t", h=H),
                                      causal_q[:, :].unsqueeze(1).broadcast_to([P, H, P]), ALU.mult)\
                       .then_inc(taken["A"], 1)
                if name == "U":
                    dve.wait_ge(filled["U"], (CHUNKS - 1) * g + n + 1)
                    if n == 0:
                        dve.wait_ge(taken["Dt"], g + 1)
                        wait_past(dve, filled["o"], g, 1, 0)
                    for a in range(PAIRS):
                        factor = decay[:, parity, a, n:n + 1]
                        cols = slice(2 * HK * a, 2 * HK * (a + 1))
                        target = added[:, a] if n > 0 else state[:, 1, a, :, cols]
                        ins = dve.scalar_tensor_tensor(
                            out=target, in0=banks["state_ps"][:, a * P:(a + 1) * P].rearrange("p (w k) -> p w k", w=2),
                            scalar=factor, in1=own_head[:, :, :], op0=ALU.mult, op1=ALU.mult)
                    ins.then_inc(taken["U"], 1)
                    dve.wait_ge(taken["U"], (CHUNKS - 1) * g + n + 1)
                    if n > 0:
                        for a in range(PAIRS):
                            cols = slice(2 * HK * a, 2 * HK * (a + 1))
                            ins = dve.scalar_tensor_tensor(
                                out=state[:, n + 1, a, :, cols], in0=state[:, n, a, :, cols],
                                scalar=decay[:, parity, a, n:n + 1], in1=added[:, a], op0=ALU.mult, op1=ALU.add)
                    else:
                        ins = dve.memset(c.spare[:, :], 0.0)
                    ins.then_inc(state_ready, 1)
                    dve.wait_ge(state_ready, (CHUNKS - 1) * g + n + 1)
                if name == "L":
                    dve.wait_ge(filled["L"], TILES * g + n + 1)
                    wait_past(dve, exp_done, g, TILES, n - TILES + 1)
                    ins = dve.tensor_tensor(logit[:, n, :], banks["l"][:, 0:SLOTS], keep[:, parity, n, :], ALU.mult)
                    ins.then_inc(taken["L"], 1)
                    dve.wait_ge(taken["L"], TILES * g + n + 1)
                    link(dve.tensor_reduce(top[:, :], heads(logit[:, n, :]), AX.X, ALU.max))
                    dve.tensor_tensor(heads(logit[:, n, :]), heads(logit[:, n, :]), over(top[:, :]), ALU.subtract)\
                       .then_inc(shifted_ready, 1)
                if name == "pt":
                    dve.wait_ge(exp_done, TILES * g + n + 1)
                    wait_past(dve, filled["pt"], g, TILES, n - TILES + 1)
                    dve.tensor_tensor(p_keep[:, n, :], expd[:, n, :], keep[:, parity, n, :], ALU.mult)
                    dve.tensor_reduce(total[:, n * H:(n + 1) * H], heads(expd[:, n, :]), AX.X, ALU.add)\
                       .then_inc(p_ready, 1)
                    dve.wait_ge(p_ready, TILES * g + n + 1)
                if name == "B":
                    dve.wait_ge(filled["B"], TILES * g + n + 1)
                    wait_past(dve, filled["o"], g, 1, 0)
                    dve.tensor_tensor(b_sb[:, n, :, :], banks["b"][:, :].rearrange("p (h t) -> p h t", h=H),
                                      causal[:, :].unsqueeze(1).broadcast_to([P, H, P]), ALU.mult)\
                       .then_inc(taken["B"], 1)

            def take_o(g):
                wide = [P, TILES * H, HK]
                link(dve.reciprocal(inverse[:, :], total[:, :]))
                dve.wait_ge(filled["o"], g + 1)
                dve.tensor_tensor(o_sb[:, :, :], banks["o_ps"][:, :].rearrange("p (n d) -> p n d", d=HK),
                                  inverse[:, :].unsqueeze(2).broadcast_to(wide), ALU.mult).then_inc(taken["o"], 1)
                dve.wait_ge(taken["o"], g + 1)
                link(dve.tensor_tensor(o_sq[:, :, :], o_sb[:, :, :], o_sb[:, :, :], ALU.mult))
                link(dve.tensor_reduce(o_var[:, :], o_sq[:, :, :], AX.X, ALU.add))
                dve.tensor_scalar(o_var[:, :], o_var[:, :], 1.0 / HK, EPS, ALU.mult, ALU.add).then_inc(o_var_ready, 1)

            def scale_o(g):
                dve.wait_ge(o_rstd_ready, g + 1)
                wait_past(dve, filled["ont"], g, 1, 0)
                dve.tensor_tensor(on[:, :, :], o_sb[:, :, :],
                                  o_rstd[:, :].unsqueeze(2).broadcast_to([P, TILES * H, HK]), ALU.mult)\
                   .then_inc(on_ready, 1)

            def norm_out(g):
                dve.wait_ge(taken["y"], g + 1)
                ln_stats(dve, c, lambda j: y[:, j, :], post, link).then_inc(post_var, 1)

            def add_out(g):
                dve.wait_ge(post_rstd, g + 1)
                for j in range(TILES):
                    ins = dve.tensor_scalar(y[:, j, :], y[:, j, :], post.meanvar[:, j, 0:1],
                                            post.rstd[:, j:j + 1], ALU.subtract, ALU.mult)
                link(ins)
                dve.tensor_tensor(group_of(c, g), group_of(c, g), y[:, :, :], ALU.add).then_inc(x_done, 1)

            dve.wait_ge(masks, 2)
            link(dve.memset(early[:, :], 0.0))
            link(dve.memset(between[:, :, :], 0.0))
            link(dve.memset(own_head[:, :, :], 0.0))
            link(dve.memset(state[:, :, :, :, :], 0.0))
            link(dve.memset(neg_half[:, :], -0.5))
            link(dve.memset(causal[0:CH, CH:P], 0.0))
            for i in range(2):
                link(dve.memset(early[CH * i:CH * i + CH // 2, CH * i:CH * (i + 1)], 1.0))
                link(dve.memset(own_head[CH * i:CH * (i + 1), :, HK * i:HK * (i + 1)], 1.0))
            flat = between[:, :, :].rearrange("p j i -> p (j i)")
            step = CHUNKS - 1 + 2
            link(dve.memset(flat[32:64, 0::step], 1.0 / NORM))
            link(dve.memset(flat[64:96, 0::step], 1.0 / NORM))
            link(dve.memset(flat[0:32, step - 1::step], 1.0 / NORM))
            link(dve.memset(flat[96:128, 1::step], 1.0 / NORM))
            link(dve.tensor_scalar(causal_q[:, :], causal[:, :], QSCALE, None, ALU.mult))
            link(dve.tensor_tensor(sum_from_mid[:, :], causal[:, :], early[:, :], ALU.subtract))
            dve.tensor_scalar(sum_from_mid[:, :], sum_from_mid[:, :], 1.0 / NORM, None, ALU.mult).then_inc(consts_ready, 1)
            dve.wait_ge(loaded, 16 * (LOADS - 1))
            dve.tensor_scalar(w_o[:, :], w_o[:, :], norm_w[:, 0:1], None, ALU.mult).then_inc(wo_ready, 1)
            dve.wait_ge(c.loaded_first, 16)
            dve.wait_ge(c.loaded_rest, 16)
            norm_in(0)
            scale_in(0)
            for name in STEPS:
                prepare(*step_of(name), 0, 0)

            def body(g, parity, ok):
                chain.turn(g)
                if ok(-1):
                    take_o(g - 1)
                    scale_o(g - 1)
                if ok(1):
                    norm_in(g + 1)
                    scale_in(g + 1)
                if ok(-1):
                    norm_out(g - 1)
                    add_out(g - 1)
                for name in STEPS:
                    if ok(1):
                        prepare(*step_of(name), g + 1, 1 - parity)
                    if ok(0):
                        main(*step_of(name), g, parity)

            turns(dve, G, body)


def store_residual(c, out):
    with c.nc.semaphore("stored_all") as stored, c.nc.Block() as block:
        @block.sync
        def _(sp):
            sp.dma_start(out.rearrange("b (j p) d -> p (b j) d", p=P), c.x_res[:, :, :]).then_inc(stored, 16)
            sp.wait_ge(stored, 16)


def program(nc, x, out, ins, phases=(1, 2, 3, 4)):
    with ExitStack() as ctx:
        c = build_common(nc, ctx, x)
        if 1 in phases:
            gated_slots(c, *[ins["L0_attn_" + n] for n in ("Wq", "Wk", "Wv", "Wf", "g_norm_w", "Wo")])
        if 2 in phases:
            mixture_of_experts(c, *[ins["L0_ffn_" + n] for n in (
                "gate_w", "gate_b", "w1", "b1", "w3", "b3", "w2", "b2", "sw1", "sb1", "sw3", "sb3", "sw2", "sb2")])
        if 3 in phases:
            scratch = (nc.dram_tensor("parts_scratch", [2, 2, 3, P, SEQ], BF16).ap(),
                       nc.dram_tensor("max_scratch", [2, 3, 32, P], BF16).ap())
            softmax_attention(c, *[ins["L1_attn_" + n] for n in ("W_qkv", "b_qkv", "W_out", "b_out")], scratch)
        if 4 in phases:
            channel_mix(c, *[ins["L1_ffn_" + n] for n in ("W_r", "W_k", "W_v", "mu_r", "mu_k")], out)
        else:
            store_residual(c, out)


def kernel(**inputs):
    import numpy as np
    import concourse.bacc as bacc
    from concourse.bass_utils import run_bass_kernel_spmd

    nc = bacc.Bacc("TRN2", target_bir_lowering=False, num_devices=1)
    arrays, aps = {}, {}
    for name in inputs:
        a = np.ascontiguousarray(inputs[name])
        arrays["in_" + name] = a
        aps[name] = nc.dram_tensor("in_" + name, a.shape, mybir.dt.from_np(a.dtype), kind="ExternalInput").ap()
    x = aps.pop("L0_attn_x")
    out = nc.dram_tensor("out", x.shape, F32, kind="ExternalOutput").ap()
    program(nc, x, out, aps)
    return run_bass_kernel_spmd(nc, [arrays], core_ids=[0]).results[0]["out"]
```

```python
from contextlib import ExitStack

import concourse.bass as bass
import numpy as np
from concourse import mybir

ALU = mybir.AluOpType
ACT = mybir.ActivationFunctionType
AX = mybir.AxisListType
F32 = mybir.dt.float32
BF16 = mybir.dt.bfloat16

P = 128
D = 128
SEQ = 512
TILES = SEQ // P
EPS = 1e-5


class LayerSemaphores:

    def __init__(self, nc):
        self.nc, self.held = nc, []

    def get(self, name):
        self.held.append(self.nc.alloc_semaphore(name))
        return self.held[-1]

    def __enter__(self):
        return self

    def __exit__(self, *_):
        self.nc.clear_and_free_semaphores(self.held)
        self.nc.all_engine_barrier()


class Common:
    pass


def parse_steps(text, ahead):
    steps = []
    for word in text.split():
        name = word.rstrip("0123456789+-")
        number = "".join(ch for ch in word if ch.isdigit())
        steps.append((name, int(number or 0), 2 if "+" in word else -1 if "-" in word else int(name in ahead or word in ahead)))
    return steps


def run_steps(steps, g, parity, ok, run):
    for name, n, shift in steps:
        if ok(shift):
            run(name, n, g + shift, (parity + shift) % 2)


def first_steps(steps, run):
    run("ni", 0, 0, 0)
    if ("si", 0, 2) in steps:
        run("si", 0, 0, 0)
    run_steps(steps, -1, 1, lambda shift: shift >= 1, run)


def ln_stats(dve, c, source, bufs, link):
    for j in range(TILES):
        ins = dve.bn_stats(bufs.stats[:, j, :], source(j))
    link(ins)
    dve.memset(c.spare[:, :], 0.0)
    for j in range(TILES):
        ins = dve.bn_aggr(bufs.meanvar[:, j, :], bufs.stats[:, j, :])
    link(ins)
    return dve.tensor_scalar(bufs.vareps[:, :], bufs.meanvar[:, :, 1], EPS, None, ALU.add)


def build_common(nc, ctx, x_in):
    c = Common()
    c.nc = nc
    c.groups = x_in.shape[0]
    c.x_res = ctx.enter_context(nc.sbuf_tensor("x_res", [P, c.groups * TILES, D], F32))
    c.ident = ctx.enter_context(nc.sbuf_tensor("ident", [P, P], F32))
    c.neg_half = ctx.enter_context(nc.sbuf_tensor("neg_half", [P, TILES], F32))
    c.zero = ctx.enter_context(nc.sbuf_tensor("zero", [P, 1], F32))
    c.spare = ctx.enter_context(nc.sbuf_tensor("spare", [P, 1], F32))
    c.loaded_first = ctx.enter_context(nc.semaphore("x_first_loaded"))
    c.loaded_rest = ctx.enter_context(nc.semaphore("x_rest_loaded"))
    c.consts = ctx.enter_context(nc.semaphore("consts_ready"))
    c.ident_zero = ctx.enter_context(nc.semaphore("ident_zeroed"))
    tokens = x_in.rearrange("b (j p) d -> p (b j) d", p=P)
    first = 2 * TILES
    with nc.Block() as block:
        @block.sync
        def _(sp):
            sp.dma_start(c.x_res[:, 0:first, :], tokens[:, 0:first, :]).then_inc(c.loaded_first, 16)
            sp.dma_start(c.x_res[:, first:, :], tokens[:, first:, :]).then_inc(c.loaded_rest, 16)

        @block.gpsimd
        def _(pool):
            pool.memset(c.neg_half[:, :], -0.5).then_inc(c.consts, 1)
            pool.memset(c.zero[:, :], 0.0).then_inc(c.consts, 1)
            pool.memset(c.ident[:, :], 0.0).then_inc(c.ident_zero, 1)
            pool.wait_ge(c.ident_zero, 1)
            pool.affine_select(out=c.ident[:, :], in_=c.ident[:, :], compare_op=ALU.not_equal, fill=1.0,
                               base=0, pattern=[[-1, P]], channel_multiplier=1).then_inc(c.consts, 1)
    return c


def tile_of(c, g, j):
    return c.x_res[:, bass.ds(g * TILES + j, 1), :].rearrange("p a d -> p (a d)")


def group_of(c, g):
    return c.x_res[:, bass.ds(g * TILES, TILES), :]


class LnBufs:
    def __init__(self, sb, name):
        self.stats = sb(name + "_stats", [P, TILES, 6], F32)
        self.meanvar = sb(name + "_meanvar", [P, TILES, 2], F32)
        self.vareps = sb(name + "_vareps", [P, TILES], F32)
        self.rstd = sb(name + "_rstd", [P, TILES], F32)


class Ahead:

    def __init__(self, c, ctx, ins):
        nc = c.nc

        def sb(name, shape):
            return ctx.enter_context(nc.sbuf_tensor("ahead_" + name, shape, F32))

        gate_w, gate_b, w1, b1, w3, b3, w2, b2, sw1, sb1, sw3, sb3, sw2, sb2 = (ins["L0_ffn_" + n] for n in (
            "gate_w", "gate_b", "w1", "b1", "w3", "b3", "w2", "b2", "sw1", "sb1", "sw3", "sb3", "sw2", "sb2"))
        E, _, HID = w1.shape
        N_E = E + 1
        hidden = N_E * HID
        chunks = -(-hidden // P)
        routed = E * HID // P
        last = hidden - (chunks - 1) * P
        self.area = sb("area", [P, 2 * hidden])
        self.up = [self.area[:, n * hidden:(n + 1) * hidden] for n in range(2)]
        self.up_bias = [sb(f"up_bias{n}", [P, chunks]) for n in range(2)]
        self.down_bias = sb("down_bias", [3 * N_E, D])
        self.gate_raw, self.gate_bias = sb("gate_raw", [E, D]), sb("gate_bias", [P, E])
        self.experts_loaded = ctx.enter_context(nc.semaphore("experts_loaded"))
        experts = []
        for n, (w, sw, b, s_b) in enumerate(((w1, sw1, b1, sb1), (w3, sw3, b3, sb3))):
            experts += [
                (self.up[n][:, 0:E * HID].rearrange("p (e h) -> p e h", e=E), w.rearrange("e d h -> d e h")),
                (self.up[n][:, E * HID:], sw),
                (self.up_bias[n][:, 0:routed], b.rearrange("e h -> (e h)").rearrange("(c p) -> p c", p=P)),
                (self.up_bias[n][:, routed:routed + 1], s_b[0:P].rearrange("(p a) -> p a", a=1)),
                (self.up_bias[n][0:last, routed + 1:chunks], s_b[P:HID].rearrange("(p a) -> p a", a=1))]
        experts += [(self.gate_raw[:, :], gate_w), (self.gate_bias[:, :], gate_b.partition_broadcast(P))]
        for n in range(3):
            experts += [(self.down_bias[n * N_E:n * N_E + E, :], b2),
                        (self.down_bias[n * N_E + E:(n + 1) * N_E, :], sb2.rearrange("(a d) -> a d", a=1))]

        W_qkv, b_qkv, W_out, b_out = (ins["L1_attn_" + n] for n in ("W_qkv", "b_qkv", "W_out", "b_out"))
        H = 16
        DH = D // H
        self.w_qkv, self.w_out = sb("w_qkv", [P, 3 * D]), sb("w_out", [P, D])
        self.bias_qk, self.bias_v, self.bias_out = sb("bias_qk", [P, 2]), sb("bias_v", [P, 3 * D]), sb("bias_out", [P, D])
        self.attention_loaded = ctx.enter_context(nc.semaphore("attention_loaded"))
        per_head = b_qkv.rearrange("(h c d) -> c d h", h=H, c=3)
        attention = [(self.w_qkv[:, :], W_qkv), (self.w_out[:, :], W_out),
                     (self.bias_v[:, :], b_qkv.partition_broadcast(P)),
                     (self.bias_out[:, :], b_out.partition_broadcast(P))]
        attention += [(self.bias_qk[d * H:(d + 1) * H, n:n + 1], per_head[n, d, :].rearrange("(h a) -> h a", a=1))
                      for n in range(2) for d in range(DH)]

        self.w_mix, self.mu = sb("w_mix", [P, 3, D]), sb("mu", [P, 2])
        self.mix_loaded = ctx.enter_context(nc.semaphore("mix_loaded"))
        mix = [(self.w_mix[:, n, :], ins["L1_ffn_" + w]) for n, w in enumerate(("W_r", "W_k", "W_v"))]
        mix += [(self.mu[:, n:n + 1], ins["L1_ffn_" + m].rearrange("(p a) -> p a", a=1))
                for n, m in enumerate(("mu_r", "mu_k"))]
        self.groups = ((experts, self.experts_loaded), (attention, self.attention_loaded), (mix, self.mix_loaded))
        self.experts_count, self.attention_count, self.mix_count = (16 * len(g) for g, _ in self.groups)

    def load(self, sp):
        for transfers, loaded in self.groups:
            for target, source in transfers:
                sp.dma_start(target, source, allow_slow_non_contiguous=True).then_inc(loaded, 16)


def channel_mix(c, ahead, out):
    nc = c.nc
    G = c.groups
    STEPS = parse_steps("si k sq ni+ r xt yn- v mx y ad- no", ("si", "xt", "mx"))
    with ExitStack() as ctx:
        semaphores = ctx.enter_context(LayerSemaphores(nc))

        def sb(name, shape, dt):
            return ctx.enter_context(nc.sbuf_tensor("cm_" + name, shape, dt))

        def sem(name):
            return semaphores.get("cm_" + name)

        def bank(name):
            return ctx.enter_context(nc.psum_tensor("cm_" + name, [P, 512], F32))

        w_raw, mu = ahead.w_mix, ahead.mu
        w_t = sb("w_t", [P, 3, D], F32)
        one_minus_mu = sb("one_minus_mu", [P, 2], F32)
        pre, post = LnBufs(sb, "pre"), LnBufs(sb, "post")
        xn = sb("xn", [P, 2, TILES, D], F32)
        xn_t = sb("xn_t", [P, 2, SEQ + 1], F32)
        scaled = sb("scaled", [P, 2, 2, SEQ], F32)
        mixed = sb("mixed", [P, 2, 2, SEQ], F32)
        k_relu = sb("k_relu", [P, 2, SEQ], F32)
        k_act = sb("k_act", [P, 2, SEQ], F32)
        r_sb = sb("r_sb", [P, 2, SEQ], F32)
        y = sb("y", [P, 2, TILES, D], F32)
        yn = sb("yn", [P, TILES, D], F32)
        xn_ps = [bank(f"xn_ps{i}") for i in range(2)]
        r_ps = [bank(f"r_ps{i}") for i in range(2)]
        k_ps = bank("k_ps")
        v_ps = [bank(f"v_ps{i}") for i in range(2)]
        w_ps = bank("w_ps")

        w_turned, w_ready = sem("w_turned"), sem("w_ready")
        mu_ready = sem("mu_ready")
        edge_zeroed = sem("edge_zeroed")
        pre_var, pre_rstd = sem("pre_var"), sem("pre_rstd")
        post_var, post_rstd = sem("post_var"), sem("post_rstd")
        xn_ready, xn_turned = sem("xn_ready"), sem("xn_turned")
        xn_t_ready, scaled_ready, mixed_ready = sem("xn_t_ready"), sem("scaled_ready"), sem("mixed_ready")
        k_done, k_relu_ready, k_act_ready = sem("k_done"), sem("k_relu_ready"), sem("k_act_ready")
        r_done, r_ready, v_done = sem("r_done"), sem("r_ready"), sem("v_done")
        y_ready, yn_ready = sem("y_ready"), sem("yn_ready")
        x_done, stored = sem("x_done"), sem("stored")
        dve_chain = sem("dve_chain")

        block = ctx.enter_context(nc.Block())
        out_tokens = out.rearrange("b (j p) d -> b p j d", p=P)

        @block.sync
        def _(sp):
            with sp.Fori(0, G) as g:
                sp.wait_ge(x_done, g + 1)
                sp.dma_start(out_tokens[bass.ds(g, 1), :, :, :].rearrange("b p j d -> (b p) j d"),
                             group_of(c, g)).then_inc(stored, 16)
            sp.wait_ge(stored, 16 * G)

        @block.gpsimd
        def _(pool):
            def rstd(bufs, var, done, g):
                pool.wait_ge(var, g + 1)
                pool.tensor_tensor(bufs.rstd[:, :], bufs.vareps[:, :], c.neg_half[:, :], ALU.pow).then_inc(done, 1)

            def run(name, n, g, parity):
                if name == "ni":
                    rstd(pre, pre_var, pre_rstd, g)
                if name == "no":
                    rstd(post, post_var, post_rstd, g)
                if name == "sq":
                    pool.wait_ge(k_relu_ready, g + 1)
                    wait_past(pool, v_done, g, 1, -1)
                    pool.tensor_tensor(k_act[:, parity, :], k_relu[:, parity, :], k_relu[:, parity, :],
                                       ALU.mult).then_inc(k_act_ready, 1)
                if name == "ad":
                    pool.wait_ge(yn_ready, g + 1)
                    pool.tensor_tensor(group_of(c, g), group_of(c, g), yn[:, :, :], ALU.add).then_inc(x_done, 1)

            first_steps(STEPS, run)
            turns(pool, G, lambda g, parity, ok: run_steps(STEPS, g, parity, ok, run))

        @block.scalar
        def _(act):
            act.wait_ge(w_turned, 1)
            act.copy(w_t[:, :, :].rearrange("p n d -> p (n d)"), w_ps[:, 0:3 * D]).then_inc(w_ready, 1)
            act.wait_ge(ahead.mix_loaded, ahead.mix_count)
            act.activation(one_minus_mu[:, :], mu[:, :], ACT.Copy, bias=1.0, scale=-1.0).then_inc(mu_ready, 1)

            def run(name, n, g, parity):
                if name == "xt":
                    act.wait_ge(xn_turned, g + 1)
                    wait_past(act, mixed_ready, g, 2, -2)
                    act.copy(xn_t[:, parity, 1:SEQ + 1], xn_ps[parity][:, :]).then_inc(xn_t_ready, 1)
                    for i in range(2):
                        act.activation(scaled[:, parity, i, :], xn_ps[parity][:, :], ACT.Copy,
                                       scale=mu[:, i:i + 1]).then_inc(scaled_ready, 1)
                if name == "k":
                    act.wait_ge(k_done, g + 1)
                    wait_past(act, k_act_ready, g, 1, -1)
                    act.activation(k_relu[:, parity, :], k_ps[:, :], ACT.Relu).then_inc(k_relu_ready, 1)
                if name == "r":
                    act.wait_ge(r_done, g + 1)
                    wait_past(act, y_ready, g, 1, -1)
                    act.activation(r_sb[:, parity, :], r_ps[parity][:, :], ACT.Sigmoid).then_inc(r_ready, 1)

            first_steps(STEPS, run)
            turns(act, G, lambda g, parity, ok: run_steps(STEPS, g, parity, ok, run))

        @block.tensor
        def _(pe):
            pe.wait_ge(c.consts, 3)
            pe.wait_ge(ahead.mix_loaded, ahead.mix_count)
            for n in range(3):
                mm = pe.transpose(w_ps[:, n * D:(n + 1) * D], w_raw[:, n, :], c.ident[:, :])
            mm.then_inc(w_turned, 1)
            pe.wait_ge(w_ready, 1)

            def run(name, n, g, parity):
                if name == "xt":
                    pe.wait_ge(xn_ready, g + 1)
                    wait_past(pe, scaled_ready, g, 2, -2)
                    for j in range(TILES):
                        mm = pe.transpose(xn_ps[parity][:, j * P:(j + 1) * P], xn[:, parity, j, :], c.ident[:, :])
                    mm.then_inc(xn_turned, 1)
                if name == "k":
                    pe.wait_ge(mixed_ready, 2 * g + 2)
                    wait_past(pe, k_relu_ready, g, 1, 0)
                    pe.matmul(k_ps[:, :], w_t[:, 1, :], mixed[:, parity, 1, :], start=True, stop=True).then_inc(k_done, 1)
                if name == "r":
                    pe.wait_ge(mixed_ready, 2 * g + 2)
                    wait_past(pe, r_ready, g, 1, -1)
                    for j in range(TILES):
                        mm = pe.matmul(r_ps[parity][:, j * P:(j + 1) * P], mixed[:, parity, 0, j * P:(j + 1) * P],
                                       w_t[:, 0, :], start=True, stop=True)
                    mm.then_inc(r_done, 1)
                if name == "v":
                    pe.wait_ge(k_act_ready, g + 1)
                    wait_past(pe, y_ready, g, 1, -1)
                    for j in range(TILES):
                        mm = pe.matmul(v_ps[parity][:, j * P:(j + 1) * P], k_act[:, parity, j * P:(j + 1) * P],
                                       w_t[:, 2, :], start=True, stop=True)
                    mm.then_inc(v_done, 1)

            first_steps(STEPS, run)
            turns(pe, G, lambda g, parity, ok: run_steps(STEPS, g, parity, ok, run))

        @block.vector
        def _(dve):
            chain = Chain(dve, dve_chain, G, 4)
            link = chain.link

            def run(name, n, g, parity):
                if name == "ni":
                    ln_stats(dve, c, lambda j: tile_of(c, g, j), pre, link).then_inc(pre_var, 1)
                if name == "si":
                    dve.wait_ge(pre_rstd, g + 1)
                    wait_past(dve, xn_turned, g, 1, -1)
                    for j in range(TILES):
                        ins = dve.tensor_scalar(xn[:, parity, j, :], tile_of(c, g, j), pre.meanvar[:, j, 0:1],
                                                pre.rstd[:, j:j + 1], ALU.subtract, ALU.mult)
                    ins.then_inc(xn_ready, 1)
                if name == "mx":
                    dve.wait_ge(xn_t_ready, g + 1)
                    wait_past(dve, r_done, g, 1, -1)
                    for i in (0, 1):
                        dve.wait_ge(scaled_ready, 2 * g + i + 1)
                        dve.scalar_tensor_tensor(out=mixed[:, parity, i, :], in0=xn_t[:, parity, 0:SEQ],
                                                 scalar=one_minus_mu[:, i:i + 1], in1=scaled[:, parity, i, :],
                                                 op0=ALU.mult, op1=ALU.add).then_inc(mixed_ready, 1)
                if name == "y":
                    dve.wait_ge(v_done, g + 1)
                    dve.wait_ge(r_ready, g + 1)
                    wait_past(dve, yn_ready, g, 1, -1)
                    dve.tensor_tensor(y[:, parity, :, :].rearrange("p j d -> p (j d)"), r_sb[:, parity, :],
                                      v_ps[parity][:, :], ALU.mult).then_inc(y_ready, 1)
                if name == "no":
                    dve.wait_ge(y_ready, g + 1)
                    ln_stats(dve, c, lambda j: y[:, parity, j, :], post, link).then_inc(post_var, 1)
                if name == "yn":
                    dve.wait_ge(post_rstd, g + 1)
                    wait_past(dve, x_done, g, 1, 0)
                    for j in range(TILES):
                        ins = dve.tensor_scalar(yn[:, j, :], y[:, parity, j, :], post.meanvar[:, j, 0:1],
                                                post.rstd[:, j:j + 1], ALU.subtract, ALU.mult)
                    ins.then_inc(yn_ready, 1)

            dve.memset(xn_t[:, :, 0:1], 0.0).then_inc(edge_zeroed, 1)
            dve.wait_ge(edge_zeroed, 1)
            dve.wait_ge(c.loaded_first, 16)
            dve.wait_ge(c.loaded_rest, 16)
            dve.wait_ge(mu_ready, 1)
            first_steps(STEPS, run)

            def body(g, parity, ok):
                chain.turn(g)
                run_steps(STEPS, g, parity, ok, run)

            turns(dve, G, body)


def softmax_attention(c, ahead, scratch):
    nc = c.nc
    G = c.groups
    H = 16
    DH = D // H
    QUADS = H // 4
    HALF = H // 2
    PARTS = 3
    ROWS = PARTS * PARTS * DH
    MAX_ROW = P - PARTS
    TWO_ONES = float(np.array([0x3F803F80], np.uint32).view(np.float32)[0])
    VW = DH + 1
    SCALE = float(DH) ** -0.5
    AHEAD = ("A", "mx0", "tmx0", "v", "tv")
    STEPS = parse_steps(
        "tot2- ni+ V12- A0 B0 A1 A2 B1 A3 V13- mx1 tmx1 A4 B2 A5 A6 B3 A7 A8 B4 A9 V14- A10 B5 A11 A12 B6 "
        "A13 V15- xt+ txt+ A14 to3- B7 A15 q+ ot3- tq+ A16 tot3- B8 A17 V0 A18 B9 A19 A20 B10 A21 V1 A22 "
        "B11 A23 k+ tk+ A24 B12 A25 V2 A26 B13 A27 at- tat- A28 B14 A29 V3 to0 A30 B15 A31 A32 B16 A33 A34 "
        "V4 A35 B17 A36 ot0 y- tot0 B18 V5 ty- A37 A38 B19 A39 V6 A40 mx0 B20 A41 tmx0 A42 B21 A43 A44 B22 "
        "v A45 tv V7 to1 A46 B23 A47 ot1 tot1 A48 B24 A49 V8 A50 B25 A51 A52 B26 A53 V9 A54 B27 A55 A56 B28 "
        "A57 V10 A58 B29 A59 A60 B30 A61 V11 to2 A62 B31 A63 ot2", AHEAD)
    A_N = H * TILES
    B_N = H * TILES // 2

    with ExitStack() as ctx:
        semaphores = ctx.enter_context(LayerSemaphores(nc))

        def sb(name, shape, dt):
            return ctx.enter_context(nc.sbuf_tensor("sa_" + name, shape, dt))

        def sem(name):
            return semaphores.get("sa_" + name)

        def bank(name, n=1):
            return ctx.enter_context(nc.psum_tensor("sa_" + name, [P, 512 * n], F32))

        w_raw, w_o, bias_qk = ahead.w_qkv, ahead.w_out, ahead.bias_qk
        bias_v, bias_o = ahead.bias_v, ahead.bias_out
        pre, post = LnBufs(sb, "pre"), LnBufs(sb, "post")
        xn = sb("xn", [P, TILES, D], F32)
        xn_t = sb("xn_t", [P, 2, SEQ], F32)
        qk = sb("qk", [P, 2, SEQ], F32)
        rest = sb("rest", [P, 2, SEQ], F32)
        parts = sb("parts", [P, 2, PARTS, SEQ], BF16)
        q_rows = sb("q_rows", [P, 2, H, SEQ], BF16)
        k_rows = sb("k_rows", [P, 2, H, SEQ], BF16)
        at = [0]

        def cut(*shape):
            size = int(np.prod(shape))
            at[0] += size
            return ahead.area[:, at[0] - size:at[0]]

        v_one = cut(2, TILES, H, VW).rearrange("p (g j h w) -> p g j h w", g=2, j=TILES, h=H)
        o_t = cut(2, SEQ).rearrange("p (g t) -> p g t", g=2)
        attn_t = cut(SEQ)
        w_q, w_k, w_v = cut(D), cut(D), cut(D)
        maxima = sb("maxima", [P, 2, A_N], F32)
        neg_max = sb("neg_max", [32, D], F32)
        max_rest = sb("max_rest", [32, D], F32)
        max_parts = sb("max_parts", [32, PARTS, D], BF16)
        probs = sb("probs", [P, 8, TILES, SEQ], F32)
        rsum = sb("rsum", [P, TILES, 4], F32)
        attn = sb("attn", [P, TILES, H, DH], F32)
        y = sb("y", [P, TILES, D], F32)

        ring = [bank(f"ring{i}")[:, :] for i in range(3)]
        users = [(name, n) for name, n, _ in STEPS if name in ("A", "xt", "q", "k", "v", "mx", "ot", "at", "y")]

        def ring_bank(name, n=0):
            return ring[users.index((name, n)) % 3]

        b_ps = [bank(f"b_ps{i}", 2) for i in range(2)]
        o_ps = bank("o_ps")

        w_ready, bias_ready = sem("w_ready"), sem("bias_ready")
        edges_set, zeros_set, o_cleared = sem("edges_set"), sem("zeros_set"), sem("o_cleared")
        pre_var, pre_rstd = sem("pre_var"), sem("pre_rstd")
        post_var, post_rstd = sem("post_var"), sem("post_rstd")
        xn_ready = sem("xn_ready")
        pre_centred, post_centred, y_scaled = sem("pre_centred"), sem("post_centred"), sem("y_scaled")
        per_seq = {"A": A_N, "xt": 1, "q": 1, "k": 1, "v": 1, "mx": 2, "ot": QUADS, "at": 1, "y": 1}
        filled = {n: sem(n + "_filled") for n in per_seq}
        taken = {n: sem(n + "_taken") for n in per_seq}
        split = sem("split_steps")
        max_split = sem("max_split_steps")
        parts_stored, max_stored = sem("parts_stored"), sem("max_stored")
        rows_loaded = [[sem(f"rows_loaded{i}{n}") for n in range(2)] for i in range(2)]
        max_loaded = sem("max_loaded")
        a_filled, a_taken = filled["A"], taken["A"]
        b_filled, exp_done = sem("b_filled"), sem("exp_done")
        pv_done, o_taken = sem("pv_done"), sem("o_taken")
        x_done = sem("x_done")
        chain_sem = sem("dve_chain")

        parts_dram, max_dram = scratch
        block = ctx.enter_context(nc.Block())

        @block.sync
        def _(sp):
            def value(v):
                return v if isinstance(v, int) else sp.snap(v)

            def values_of_parts(g, parity):
                return value(48 * (g - parity)), value(4 * (g + 1)), value(32 * (g + 1))

            def store_parts(parity, again, loads, splits):
                if again:
                    for half in range(2):
                        sp.wait_ge(rows_loaded[parity][half], loads)
                sp.wait_ge(split, splits)
                for n in range(2):
                    sp.dma_start(parts_dram[parity, n].rearrange("i c t -> c i t"), parts[:, n, :, :])\
                      .then_inc(parts_stored, 16)

            def load_rows(parity, half, stores, reads):
                if stores is not None:
                    sp.wait_ge(parts_stored, stores)
                if reads is not None:
                    sp.wait_ge(b_filled, reads)
                heads = slice(half * HALF, (half + 1) * HALF)
                q_src, k_src = (parts_dram[parity, n].rearrange("i (d h) t -> i d h t", h=H) for n in range(2))
                for i in range(PARTS):
                    sp.dma_start(q_rows[i * PARTS * DH:(i + 1) * PARTS * DH, parity, heads, :],
                                 q_src.rearrange("i d h t -> (i d) h t")[:, heads, :])\
                      .then_inc(rows_loaded[parity][half], 16)
                    sp.dma_start(k_rows[i * PARTS * DH:(i + 1) * PARTS * DH, parity, heads, :],
                                 k_src[i][:, heads, :].unsqueeze(0).broadcast_to([PARTS, DH, HALF, SEQ]))\
                      .then_inc(rows_loaded[parity][half], 16)

            def values_of_max(n):
                return value(4 * n + 4), value(16 * n - 16), value(16 * n + 16)

            def load_max(parity, half, again, splits, loads, stores):
                sp.wait_ge(max_split, splits)
                if again:
                    sp.wait_ge(max_loaded, loads)
                sp.dma_start(max_dram[half].rearrange("i a t -> a i t"), max_parts[:, :, :]).then_inc(max_stored, 16)
                sp.wait_ge(max_stored, stores)
                sp.dma_start(q_rows[MAX_ROW:P, parity, half * HALF:(half + 1) * HALF, :],
                             max_dram[half].rearrange("i (h q) t -> i h (q t)", q=TILES)).then_inc(max_loaded, 16)

            for g in range(2):
                sp.wait_ge(edges_set, 2 + g)
                sp.wait_ge(zeros_set, 1 + g)
                store_parts(g, False, 0, 4 * (g + 1))
                for half in range(2):
                    load_rows(g, half, 32 * (g + 1) if half == 0 else None, None)
            load_max(0, 0, False, *values_of_max(0))

            def body(g, parity, ok):
                reads = [value(B_N * g + B_N // 2 * (half + 1)) for half in range(2)]
                loads, splits, stores = values_of_parts(g + 2, parity)
                max_now, max_next = values_of_max(2 * g + 1), values_of_max(2 * g + 2)
                if ok(0):
                    load_max(parity, 1, not isinstance(g, int) or g > 0, *max_now)
                if ok(2):
                    store_parts(parity, True, loads, splits)
                    load_rows(parity, 0, stores, reads[0])
                if ok(1):
                    load_max(1 - parity, 0, True, *max_next)
                if ok(2):
                    load_rows(parity, 1, None, reads[1])

            turns(sp, G, body)

        @block.gpsimd
        def _(pool):
            def rstd(bufs, var, done, g):
                pool.wait_ge(var, g + 1)
                pool.tensor_tensor(bufs.rstd[:, :], bufs.vareps[:, :], c.neg_half[:, :], ALU.pow).then_inc(done, 1)

            def scale_in(g):
                rstd(pre, pre_var, pre_rstd, g)
                pool.wait_ge(pre_rstd, g + 1)
                wait_past(pool, filled["xt"], g, 1, 0)
                wide = [P, TILES, D]
                pool.tensor_tensor(xn[:, :, :], group_of(c, g), pre.meanvar[:, :, 0:1].broadcast_to(wide), ALU.subtract)\
                    .then_inc(pre_centred, 1)
                pool.wait_ge(pre_centred, g + 1)
                pool.tensor_tensor(xn[:, :, :], xn[:, :, :], pre.rstd[:, :].unsqueeze(2).broadcast_to(wide), ALU.mult)\
                    .then_inc(xn_ready, 1)

            def norm_out(g):
                rstd(post, post_var, post_rstd, g)
                pool.wait_ge(post_rstd, g + 1)
                wide = [P, TILES, D]
                pool.tensor_tensor(y[:, :, :], y[:, :, :], post.meanvar[:, :, 0:1].broadcast_to(wide), ALU.subtract)\
                    .then_inc(post_centred, 1)
                pool.wait_ge(post_centred, g + 1)
                pool.tensor_tensor(y[:, :, :], y[:, :, :], post.rstd[:, :].unsqueeze(2).broadcast_to(wide), ALU.mult)\
                    .then_inc(y_scaled, 1)
                pool.wait_ge(y_scaled, g + 1)
                pool.tensor_tensor(group_of(c, g), group_of(c, g), y[:, :, :], ALU.add).then_inc(x_done, 1)

            def zeros(*shape):
                return c.zero[:, :].unsqueeze(1).broadcast_to([P, *shape])

            def split_qk(g):
                pool.wait_ge(taken["q"], g + 1)
                pool.wait_ge(taken["k"], g + 1)
                if not (isinstance(g, int) and g == 0):
                    pool.wait_ge(parts_stored, 32 * g)
                pool.tensor_tensor(parts[:, :, 0, :], qk[:, :, :], zeros(2, SEQ), ALU.add).then_inc(split, 1)
                pool.wait_ge(split, 4 * g + 1)
                pool.tensor_tensor(rest[:, :, :], qk[:, :, :], parts[:, :, 0, :], ALU.subtract).then_inc(split, 1)
                pool.wait_ge(split, 4 * g + 2)
                pool.tensor_tensor(parts[:, :, 1, :], rest[:, :, :], zeros(2, SEQ), ALU.add).then_inc(split, 1)
                pool.wait_ge(split, 4 * g + 3)
                pool.tensor_tensor(parts[:, :, 2, :], rest[:, :, :], parts[:, :, 1, :], ALU.subtract).then_inc(split, 1)

            def split_max(g, half):
                n = 2 * g + half
                pool.wait_ge(taken["mx"], n + 1)
                if not (isinstance(n, int) and n == 0):
                    pool.wait_ge(max_stored, 16 * n)
                pool.tensor_tensor(max_parts[:, 0, :], neg_max[:, :], c.zero[0:32, :].broadcast_to([32, D]), ALU.add).then_inc(max_split, 1)
                pool.wait_ge(max_split, 4 * n + 1)
                pool.tensor_tensor(max_rest[:, :], neg_max[:, :], max_parts[:, 0, :], ALU.subtract).then_inc(max_split, 1)
                pool.wait_ge(max_split, 4 * n + 2)
                pool.tensor_tensor(max_parts[:, 1, :], max_rest[:, :], c.zero[0:32, :].broadcast_to([32, D]), ALU.add).then_inc(max_split, 1)
                pool.wait_ge(max_split, 4 * n + 3)
                pool.tensor_tensor(max_parts[:, 2, :], max_rest[:, :], max_parts[:, 1, :], ALU.subtract).then_inc(max_split, 1)

            pool.wait_ge(c.consts, 3)
            pool.memset(v_one[:, :, :, :, DH:VW], 1.0).then_inc(edges_set, 1)
            pool.wait_ge(edges_set, 1)
            for g in range(2):
                scale_in(g)
                pool.wait_ge(xn_ready, g + 1)
                pool.memset(k_rows[64:P, g, :, :].rearrange("p h t -> p (h t)").bitcast(F32), TWO_ONES)\
                    .then_inc(edges_set, 1)
                pool.wait_ge(edges_set, g + 2)
                split_qk(g)
            split_max(0, 0)

            def body(g, parity, ok):
                if ok(0):
                    split_max(g, 1)
                if ok(2):
                    scale_in(g + 2)
                    split_qk(g + 2)
                if ok(-1):
                    norm_out(g - 1)
                if ok(1):
                    split_max(g + 1, 0)

            turns(pool, G, body)

        @block.scalar
        def _(act):
            act.wait_ge(ahead.attention_loaded, ahead.attention_count)
            act.mul(bias_qk[:, 0:1], bias_qk[:, 0:1], SCALE).then_inc(bias_ready, 1)
            act.wait_ge(bias_ready, 1)

            def copy_xt(g, parity):
                act.wait_ge(filled["xt"], g + 1)
                if not (isinstance(g, int) and g < 2):
                    act.wait_ge(filled["v"], g - 1)
                act.copy(xn_t[:, parity, :], ring_bank("xt")).then_inc(taken["xt"], 1)

            def copy_qk(g, n):
                name = "qk"[n]
                act.wait_ge(filled[name], g + 1)
                if not (isinstance(g, int) and g == 0):
                    act.wait_ge(split, 4 * g)
                act.activation(qk[:, n, :], ring_bank(name), ACT.Identity, bias=bias_qk[:, n:n + 1],
                               scale=SCALE if n == 0 else 1.0).then_inc(taken[name], 1)

            def exps(g, parity, h, n):
                act.wait_ge(b_filled, B_N * g + 2 * h + n + 1)
                if h % 4 == 0 and n == 0:
                    wait_past(act, pv_done, g, QUADS, h // 4 - 1)
                act.activation(probs[:, h % 8, 2 * n:2 * n + 2, :].rearrange("p a t -> p (a t)"),
                               b_ps[n][:, :], ACT.Exp).then_inc(exp_done, 1)

            def take_o(g, quad):
                act.wait_ge(pv_done, QUADS * g + quad + 1)
                wait_past(act, filled["ot"], g, QUADS, quad - 1)
                act.copy(o_t[:, quad % 2, :], o_ps[:, :]).then_inc(o_taken, 1)

            for g in range(2):
                copy_xt(g, g)
                copy_qk(g, 0)
                copy_qk(g, 1)

            def run(name, n, g, parity):
                if name == "B":
                    exps(g, parity, n // 2, n % 2)
                if name == "txt":
                    copy_xt(g, parity)
                if name in ("tq", "tk"):
                    copy_qk(g, ("tq", "tk").index(name))
                if name == "to":
                    take_o(g, n)
                if name == "tat":
                    act.wait_ge(filled["at"], g + 1)
                    wait_past(act, filled["y"], g, 1, 0)
                    act.copy(attn_t[:, :], ring_bank("at")).then_inc(taken["at"], 1)

            turns(act, G, lambda g, parity, ok: run_steps(STEPS, g, parity, ok, run))

        @block.tensor
        def _(pe):
            last = [None, None, None]

            def claim(name, n=0):
                free = last[users.index((name, n)) % 3]
                if free is not None:
                    pe.wait_ge(*free)
                return ring_bank(name, n)

            def left_by(name, g, n=0):
                last[users.index((name, n)) % 3] = (taken[name], g * per_seq[name] + n + 1)

            def use(name, ins, g, n=0):
                ins.then_inc(filled[name], 1)
                left_by(name, g, n)

            def turn_x(g, parity):
                pe.wait_ge(xn_ready, g + 1)
                small = claim("xt")
                for j in range(TILES):
                    mm = pe.transpose(small[:, j * P:(j + 1) * P], xn[:, j, :], c.ident[:, :])
                use("xt", mm, g)

            def project_qk(g, parity, n):
                pe.wait_ge(taken["xt"], g + 1)
                small = claim("qk"[n])
                use("qk"[n], pe.matmul(small[:, :], (w_q, w_k)[n][:, :], xn_t[:, parity, :], start=True, stop=True), g)

            def project_v(g, parity):
                pe.wait_ge(taken["xt"], g + 1)
                small = claim("v")
                for j in range(TILES):
                    mm = pe.matmul(small[:, j * P:(j + 1) * P], xn_t[:, parity, j * P:(j + 1) * P], w_v[:, :],
                                   start=True, stop=True)
                use("v", mm, g)

            def turn_max(g, parity, half):
                pe.wait_ge(a_taken, A_N * g + A_N // 2 * (half + 1))
                small = claim("mx", half)
                use("mx", pe.transpose(small[0:32, 0:P], maxima[:, parity, 32 * half:32 * half + 32], c.ident[:, :]),
                    g, half)

            def pass_a(g, parity, h, j):
                if h % HALF == 0 and j == 0:
                    pe.wait_ge(rows_loaded[parity][h // HALF], 48 * (g - parity) + 96)
                scores = claim("A", h * TILES + j)
                use("A", pe.matmul(scores, q_rows[0:MAX_ROW, parity, h, j * P:(j + 1) * P],
                                   k_rows[0:MAX_ROW, parity, h, :], start=True, stop=True), g, h * TILES + j)

            def pass_b(g, parity, h, n):
                if h % HALF == 0 and n == 0:
                    pe.wait_ge(max_loaded, 32 * g + 16 * (h // HALF) + 16)
                wait_past(pe, exp_done, g, B_N, 2 * h + n - 1)
                for a in range(2):
                    kb = 2 * n + a
                    mm = pe.matmul(b_ps[n][:, a * 512:(a + 1) * 512], k_rows[:, parity, h, kb * P:(kb + 1) * P],
                                   q_rows[:, parity, h, :], start=True, stop=True)
                mm.then_inc(b_filled, 1)

            def values(g, parity, quad, kb):
                if kb == 0:
                    if quad == 0:
                        pe.wait_ge(taken["v"], g + 1)
                    pe.wait_ge(exp_done, B_N * g + 8 * quad + 8)
                    wait_past(pe, o_taken, g, QUADS, quad)
                for n in range(4):
                    h = 4 * quad + n
                    mm = pe.matmul(o_ps[32 * n:32 * n + VW, :], v_one[:, parity, kb, h, :],
                                   probs[:, h % 8, kb, :], start=(kb == 0), stop=(kb == TILES - 1))
                if kb == TILES - 1:
                    mm.then_inc(pv_done, 1)

            def turn_o(g, quad):
                pe.wait_ge(o_taken, QUADS * g + quad + 1)
                small = claim("ot", quad)
                for j in range(TILES):
                    mm = pe.transpose(small[:, j * P:(j + 1) * P], o_t[:, quad % 2, j * P:(j + 1) * P], c.ident[:, :])
                use("ot", mm, g, quad)

            def turn_attn(g):
                pe.wait_ge(taken["ot"], QUADS * g + QUADS)
                small = claim("at")
                for j in range(TILES):
                    mm = pe.transpose(small[:, j * P:(j + 1) * P], attn[:, j, :, :].rearrange("p h d -> p (h d)"),
                                      c.ident[:, :])
                use("at", mm, g)

            def project_out(g):
                pe.wait_ge(taken["at"], g + 1)
                small = claim("y")
                for j in range(TILES):
                    mm = pe.matmul(small[:, j * P:(j + 1) * P], attn_t[:, j * P:(j + 1) * P], w_o[:, :],
                                   start=True, stop=True)
                use("y", mm, g)

            pe.wait_ge(w_ready, 3)
            pe.wait_ge(edges_set, 2)
            pe.wait_ge(o_cleared, 1)
            turn_x(0, 0)
            project_qk(0, 0, 0)
            project_qk(0, 0, 1)
            project_v(0, 0)
            for h in range(H):
                for j in range(TILES):
                    pass_a(0, 0, h, j)
                if h == 1:
                    turn_x(1, 1)
                if h in (2, 3):
                    project_qk(1, 1, h - 2)
                if h == HALF:
                    turn_max(0, 0, 0)

            def run(name, n, g, parity):
                if name == "A":
                    pass_a(g, parity, n // TILES, n % TILES)
                if name == "B":
                    pass_b(g, parity, n // 2, n % 2)
                if name == "V":
                    values(g, parity, n // TILES, n % TILES)
                if name == "mx":
                    turn_max(g, parity, n)
                if name == "xt":
                    turn_x(g, parity)
                if name in ("q", "k"):
                    project_qk(g, parity, "qk".index(name))
                if name == "v":
                    project_v(g, parity)
                if name == "ot":
                    turn_o(g, n)
                if name == "at":
                    turn_attn(g)
                if name == "y":
                    project_out(g)

            def body(g, parity, ok):
                if not isinstance(g, int) or g == G - 2:
                    for name, n, shift in STEPS:
                        if (name, n) in users:
                            left_by(name, g - 1 + shift, n)
                run_steps(STEPS, g, parity, ok, run)

            turns(pe, G, body)

        @block.vector
        def _(dve):
            chain = Chain(dve, chain_sem, G, 8)
            link = chain.link

            def norm_in(g):
                for j in range(TILES):
                    ins = dve.bn_stats(pre.stats[:, j, :], tile_of(c, g, j))
                link(ins)
                dve.memset(c.spare[:, :], 0.0)
                for j in range(TILES):
                    ins = dve.bn_aggr(pre.meanvar[:, j, :], pre.stats[:, j, :])
                link(ins)
                dve.tensor_scalar(pre.vareps[:, :], pre.meanvar[:, :, 1], EPS, None, ALU.add).then_inc(pre_var, 1)

            def take_max(g, half):
                dve.wait_ge(filled["mx"], 2 * g + half + 1)
                n = 2 * g + half
                if not (isinstance(n, int) and n == 0):
                    dve.wait_ge(max_split, 4 * n)
                dve.tensor_scalar(neg_max[:, :], ring_bank("mx", half)[0:32, 0:P], -1.0, None, ALU.mult).then_inc(taken["mx"], 1)

            def take_v(g, parity):
                dve.wait_ge(filled["v"], g + 1)
                wait_past(dve, pv_done, g, QUADS, -QUADS)
                bias = bias_v[:, :].rearrange("p (h c d) -> p h c d", h=H, c=3)[:, :, 2, :]
                dve.tensor_tensor(v_one[:, parity, :, :, 0:DH],
                                  ring_bank("v").rearrange("p (j h d) -> p j h d", j=TILES, h=H),
                                  bias.unsqueeze(1).broadcast_to([P, TILES, H, DH]), ALU.add).then_inc(taken["v"], 1)

            def maxima_of(g, parity, h, j):
                at = h * TILES + j
                dve.wait_ge(a_filled, A_N * g + at + 1)
                if at == 0:
                    wait_past(dve, filled["mx"], g, 2, -2)
                dve.tensor_reduce(maxima[:, parity, at:at + 1], ring_bank("A", at), AX.X, ALU.max)\
                   .then_inc(a_taken, 1)

            def take_attn(g, quad):
                dve.wait_ge(filled["ot"], QUADS * g + quad + 1)
                wait_past(dve, taken["ot"], g, QUADS, quad)
                if quad == 0:
                    wait_past(dve, filled["at"], g, 1, 0)
                o = ring_bank("ot", quad).rearrange("p (j n d) -> p j n d", j=TILES, n=4)
                link(dve.reciprocal(rsum[:, :, :], o[:, :, :, DH]))
                dve.tensor_tensor(attn[:, :, 4 * quad:4 * quad + 4, :], o[:, :, :, 0:DH],
                                  rsum[:, :, :].unsqueeze(3).broadcast_to([P, TILES, 4, DH]), ALU.mult)\
                   .then_inc(taken["ot"], 1)

            def add_out_bias(g):
                dve.wait_ge(filled["y"], g + 1)
                wait_past(dve, x_done, g, 1, 0)
                dve.tensor_tensor(y[:, :, :], ring_bank("y").rearrange("p (j d) -> p j d", j=TILES),
                                  bias_o[:, :].unsqueeze(1).broadcast_to([P, TILES, D]), ALU.add).then_inc(taken["y"], 1)
                dve.wait_ge(taken["y"], g + 1)
                for j in range(TILES):
                    ins = dve.bn_stats(post.stats[:, j, :], y[:, j, :])
                link(ins)
                dve.memset(c.spare[:, :], 0.0)
                for j in range(TILES):
                    ins = dve.bn_aggr(post.meanvar[:, j, :], post.stats[:, j, :])
                link(ins)
                dve.tensor_scalar(post.vareps[:, :], post.meanvar[:, :, 1], EPS, None, ALU.add).then_inc(post_var, 1)

            dve.wait_ge(c.loaded_first, 16)
            dve.wait_ge(c.loaded_rest, 16)
            dve.wait_ge(ahead.attention_loaded, ahead.attention_count)
            w_heads = w_raw[:, :].rearrange("p (h c d) -> p c h d", h=H, c=3)
            for n, w in enumerate((w_q, w_k)):
                dve.tensor_copy(w[:, :].rearrange("p (d h) -> p h d", d=DH), w_heads[:, n]).then_inc(w_ready, 1)
            dve.tensor_copy(w_v[:, :].rearrange("p (h d) -> p h d", h=H), w_heads[:, 2]).then_inc(w_ready, 1)
            dve.memset(o_ps[:, :], 0.0).then_inc(o_cleared, 1)
            for g in range(2):
                if g > 0:
                    dve.wait_ge(xn_ready, g)
                norm_in(g)
                dve.memset(q_rows[64:P, g, :, :], 0.0).then_inc(zeros_set, 1)
            take_v(0, 0)
            for h in range(H):
                for j in range(TILES):
                    maxima_of(0, 0, h, j)
                if h == HALF:
                    take_max(0, 0)

            def run(name, n, g, parity):
                if name == "A":
                    maxima_of(g, parity, n // TILES, n % TILES)
                if name == "tmx":
                    take_max(g, n)
                if name == "ni":
                    norm_in(g)
                if name == "tv":
                    take_v(g, parity)
                if name == "tot":
                    take_attn(g, n)
                if name == "ty":
                    add_out_bias(g)

            def body(g, parity, ok):
                chain.turn(g)
                run_steps(STEPS, g, parity, ok, run)

            turns(dve, G, body)


def turns(eng, groups, body):
    def fixed(g):
        body(g, g % 2, lambda d: 0 <= g + d < groups)
    fixed(0)
    fixed(1)
    with eng.Fori(1, groups // 2 - 1) as i:
        for parity in range(2):
            body(2 * i + parity, parity, lambda d: True)
    for g in range(groups - 2, groups + 1):
        fixed(g)


def wait_past(eng, semaphore, g, n, at):
    if isinstance(g, int) and n * g + at <= 0:
        return
    eng.wait_ge(semaphore, g * n + at)


class Chain:

    def __init__(self, eng, semaphore, groups, per_turn):
        self.eng, self.semaphore, self.groups, self.per_turn = eng, semaphore, groups, per_turn
        self.base, self.n, self.loop_base = 0, 0, None

    def turn(self, g):
        if not isinstance(g, int):
            if self.loop_base is None:
                self.loop_base = self.base + self.n
            else:
                assert self.n == self.per_turn, self.n
            self.base, self.n = self.loop_base + self.per_turn * (g - 2), 0
        elif g == self.groups - 2 and self.loop_base is not None:
            self.base, self.n = self.loop_base + self.per_turn * (self.groups - 4), 0

    def link(self, ins):
        ins.then_inc(self.semaphore, 1)
        self.n += 1
        self.eng.wait_ge(self.semaphore, self.base + self.n)


def mixture_of_experts(c, ahead, w2, sw2):
    nc = c.nc
    G = c.groups
    E, HID, _ = w2.shape
    N_E = E + 1
    PARTS = 3
    CHUNKS = -(-N_E * HID // P)
    ROUTED = E * HID // P
    LAST = N_E * HID - (CHUNKS - 1) * P
    assert E * HID % P == 0 and CHUNKS == ROUTED + 2
    size = [P] * (CHUNKS - 1) + [LAST]

    with ExitStack() as ctx:
        semaphores = ctx.enter_context(LayerSemaphores(nc))

        def sb(name, shape, dt):
            return ctx.enter_context(nc.sbuf_tensor("me_" + name, shape, dt))

        def sem(name):
            return semaphores.get("me_" + name)

        def bank(name):
            return ctx.enter_context(nc.psum_tensor("me_" + name, [P, 512], F32))

        up, up_bias, down_bias = ahead.up, ahead.up_bias, ahead.down_bias
        gate_raw, gate_bias = ahead.gate_raw, ahead.gate_bias
        down = sb("w_down", [P, CHUNKS, D], F32)
        gate_t = sb("gate_t", [P, E], F32)
        one_hot0 = sb("one_hot0", [N_E, N_E * HID], BF16)
        one_hot = sb("one_hot", [PARTS * N_E, N_E * HID], BF16)
        ident_bf = sb("ident_bf", [P, P], BF16)
        iota = sb("iota", [P, TILES, E], F32)
        euler = sb("euler", [P, TILES, E], F32)
        pre, post = LnBufs(sb, "pre"), LnBufs(sb, "post")
        xn = sb("xn", [P, TILES, D], F32)
        xn_t = sb("xn_t", [P, 2, SEQ], F32)
        top = sb("top", [P, TILES], F32)
        shifted = sb("shifted", [P, TILES, E], F32)
        expd = sb("expd", [P, TILES, E], F32)
        total = sb("total", [P, TILES], F32)
        inverse = sb("inverse", [P, TILES], F32)
        score = sb("score", [P, TILES, E], F32)
        biased = sb("biased", [P, 2, TILES, E], F32)
        place = sb("place", [P, TILES, E], F32)
        chosen = sb("chosen", [P, 2, TILES, E], F32)
        weight = sb("weight", [P, TILES, N_E], F32)
        w_rest = sb("w_rest", [P, TILES, N_E], F32)
        w_parts = sb("w_parts", [P, TILES, PARTS * N_E], BF16)
        wt_bf = sb("wt_bf", [PARTS * N_E, 2, SEQ], BF16)
        wt_f = sb("wt_f", [PARTS * N_E, 2, SEQ], F32)
        first = sb("first", [P, 2, SEQ], F32)
        both = sb("both", [P, 2, SEQ], F32)
        act_out = sb("act_out", [P, 2, SEQ], F32)
        hidden = sb("hidden", [P, CHUNKS, SEQ], F32)
        y = sb("y", [P, TILES, D], F32)

        up_ps = [[bank(f"up{n}_ps{i}") for i in range(2)] for n in range(2)]
        wb_ps = [bank(f"wb_ps{i}") for i in range(2)]
        y_ps = bank("y_ps")
        small = bank("small")
        small_bf = small[:, :].bitcast(BF16)

        down_loaded, hot_zero, hot_ready, hot_spread = sem("down_loaded"), sem("hot_steps"), sem("hot_ready"), sem("hot_spread")
        ones_set, gate_turned, gate_ready = sem("ones_set"), sem("gate_turned"), sem("gate_ready")
        pre_var, pre_rstd = sem("pre_var"), sem("pre_rstd")
        post_var, post_rstd = sem("post_var"), sem("post_rstd")
        xn_ready, xn_turned, xn_t_ready = sem("xn_ready"), sem("xn_turned"), sem("xn_t_ready")
        logits_done, logits_read = sem("logits_done"), sem("logits_read")
        shifted_ready, exp_ready = sem("shifted_ready"), sem("exp_ready")
        parts_ready, wt_turned, wt_ready = sem("parts_ready"), sem("wt_turned"), sem("wt_ready")
        up_done = [sem(f"up{n}_done") for n in range(2)]
        wb_done = sem("wb_done")
        first_ready, both_ready, act_ready, hidden_ready = (sem(n) for n in ("first_ready", "both_ready", "act_ready",
                                                                             "hidden_ready"))
        down_done, y_ready, x_done = sem("down_done"), sem("y_ready"), sem("x_done")
        dve_chain = sem("dve_chain")

        block = ctx.enter_context(nc.Block())

        @block.sync
        def _(sp):
            sp.dma_start(down[:, 0:ROUTED, :], w2.rearrange("e h d -> (e h) d").rearrange("(c p) d -> p c d", p=P))\
              .then_inc(down_loaded, 16)
            sp.dma_start(down[:, ROUTED, :], sw2[0:P, :]).then_inc(down_loaded, 16)
            sp.dma_start(down[0:LAST, ROUTED + 1, :], sw2[P:HID, :]).then_inc(down_loaded, 16)
            sp.wait_ge(hot_ready, 1)
            for n in range(PARTS):
                sp.dma_start(one_hot[n * N_E:(n + 1) * N_E, :], one_hot0[:, :]).then_inc(hot_spread, 16)

        @block.gpsimd
        def _(pool):
            steps = [0]

            def step(ins):
                ins.then_inc(hot_zero, 1)
                steps[0] += 1
                pool.wait_ge(hot_zero, steps[0])

            step(pool.memset(one_hot0[:, :], 1.0))
            step(pool.affine_select(out=one_hot0[:, :], in_=one_hot0[:, :], compare_op=ALU.is_ge, fill=0.0, base=0,
                                    pattern=[[1, N_E * HID]], channel_multiplier=-HID))
            pool.affine_select(out=one_hot0[:, :], in_=one_hot0[:, :], compare_op=ALU.is_ge, fill=0.0,
                               base=HID - 1, pattern=[[-1, N_E * HID]], channel_multiplier=HID).then_inc(hot_ready, 1)
            pool.wait_ge(hot_ready, 1)
            step(pool.memset(euler[:, :, :], 2.718281828459045))
            step(pool.memset(weight[:, :, E:N_E], 1.0))
            pool.iota(iota[:, :, :], pattern=[[0, TILES], [1, E]], base=0, channel_multiplier=0,
                      allow_small_or_imprecise_dtypes=True).then_inc(ones_set, 1)
            pool.wait_ge(ones_set, 1)

            def rstd(bufs, var, done, g):
                pool.wait_ge(var, g + 1)
                pool.tensor_tensor(bufs.rstd[:, :], bufs.vareps[:, :], c.neg_half[:, :], ALU.pow).then_inc(done, 1)

            def exps(g):
                pool.wait_ge(shifted_ready, g + 1)
                pool.tensor_tensor(expd[:, :, :], euler[:, :, :], shifted[:, :, :], ALU.pow).then_inc(exp_ready, 1)

            rstd(pre, pre_var, pre_rstd, 0)
            exps(0)

            def body(g, parity, ok):
                if ok(1):
                    rstd(pre, pre_var, pre_rstd, g + 1)
                if ok(-1):
                    rstd(post, post_var, post_rstd, g - 1)
                if ok(1):
                    exps(g + 1)

            turns(pool, G, body)

        @block.scalar
        def _(act):
            act.wait_ge(gate_turned, 1)
            act.copy(gate_t[:, :], small[:, 0:E]).then_inc(gate_ready, 1)
            act.wait_ge(ahead.experts_loaded, ahead.experts_count)

            def copy_xt(g, parity):
                act.wait_ge(xn_turned, g + 1)
                wait_past(act, up_done[1], g, CHUNKS, -CHUNKS)
                act.copy(xn_t[:, parity, :], small[:, :]).then_inc(xn_t_ready, 1)

            def copy_wt(g, parity):
                act.wait_ge(wt_turned, g + 1)
                wait_past(act, wb_done, g, CHUNKS, -CHUNKS)
                act.copy(wt_bf[:, parity, :], small_bf[0:PARTS * N_E, 0:SEQ]).then_inc(wt_ready, 1)
                act.copy(wt_f[:, parity, :], small_bf[0:PARTS * N_E, 0:SEQ]).then_inc(wt_ready, 1)

            def add_bias(g, parity, n):
                b = (parity + n) % 2
                act.wait_ge(up_done[0], CHUNKS * g + n + 1)
                wait_past(act, both_ready, g, CHUNKS, n - 1)
                act.activation(first[0:size[n], b, :], up_ps[0][b][0:size[n], :], ACT.Identity,
                               bias=up_bias[0][0:size[n], n:n + 1]).then_inc(first_ready, 1)

            def silu(g, parity, n):
                b = (parity + n) % 2
                act.wait_ge(both_ready, CHUNKS * g + n + 1)
                wait_past(act, hidden_ready, g, CHUNKS, n - 1)
                act.activation(act_out[0:size[n], b, :], both[0:size[n], b, :], ACT.Silu).then_inc(act_ready, 1)

            copy_xt(0, 0)
            copy_wt(0, 0)

            def body(g, parity, ok):
                for n in range(CHUNKS):
                    if ok(0):
                        add_bias(g, parity, n)
                    if n == 0 and ok(-1):
                        silu(g - 1, 1 - parity, CHUNKS - 1)
                    if n > 0 and ok(0):
                        silu(g, parity, n - 1)
                    if n == 2 and ok(-1):
                        act.wait_ge(down_done, CHUNKS * g)
                        wait_past(act, x_done, g, 1, -1)
                        act.copy(y[:, :, :].rearrange("p j d -> p (j d)"), y_ps[:, :]).then_inc(y_ready, 1)
                    if n == 3 and ok(1):
                        copy_xt(g + 1, 1 - parity)
                    if n == 12 and ok(1):
                        copy_wt(g + 1, 1 - parity)

            turns(act, G, body)

        @block.tensor
        def _(pe):
            pe.wait_ge(c.consts, 3)
            pe.wait_ge(ahead.experts_loaded, ahead.experts_count)
            pe.transpose(small[:, 0:E], gate_raw[:, :], c.ident[0:E, 0:E]).then_inc(gate_turned, 1)
            pe.wait_ge(gate_ready, 1)

            def turn_x(g):
                pe.wait_ge(xn_ready, g + 1)
                wait_past(pe, wt_ready, g, 2, 0)
                for j in range(TILES):
                    mm = pe.transpose(small[:, j * P:(j + 1) * P], xn[:, j, :], c.ident[:, :])
                mm.then_inc(xn_turned, 1)

            def logits(g, parity):
                pe.wait_ge(xn_t_ready, g + 1)
                for j in range(TILES):
                    mm = pe.matmul(small[:, j * E:(j + 1) * E], xn_t[:, parity, j * P:(j + 1) * P], gate_t[:, :],
                                   start=True, stop=True)
                mm.then_inc(logits_done, 1)

            def turn_weights(g):
                pe.wait_ge(parts_ready, g + 1)
                for j in range(TILES):
                    mm = pe.transpose(small_bf[0:PARTS * N_E, j * P:(j + 1) * P], w_parts[:, j, :], ident_bf[:, :])
                mm.then_inc(wt_turned, 1)

            def up_products(g, parity, n):
                b = (parity + n) % 2
                cols = slice(n * P, n * P + size[n])
                for k, used in ((0, first_ready), (1, both_ready)):
                    wait_past(pe, used, g, CHUNKS, n - 1)
                    pe.matmul(up_ps[k][b][0:size[n], :], up[k][:, cols], xn_t[:, parity, :], start=True, stop=True)\
                      .then_inc(up_done[k], 1)
                if n == 0 and isinstance(g, int) and g == 0:
                    pe.wait_ge(hot_spread, 48)
                wait_past(pe, hidden_ready, g, CHUNKS, n - 1)
                pe.matmul(wb_ps[b][0:size[n], :], one_hot[:, cols], wt_bf[:, parity, :], start=True, stop=True)\
                  .then_inc(wb_done, 1)

            def down_product(g, parity, n):
                pe.wait_ge(hidden_ready, CHUNKS * g + n + 1)
                if n == 0:
                    if isinstance(g, int) and g == 0:
                        pe.wait_ge(down_loaded, 48)
                    wait_past(pe, y_ready, g, 1, 0)
                    for j in range(TILES):
                        pe.matmul(y_ps[:, j * D:(j + 1) * D], wt_f[:, parity, j * P:(j + 1) * P], down_bias[:, :],
                                  start=(j == 0), stop=False, skip_group_check=True)
                for j in range(TILES):
                    mm = pe.matmul(y_ps[:, j * D:(j + 1) * D], hidden[0:size[n], n, j * P:(j + 1) * P],
                                   down[0:size[n], n, :], start=False, stop=(n == CHUNKS - 1), skip_group_check=True)
                mm.then_inc(down_done, 1)

            turn_x(0)
            logits(0, 0)
            turn_weights(0)
            pe.wait_ge(wt_ready, 2)

            def body(g, parity, ok):
                if ok(0):
                    wait_past(pe, wt_ready, g, 2, 2)
                for n in range(CHUNKS):
                    if ok(0):
                        up_products(g, parity, n)
                    if n < 2 and ok(-1):
                        down_product(g - 1, 1 - parity, CHUNKS - 2 + n)
                    if n >= 2 and ok(0):
                        down_product(g, parity, n - 2)
                    if n == 2 and ok(1):
                        turn_x(g + 1)
                    if n == 4 and ok(1):
                        logits(g + 1, 1 - parity)
                    if n == 12 and ok(1):
                        turn_weights(g + 1)

            turns(pe, G, body)

        @block.vector
        def _(dve):
            chain = Chain(dve, dve_chain, G, 26)
            link = chain.link

            def norm_in(g):
                ln_stats(dve, c, lambda j: tile_of(c, g, j), pre, link).then_inc(pre_var, 1)

            def scale_in(g):
                dve.wait_ge(pre_rstd, g + 1)
                wait_past(dve, xn_turned, g, 1, 0)
                for j in range(TILES):
                    ins = dve.tensor_scalar(xn[:, j, :], tile_of(c, g, j), pre.meanvar[:, j, 0:1],
                                            pre.rstd[:, j:j + 1], ALU.subtract, ALU.mult)
                ins.then_inc(xn_ready, 1)

            def over(t):
                return t.unsqueeze(2).broadcast_to([P, TILES, E])

            def route_shift(g):
                dve.wait_ge(logits_done, g + 1)
                logit = small[:, 0:TILES * E].rearrange("p (j e) -> p j e", j=TILES)
                link(dve.tensor_reduce(top[:, :], logit, AX.X, ALU.max))
                dve.tensor_tensor(shifted[:, :, :], logit, over(top[:, :]), ALU.subtract).then_inc(shifted_ready, 1)

            def route_scores(g):
                dve.wait_ge(exp_ready, g + 1)
                link(dve.tensor_reduce(total[:, :], expd[:, :, :], AX.X, ALU.add))
                link(dve.reciprocal(inverse[:, :], total[:, :]))
                link(dve.tensor_tensor(score[:, :, :], expd[:, :, :], over(inverse[:, :]), ALU.mult))
                link(dve.tensor_tensor(biased[:, 0], score[:, :, :],
                                       gate_bias[:, :].unsqueeze(1).broadcast_to([P, TILES, E]), ALU.add))

            def route_pick(n):
                link(dve.tensor_reduce(top[:, :], biased[:, n], AX.X, ALU.max))
                link(dve.tensor_tensor(place[:, :, :], biased[:, n], over(top[:, :]), ALU.is_lt))
                flat = place[:, :, :].rearrange("p j e -> p (j e)")
                link(dve.scalar_tensor_tensor(out=flat, in0=flat, scalar=float(E),
                                              in1=iota[:, :, :].rearrange("p j e -> p (j e)"),
                                              op0=ALU.mult, op1=ALU.add))
                link(dve.tensor_reduce(top[:, :], place[:, :, :], AX.X, ALU.min))
                link(dve.tensor_tensor(chosen[:, n], iota[:, :, :], over(top[:, :]), ALU.is_equal))
                if n == 0:
                    link(dve.scalar_tensor_tensor(out=biased[:, 1].rearrange("p j e -> p (j e)"),
                                                  in0=chosen[:, 0].rearrange("p j e -> p (j e)"), scalar=-1e30,
                                                  in1=biased[:, 0].rearrange("p j e -> p (j e)"),
                                                  op0=ALU.mult, op1=ALU.add))

            def route_weights():
                link(dve.tensor_tensor(place[:, :, :], chosen[:, 0], chosen[:, 1], ALU.add))
                link(dve.tensor_tensor(weight[:, :, 0:E], score[:, :, :], place[:, :, :], ALU.mult))

            def split_weights(g):
                wait_past(dve, wt_turned, g, 1, 0)
                parts = [w_parts[:, :, n * N_E:(n + 1) * N_E] for n in range(PARTS)]
                link(dve.tensor_scalar(parts[0], weight[:, :, :], 0.0, None, ALU.add))
                link(dve.tensor_tensor(w_rest[:, :, :], weight[:, :, :], parts[0], ALU.subtract))
                link(dve.tensor_scalar(parts[1], w_rest[:, :, :], 0.0, None, ALU.add))
                dve.tensor_tensor(parts[2], w_rest[:, :, :], parts[1], ALU.subtract).then_inc(parts_ready, 1)

            def multiply(g, parity, n):
                b = (parity + n) % 2
                dve.wait_ge(up_done[1], CHUNKS * g + n + 1)
                dve.wait_ge(first_ready, CHUNKS * g + n + 1)
                wait_past(dve, act_ready, g, CHUNKS, n - 1)
                dve.scalar_tensor_tensor(out=both[0:size[n], b, :], in0=up_ps[1][b][0:size[n], :],
                                         scalar=up_bias[1][0:size[n], n:n + 1], in1=first[0:size[n], b, :],
                                         op0=ALU.add, op1=ALU.mult).then_inc(both_ready, 1)

            def weigh(g, parity, n):
                b = (parity + n) % 2
                dve.wait_ge(act_ready, CHUNKS * g + n + 1)
                dve.wait_ge(wb_done, CHUNKS * g + n + 1)
                wait_past(dve, down_done, g, CHUNKS, n + 1 - CHUNKS)
                dve.tensor_tensor(hidden[0:size[n], n, :], act_out[0:size[n], b, :], wb_ps[b][0:size[n], :],
                                  ALU.mult).then_inc(hidden_ready, 1)

            def norm_out(g):
                dve.wait_ge(y_ready, g + 1)
                ln_stats(dve, c, lambda j: y[:, j, :], post, link).then_inc(post_var, 1)

            def add_out(g):
                dve.wait_ge(post_rstd, g + 1)
                for j in range(TILES):
                    ins = dve.tensor_scalar(y[:, j, :], y[:, j, :], post.meanvar[:, j, 0:1],
                                            post.rstd[:, j:j + 1], ALU.subtract, ALU.mult)
                link(ins)
                dve.tensor_tensor(group_of(c, g), group_of(c, g), y[:, :, :], ALU.add).then_inc(x_done, 1)

            dve.wait_ge(c.loaded_first, 16)
            dve.wait_ge(c.loaded_rest, 16)
            dve.wait_ge(ahead.experts_loaded, ahead.experts_count)
            dve.wait_ge(ones_set, 1)
            dve.wait_ge(c.consts, 3)
            link(dve.tensor_copy(ident_bf[:, :], c.ident[:, :]))
            norm_in(0)
            scale_in(0)
            route_shift(0)
            route_scores(0)
            route_pick(0)
            route_pick(1)
            route_weights()
            split_weights(0)

            def body(g, parity, ok):
                chain.turn(g)
                for n in range(CHUNKS):
                    if ok(0):
                        multiply(g, parity, n)
                    if n == 0 and ok(-1):
                        weigh(g - 1, 1 - parity, CHUNKS - 1)
                    if n > 0 and ok(0):
                        weigh(g, parity, n - 1)
                    if n == 0 and ok(1):
                        norm_in(g + 1)
                    if n == 1 and ok(1):
                        scale_in(g + 1)
                    if n == 3 and ok(-1):
                        norm_out(g - 1)
                    if n == 4 and ok(-1):
                        add_out(g - 1)
                    if n == 5 and ok(1):
                        route_shift(g + 1)
                    if n == 7 and ok(1):
                        route_scores(g + 1)
                    if n == 8 and ok(1):
                        route_pick(0)
                    if n == 9 and ok(1):
                        route_pick(1)
                    if n == 10 and ok(1):
                        route_weights()
                        split_weights(g + 1)

            turns(dve, G, body)


def gated_slots(c, ahead, Wq, Wk, Wv, Wf, g_norm_w, Wo):
    nc = c.nc
    G = c.groups
    H = 4
    HK = D // H
    M = Wf.shape[1] // H
    SLOTS = H * M
    PAIRS = SLOTS // P
    CH = 64
    PER_TILE = P // CH
    CHUNKS = SEQ // CH
    QSCALE = -float(HK) ** -0.5 / 4
    NORM = 8.0
    assert M == 64 and HK == 32 and PAIRS == 2 and PER_TILE == 2

    PREPARE = ("xt", "q", "k", "qs", "ks", "kt", "vf", "zf", "ln", "gl", "ga", "G", "wr", "D", "Dt", "U", "S", "H", "st")
    STEPS = parse_steps(
        "A0 mA0 xt L0 dL0 eL0 B3- mB3- q k ks o3- qs to- vf0 zf0 pk0 pt0 vf1 zf1 A1 mA1 ln so- gl B0 mB0 "
        "ont- L1 dL1 eL1 A2 mA2 G0 y- ga pk1 pt1 no- G1 wr0 D o0 kt wr1 ni+ B1 mB1 Dt ao- L2 dL2 eL2 U o1 "
        "pk2 pt2 S A3 mA3 st0 st1 B2 mB2 L3 dL3 eL3 o2 H pk3 pt3 si+", PREPARE)

    with ExitStack() as ctx:
        semaphores = ctx.enter_context(LayerSemaphores(nc))

        def sb(name, shape, dt=F32):
            return ctx.enter_context(nc.sbuf_tensor("gs_" + name, shape, dt))

        def sem(name):
            return semaphores.get("gs_" + name)

        w_q, w_k, w_o = sb("w_q", [P, D]), sb("w_k", [P, D]), sb("w_o", [P, D])
        w_vf = sb("w_vf", [P, D + SLOTS])
        norm_w = sb("norm_w", [P, 1])
        causal = sb("causal", [P, P])
        causal_q = sb("causal_q", [P, P])
        sum_from_mid = sb("sum_from_mid", [P, P])
        early = sb("early", [P, P])
        between = sb("between", [P, TILES, CHUNKS - 1])
        neg_half = sb("neg_half", [P, TILES * H])
        pre, post = LnBufs(sb, "pre"), LnBufs(sb, "post")
        xn = sb("xn", [P, TILES, D])
        xn_t = sb("xn_t", [P, SEQ])
        tanh_q, tanh_k = sb("tanh_q", [P, SEQ]), sb("tanh_k", [P, SEQ])
        q_t = sb("q_t", [P, SEQ])
        q_own = sb("q_own", [P, 2, TILES, H, P])
        k_t = sb("k_t", [P, 2, SEQ])
        kv = sb("kv", [P, 2, TILES, 2, D])
        abs_z = sb("abs_z", [P, 2, SLOTS])
        exp_z = sb("exp_z", [P, TILES, SLOTS])
        log_z = sb("log_z", [P, TILES, SLOTS])
        gate_log = sb("gate_log", [P, TILES, SLOTS])
        gate = sb("gate", [P, TILES, SLOTS])
        keep = sb("keep", [P, 2, TILES, SLOTS])
        unkeep = sb("unkeep", [P, TILES, SLOTS])
        write = sb("write", [P, 2, TILES, SLOTS])
        write_t = sb("write_t", [P, 2, TILES, PAIRS, P])
        decay_rows = sb("decay_rows", [CHUNKS - 1, SLOTS])
        decay = sb("decay", [P, PAIRS, CHUNKS - 1])
        undecayed = sb("undecayed", [P, CHUNKS - 1, PAIRS, 2 * HK])
        state = sb("state", [P, 2, CHUNKS, PAIRS, 2 * HK])
        state_k = sb("state_k", [P, 2, CHUNKS - 1, M])
        a_sb = sb("a_sb", [P, TILES, H, P])
        logit = sb("logit", [P, TILES, SLOTS])
        expd = sb("expd", [P, TILES, SLOTS])
        p_keep = sb("p_keep", [P, TILES, SLOTS])
        p_own = sb("p_own", [P, TILES, PAIRS, 2, P])
        b_sb = sb("b_sb", [P, TILES, H, P])
        top = sb("top", [P, H])
        total = sb("total", [P, TILES * H])
        inverse = sb("inverse", [P, TILES * H])
        o_sb = sb("o_sb", [P, TILES * H, HK])
        o_sq = sb("o_sq", [P, TILES * H, HK])
        o_var = sb("o_var", [P, TILES * H])
        o_rstd = sb("o_rstd", [P, TILES * H])
        on = sb("on", [P, TILES * H, HK])
        on_t = sb("on_t", [P, SEQ])
        y = sb("y", [P, TILES, D])

        prep = ctx.enter_context(nc.psum_tensor("gs_prep", [P, 2, 512], F32))
        banks = {n: ctx.enter_context(nc.psum_tensor("gs_" + n, [P, 512], F32))[:, :]
                 for n in ("prep2", "a", "b", "l", "pt", "o_ps")}
        banks.update(prep0=prep[:, 0, :], prep1=prep[:, 1, :])

        per_seq = {"xt": 1, "q": 1, "k": 1, "kt": 1, "vf": 2, "G": 2, "D": 1, "Dt": 1, "st": 2, "A": TILES,
                   "L": TILES, "pt": TILES, "B": TILES, "U": 1, "H": 1, "o": 1, "ont": 1, "y": 1}
        bank_of = {"xt": ["prep2"], "q": ["prep0"], "k": ["prep1"], "kt": ["prep2"], "D": ["prep2"], "Dt": ["prep2"],
                   "H": ["prep2"], "vf": ["prep0", "prep1"], "U": ["prep0", "prep1"], "A": ["a"], "B": ["b"],
                   "L": ["l"], "y": ["l"], "pt": ["pt"], "ont": ["pt"], "o": ["o_ps"]}
        filled = {n: sem(n + "_filled") for n in per_seq}
        taken = {n: sem(n + "_taken") for n in per_seq}
        loaded, masks, wo_ready = sem("loaded"), sem("mask_steps"), sem("wo_ready")
        consts_ready = sem("consts_ready")
        pre_var, pre_rstd, xn_ready = sem("pre_var"), sem("pre_rstd"), sem("xn_ready")
        post_var, post_rstd, x_done = sem("post_var"), sem("post_rstd"), sem("x_done")
        tanh_done = sem("tanh_done")
        abs_done, exp_z_done, log_done, gates_done = sem("abs_done"), sem("exp_z_done"), sem("log_done"), sem("gates_done")
        gate_log_ready, write_ready = sem("gate_log_ready"), sem("write_ready")
        shifted_ready, exp_done, p_ready = sem("shifted_ready"), sem("exp_done"), sem("p_ready")
        total_ready = sem("total_ready")
        state_ready = sem("state_ready")
        own_zero, q_own_ready = sem("own_zero"), sem("q_own_ready")
        o_var_ready, o_rstd_ready, on_ready = sem("o_var_ready"), sem("o_rstd_ready"), sem("on_ready")
        dve_chain = sem("dve_chain")
        LOADS = 10

        block = ctx.enter_context(nc.Block())

        @block.sync
        def _(sp):
            sp.dma_start(w_q[:, :], Wq).then_inc(loaded, 16)
            sp.dma_start(w_k[:, :], Wk).then_inc(loaded, 16)
            sp.dma_start(w_vf[:, 0:D], Wv).then_inc(loaded, 16)
            sp.dma_start(w_vf[:, D:], Wf).then_inc(loaded, 16)
            sp.dma_start(w_o[:, :], Wo).then_inc(loaded, 16)
            for h in range(H):
                sp.dma_start(norm_w[h * HK:(h + 1) * HK, :], g_norm_w.rearrange("(p a) -> p a", a=1)).then_inc(loaded, 16)
            ahead.load(sp)

        @block.gpsimd
        def _(pool):
            def rstd(bufs, var, done, g):
                pool.wait_ge(var, g + 1)
                pool.tensor_tensor(bufs.rstd[:, :], bufs.vareps[:, :], c.neg_half[:, :], ALU.pow).then_inc(done, 1)

            pool.memset(causal[:, :], 1.0).then_inc(masks, 1)
            pool.wait_ge(masks, 1)
            pool.affine_select(out=causal[:, :], in_=causal[:, :], compare_op=ALU.is_ge, fill=0.0, base=0,
                               pattern=[[1, P]], channel_multiplier=-1).then_inc(masks, 1)
            pool.wait_ge(masks, 2)
            pool.wait_ge(c.consts, 3)
            pool.memset(q_own[:, :, :, :, :], 0.0).then_inc(own_zero, 1)
            pool.memset(p_own[:, :, :, :, :], 0.0).then_inc(own_zero, 1)
            pool.wait_ge(own_zero, 2)
            def spread_q(g, parity):
                pool.wait_ge(taken["q"], g + 1)
                wait_past(pool, filled["L"], g, TILES, -TILES)
                for h in range(H):
                    rows = slice(h * HK, (h + 1) * HK)
                    pool.tensor_tensor(q_own[rows, parity, :, h, :],
                                       q_t[rows, :].rearrange("p (j t) -> p j t", j=TILES),
                                       c.zero[rows, :].unsqueeze(2).broadcast_to([HK, TILES, P]), ALU.add)\
                        .then_inc(q_own_ready, 1)
                    pool.wait_ge(q_own_ready, H * g + h + 1)

            def run(name, n, g, parity):
                if name == "ni":
                    rstd(pre, pre_var, pre_rstd, g)
                if name == "qs":
                    spread_q(g, parity)
                if name == "to":
                    pool.wait_ge(o_var_ready, g + 1)
                    pool.tensor_tensor(o_rstd[:, :], o_var[:, :], neg_half[:, :], ALU.pow).then_inc(o_rstd_ready, 1)
                if name == "no":
                    rstd(post, post_var, post_rstd, g)

            first_steps(STEPS, run)
            turns(pool, G, lambda g, parity, ok: run_steps(STEPS, g, parity, ok, run))

        @block.scalar
        def _(act):
            act.wait_ge(loaded, 16 * (LOADS - 1))

            def take(name, g, n, out, in_, func=ACT.Copy, scale=1.0, inc=True):
                act.wait_ge(filled[name], per_seq[name] * g + n + 1)
                ins = act.activation(out, in_, func, scale=scale)
                if inc:
                    ins.then_inc(taken[name], 1)

            def run(name, n, g, parity):
                if name == "xt":
                    wait_past(act, filled["vf"], g, 2, 0)
                    take("xt", g, 0, xn_t[:, :], banks["prep2"])
                if name == "q":
                    wait_past(act, taken["q"], g, 1, 0)
                    act.wait_ge(filled["q"], g + 1)
                    act.activation(tanh_q[:, :], banks["prep0"], ACT.Tanh, scale=0.5).then_inc(tanh_done, 1)
                if name == "k":
                    wait_past(act, taken["k"], g, 1, 0)
                    act.wait_ge(filled["k"], g + 1)
                    act.activation(tanh_k[:, :], banks["prep1"], ACT.Tanh, scale=0.5).then_inc(tanh_done, 1)
                if name == "kt":
                    wait_past(act, filled["o"], g, 1, -1)
                    take("kt", g, 0, kv[:, parity, :, 0, :],
                         banks["prep2"][:, :].rearrange("p (j d) -> p j d", j=TILES))
                if name == "vf":
                    tiles = slice(2 * n, 2 * n + 2)
                    act.wait_ge(filled["vf"], 2 * g + n + 1)
                    wait_past(act, filled["o"], g, 1, -1)
                    act.activation(kv[:, parity, tiles, 1, :], prep[:, :, 0:D], ACT.Copy, scale=-1.0)
                    wait_past(act, exp_z_done, g, 2, n)
                    act.activation(abs_z[:, :, :], prep[:, :, D:D + SLOTS], ACT.Abs).then_inc(abs_done, 1)
                    act.wait_ge(abs_done, 2 * g + n + 1)
                    wait_past(act, log_done, g, 1, 0)
                    act.activation(exp_z[:, tiles, :], abs_z[:, :, :], ACT.Exp, scale=-1.0).then_inc(exp_z_done, 1)
                if name == "ln":
                    act.wait_ge(exp_z_done, 2 * g + 2)
                    wait_past(act, gate_log_ready, g, 1, 0)
                    act.activation(log_z[:, :, :], exp_z[:, :, :], ACT.Ln, bias=1.0).then_inc(log_done, 1)
                if name == "ga":
                    act.wait_ge(gate_log_ready, g + 1)
                    wait_past(act, write_ready, g, 2, 0)
                    act.activation(gate[:, :, :], gate_log[:, :, :], ACT.Exp, scale=1.0 / NORM).then_inc(gates_done, 1)
                if name == "G":
                    tiles = slice(2 * n, 2 * n + 2)
                    bank = banks[f"prep{n}"][:, :].rearrange("p (j m) -> p j m", j=2)
                    wait_past(act, p_ready, g, TILES, -TILES)
                    wait_past(act, write_ready, g, 2, n - 1)
                    take("G", g, n, unkeep[:, tiles, :], bank, ACT.Exp, scale=-1.0, inc=False)
                    take("G", g, n, keep[:, parity, tiles, :], bank, ACT.Exp)
                if name == "D":
                    wait_past(act, filled["Dt"], g, 1, 0)
                    take("D", g, 0, decay_rows[:, :], banks["prep2"][0:CHUNKS - 1, 0:SLOTS], ACT.Exp)
                if name == "H":
                    wait_past(act, filled["L"], g, TILES, -TILES)
                    take("H", g, 0, state_k[:, parity, :, :],
                         banks["prep2"][:, 0:(CHUNKS - 1) * M].rearrange("p (i m) -> p i m", m=M), scale=QSCALE)
                if name == "st":
                    wait_past(act, filled["B"], g, TILES, -TILES)
                    take("st", g, n, write_t[:, parity, 2 * n:2 * n + 2, :, :],
                         banks[f"prep{n}"][:, :].rearrange("p (j a t) -> p j a t", j=2, a=PAIRS))
                if name == "eL":
                    act.wait_ge(shifted_ready, TILES * g + n + 1)
                    wait_past(act, total_ready, g, TILES, n - TILES + 1)
                    act.activation(expd[:, n, :], logit[:, n, :], ACT.Exp).then_inc(exp_done, 1)
                if name == "pt":
                    wait_past(act, filled["o"], g, 1, 0)
                    for i in range(2):
                        rows = slice(i * M, (i + 1) * M)
                        take("pt", g, n, p_own[rows, n, :, i, :],
                             banks["pt"][rows, 0:SLOTS].rearrange("p (a t) -> p a t", a=PAIRS), inc=(i == 1))
                if name == "ont":
                    wait_past(act, filled["y"], g, 1, 0)
                    take("ont", g, 0, on_t[:, :], banks["pt"][:, :])
                if name == "y":
                    wait_past(act, x_done, g, 1, 0)
                    take("y", g, 0, y[:, :, :].rearrange("p j d -> p (j d)"), banks["l"][:, :])

            first_steps(STEPS, run)
            turns(act, G, lambda g, parity, ok: run_steps(STEPS, g, parity, ok, run))

        @block.tensor
        def _(pe):
            last = {n: None for n in banks}

            def banks_of(name, n):
                return [f"prep{n}"] if name in ("G", "st") else bank_of[name]

            def claim(name, n=0):
                for bank in banks_of(name, n):
                    if last[bank] is not None:
                        pe.wait_ge(*last[bank])
                return banks[banks_of(name, n)[0]]

            def left_by(name, n, g):
                for bank in banks_of(name, n):
                    last[bank] = (taken[name], per_seq[name] * g + (n if per_seq[name] > 1 else 0) + 1)

            def done(ins, name, g, n=0):
                ins.then_inc(filled[name], 1)
                left_by(name, n, g)

            def run(name, n, g, parity):
                tok = slice(n * P, (n + 1) * P)
                if name == "xt":
                    pe.wait_ge(xn_ready, g + 1)
                    ps = claim("xt")
                    for j in range(TILES):
                        mm = pe.transpose(ps[:, j * P:(j + 1) * P], xn[:, j, :], c.ident[:, :])
                    done(mm, "xt", g)
                if name in ("q", "k"):
                    pe.wait_ge(taken["xt"], g + 1)
                    ps = claim(name)
                    done(pe.matmul(ps[:, :], {"q": w_q, "k": w_k}[name][:, :], xn_t[:, :], start=True, stop=True), name, g)
                if name == "kt":
                    pe.wait_ge(taken["k"], g + 1)
                    ps = claim("kt")
                    for j in range(TILES):
                        mm = pe.transpose(ps[:, j * P:(j + 1) * P], k_t[:, parity, j * P:(j + 1) * P], c.ident[:, :])
                    done(mm, "kt", g)
                if name == "vf":
                    claim("vf")
                    for a in range(2):
                        j = 2 * n + a
                        mm = pe.matmul(prep[:, a, 0:D + SLOTS], xn_t[:, j * P:(j + 1) * P], w_vf[:, :],
                                       start=True, stop=True)
                    done(mm, "vf", g, n)
                if name == "G":
                    pe.wait_ge(gate_log_ready, g + 1)
                    ps = claim("G", n)
                    for a in range(2):
                        mm = pe.matmul(ps[:, a * SLOTS:(a + 1) * SLOTS], sum_from_mid[:, :], gate_log[:, 2 * n + a, :],
                                       start=True, stop=True)
                    done(mm, "G", g, n)
                if name == "D":
                    pe.wait_ge(gate_log_ready, g + 1)
                    ps = claim("D")
                    for j in range(TILES):
                        mm = pe.matmul(ps[0:CHUNKS - 1, 0:SLOTS], between[:, j, :], gate_log[:, j, :],
                                       start=(j == 0), stop=(j == TILES - 1))
                    done(mm, "D", g)
                if name == "Dt":
                    pe.wait_ge(taken["D"], g + 1)
                    ps = claim("Dt")
                    for a in range(PAIRS):
                        mm = pe.matmul(ps[:, a * 8:a * 8 + CHUNKS - 1], decay_rows[:, a * P:(a + 1) * P],
                                       c.ident[0:CHUNKS - 1, 0:CHUNKS - 1], start=True, stop=True)
                    done(mm, "Dt", g)
                if name == "U":
                    pe.wait_ge(taken["kt"], g + 1)
                    pe.wait_ge(write_ready, 2 * g + 2)
                    claim("U")
                    for ch in range(CHUNKS - 1):
                        j, rows = ch // 2, slice(CH * (ch % 2), CH * (ch % 2) + CH)
                        for h in range(H):
                            a, i = h // 2, h % 2
                            col = j * P + a * 2 * HK
                            end = h * M + (M if ch > 0 or h > 0 else 2 * M)
                            mm = pe.matmul(prep[i * M:i * M + end - h * M, ch % 2, col:col + 2 * HK],
                                           write[rows, parity, j, h * M:end],
                                           kv[rows, parity, j, :, h * HK:(h + 1) * HK], start=True, stop=True)
                    done(mm, "U", g)
                if name == "H":
                    pe.wait_ge(state_ready, g + 1)
                    ps = claim("H")
                    for ch in range(1, CHUNKS):
                        for h in range(H):
                            a, i = h // 2, h % 2
                            mm = pe.matmul(ps[h * HK:(h + 1) * HK, (ch - 1) * M:ch * M], state[:, parity, ch, a, 0:HK],
                                           c.ident[:, i * M:(i + 1) * M], start=True, stop=True)
                    done(mm, "H", g)
                if name == "st":
                    pe.wait_ge(write_ready, 2 * g + n + 1)
                    ps = claim("st", n)
                    for a in range(2):
                        for b in range(PAIRS):
                            at = (a * PAIRS + b) * P
                            mm = pe.transpose(ps[:, at:at + P], write[:, parity, 2 * n + a, b * P:(b + 1) * P],
                                              c.ident[:, :])
                    done(mm, "st", g, n)
                if name == "A":
                    pe.wait_ge(q_own_ready, H * (g + 1))
                    ps = claim("A")
                    mm = pe.matmul(ps[:, :], k_t[:, parity, tok], q_own[:, parity, n, :, :], start=True, stop=True)
                    done(mm, "A", g, n)
                if name == "L":
                    pe.wait_ge(taken["A"], TILES * g + n + 1)
                    ps = claim("L")
                    for h in range(H):
                        mm = pe.matmul(ps[:, h * M:(h + 1) * M], a_sb[:, n, h, :], write[:, parity, n, h * M:(h + 1) * M],
                                       start=(h == 0), stop=False, skip_group_check=True)
                    if n == 0:
                        pe.wait_ge(taken["H"], g + 1)
                    for i in range(PER_TILE):
                        ch = PER_TILE * n + i
                        if ch == 0:
                            continue
                        for h in range(H):
                            mm = pe.matmul(ps[CH * i:CH * i + CH, h * M:(h + 1) * M],
                                           q_own[:, parity, n, h, CH * i:CH * i + CH], state_k[:, parity, ch - 1, :],
                                           start=False, stop=(h == H - 1), skip_group_check=True)
                    done(mm, "L", g, n)
                if name == "pt":
                    pe.wait_ge(p_ready, TILES * g + n + 1)
                    ps = claim("pt")
                    for a in range(PAIRS):
                        mm = pe.transpose(ps[:, a * P:(a + 1) * P], p_keep[:, n, a * P:(a + 1) * P], c.ident[:, :])
                    done(mm, "pt", g, n)
                if name == "B":
                    pe.wait_ge(taken["pt"], TILES * g + n + 1)
                    pe.wait_ge(taken["st"], 2 * g + n // 2 + 1)
                    ps = claim("B")
                    for a in range(PAIRS):
                        mm = pe.matmul(ps[:, 2 * a * P:2 * (a + 1) * P], write_t[:, parity, n, a, :],
                                       p_own[:, n, a, :, :], start=True, stop=True)
                    done(mm, "B", g, n)
                if name == "o":
                    pe.wait_ge(taken["B"], TILES * g + n + 1)
                    ps = claim("o") if n == 0 else banks["o_ps"]
                    for h in range(H):
                        mm = pe.matmul(ps[:, n * D + h * HK:n * D + (h + 1) * HK], b_sb[:, n, h, :],
                                       kv[:, parity, n, 1, h * HK:(h + 1) * HK],
                                       start=(h == 0), stop=False, skip_group_check=True)
                    for i in range(PER_TILE):
                        ch = PER_TILE * n + i
                        if ch == 0:
                            continue
                        for h in range(H):
                            a, own = h // 2, h % 2
                            col = n * D + h * HK
                            mm = pe.matmul(ps[CH * i:CH * i + CH, col:col + HK],
                                           p_own[:, n, a, own, CH * i:CH * i + CH],
                                           state[:, parity, ch, a, HK:2 * HK],
                                           start=False, stop=(h == H - 1), skip_group_check=True)
                    if n == TILES - 1:
                        done(mm, "o", g)
                if name == "ont":
                    pe.wait_ge(on_ready, g + 1)
                    ps = claim("ont")
                    for j in range(TILES):
                        mm = pe.transpose(ps[:, j * P:(j + 1) * P],
                                          on[:, :, :].rearrange("p (j h) d -> p j (h d)", j=TILES)[:, j, :], c.ident[:, :])
                    done(mm, "ont", g)
                if name == "y":
                    pe.wait_ge(taken["ont"], g + 1)
                    ps = claim("y")
                    for j in range(TILES):
                        mm = pe.matmul(ps[:, j * D:(j + 1) * D], on_t[:, j * P:(j + 1) * P], w_o[:, :],
                                       start=True, stop=True)
                    done(mm, "y", g)

            pe.wait_ge(c.consts, 3)
            pe.wait_ge(loaded, 16 * (LOADS - 1))
            pe.wait_ge(consts_ready, 1)
            pe.wait_ge(wo_ready, 1)
            first_steps(STEPS, run)

            def body(g, parity, ok):
                if not isinstance(g, int) or g == G - 2:
                    for name, n, shift in STEPS:
                        if name in per_seq:
                            left_by(name, n, g - 1 + shift)
                run_steps(STEPS, g, parity, ok, run)

            turns(pe, G, body)

        @block.vector
        def _(dve):
            chain = Chain(dve, dve_chain, G, 18)
            link = chain.link

            def norm_in(g):
                ln_stats(dve, c, lambda j: tile_of(c, g, j), pre, link).then_inc(pre_var, 1)

            def scale_in(g):
                dve.wait_ge(pre_rstd, g + 1)
                wait_past(dve, filled["xt"], g, 1, 0)
                for j in range(TILES):
                    ins = dve.tensor_scalar(xn[:, j, :], tile_of(c, g, j), pre.meanvar[:, j, 0:1],
                                            pre.rstd[:, j:j + 1], ALU.subtract, ALU.mult)
                ins.then_inc(xn_ready, 1)

            def over(t):
                return t.unsqueeze(2).broadcast_to([P, H, M])

            def heads(t):
                return t.rearrange("p (h m) -> p h m", h=H)

            def run(name, n, g, parity):
                if name == "ni":
                    if isinstance(g, int) and g == 2:
                        dve.wait_ge(c.loaded_rest, 16)
                    norm_in(g)
                if name == "si":
                    scale_in(g)
                if name == "qs":
                    dve.wait_ge(tanh_done, 2 * g + 1)
                    wait_past(dve, q_own_ready, g, H, 0)
                    dve.scalar_tensor_tensor(out=q_t[:, :], in0=tanh_q[:, :], scalar=1.0, in1=banks["prep0"],
                                             op0=ALU.add, op1=ALU.mult).then_inc(taken["q"], 1)
                if name == "ks":
                    dve.wait_ge(tanh_done, 2 * g + 2)
                    wait_past(dve, filled["A"], g, TILES, -TILES)
                    dve.scalar_tensor_tensor(out=k_t[:, parity, :], in0=tanh_k[:, :], scalar=1.0, in1=banks["prep1"],
                                             op0=ALU.add, op1=ALU.mult).then_inc(taken["k"], 1)
                if name == "zf":
                    dve.wait_ge(abs_done, 2 * g + n + 1)
                    wait_past(dve, filled["D"], g, 1, 0)
                    dve.tensor_scalar(gate_log[:, 2 * n:2 * n + 2, :], prep[:, :, D:D + SLOTS], 0.0, None, ALU.min)\
                       .then_inc(taken["vf"], 1)
                if name == "gl":
                    dve.wait_ge(taken["vf"], 2 * g + 2)
                    dve.wait_ge(log_done, g + 1)
                    dve.tensor_tensor(gate_log[:, :, :], gate_log[:, :, :], log_z[:, :, :], ALU.subtract)\
                       .then_inc(gate_log_ready, 1)
                if name == "wr":
                    dve.wait_ge(taken["G"], 2 * g + n + 1)
                    dve.wait_ge(gates_done, g + 1)
                    wait_past(dve, filled["L"], g, TILES, -TILES)
                    tiles = slice(2 * n, 2 * n + 2)
                    dve.scalar_tensor_tensor(out=write[:, parity, tiles, :], in0=gate[:, tiles, :], scalar=1.0,
                                             in1=unkeep[:, tiles, :], op0=ALU.subtract, op1=ALU.mult)\
                       .then_inc(write_ready, 1)
                if name == "Dt":
                    dve.wait_ge(filled["Dt"], g + 1)
                    dve.tensor_copy(decay[:, :, :], banks["prep2"][:, 0:16]
                                    .rearrange("p (a i) -> p a i", a=PAIRS)[:, :, 0:CHUNKS - 1]).then_inc(taken["Dt"], 1)
                if name == "S":
                    dve.wait_ge(filled["U"], g + 1)
                    dve.wait_ge(taken["Dt"], g + 1)
                    wait_past(dve, filled["o"], g, 1, -1)
                    adds = prep[:, :, :].rearrange("p b (m a c) -> p m b a c", a=PAIRS, c=2 * HK)
                    factors = decay[:, :, :].rearrange("p a i -> p i a")
                    link(dve.tensor_tensor(state[:, parity, 1], adds[:, 0, 0],
                                           factors[:, 0].unsqueeze(2).broadcast_to([P, PAIRS, 2 * HK]), ALU.mult))
                    for i in range(1, CHUNKS - 1):
                        for a in range(PAIRS):
                            before, factor = (state[:, parity, 1, a], 1.0) if i == 1 else (
                                undecayed[:, i - 1, a], decay[:, a, i - 1:i])
                            ins = dve.scalar_tensor_tensor(
                                out=undecayed[:, i, a], in0=before, scalar=factor,
                                in1=adds[:, i // 2, i % 2, a], op0=ALU.mult, op1=ALU.add)
                        if i < CHUNKS - 2:
                            link(ins)
                    ins.then_inc(taken["U"], 1)
                    dve.wait_ge(taken["U"], g + 1)
                    dve.tensor_tensor(state[:, parity, 2:], undecayed[:, 1:],
                                      factors[:, 1:].unsqueeze(3).broadcast_to([P, CHUNKS - 2, PAIRS, 2 * HK]),
                                      ALU.mult).then_inc(state_ready, 1)
                if name == "mA":
                    dve.wait_ge(filled["A"], TILES * g + n + 1)
                    wait_past(dve, filled["L"], g, TILES, n - TILES + 1)
                    dve.tensor_tensor(a_sb[:, n, :, :], banks["a"][:, :].rearrange("p (h t) -> p h t", h=H),
                                      causal_q[:, :].unsqueeze(1).broadcast_to([P, H, P]), ALU.mult)\
                       .then_inc(taken["A"], 1)
                if name == "dL":
                    dve.wait_ge(filled["L"], TILES * g + n + 1)
                    wait_past(dve, exp_done, g, TILES, n - TILES + 1)
                    ins = dve.tensor_tensor(logit[:, n, :], banks["l"][:, 0:SLOTS], keep[:, parity, n, :], ALU.mult)
                    ins.then_inc(taken["L"], 1)
                    dve.wait_ge(taken["L"], TILES * g + n + 1)
                    link(dve.tensor_reduce(top[:, :], heads(logit[:, n, :]), AX.X, ALU.max))
                    dve.tensor_tensor(heads(logit[:, n, :]), heads(logit[:, n, :]), over(top[:, :]), ALU.subtract)\
                       .then_inc(shifted_ready, 1)
                if name == "pk":
                    dve.wait_ge(exp_done, TILES * g + n + 1)
                    wait_past(dve, filled["pt"], g, TILES, n - TILES + 1)
                    dve.tensor_tensor(p_keep[:, n, :], expd[:, n, :], keep[:, parity, n, :], ALU.mult)\
                       .then_inc(p_ready, 1)
                    dve.tensor_reduce(total[:, n * H:(n + 1) * H], heads(expd[:, n, :]), AX.X, ALU.add)\
                       .then_inc(total_ready, 1)
                if name == "mB":
                    dve.wait_ge(filled["B"], TILES * g + n + 1)
                    wait_past(dve, filled["o"], g, 1, 0)
                    dve.tensor_tensor(b_sb[:, n, :, :], banks["b"][:, :].rearrange("p (h t) -> p h t", h=H),
                                      causal[:, :].unsqueeze(1).broadcast_to([P, H, P]), ALU.mult)\
                       .then_inc(taken["B"], 1)
                if name == "to":
                    take_o(g)
                if name == "so":
                    scale_o(g)
                if name == "no":
                    norm_out(g)
                if name == "ao":
                    add_out(g)

            def take_o(g):
                wide = [P, TILES * H, HK]
                dve.wait_ge(total_ready, TILES * (g + 1))
                link(dve.reciprocal(inverse[:, :], total[:, :]))
                dve.wait_ge(filled["o"], g + 1)
                dve.tensor_tensor(o_sb[:, :, :], banks["o_ps"][:, :].rearrange("p (n d) -> p n d", d=HK),
                                  inverse[:, :].unsqueeze(2).broadcast_to(wide), ALU.mult).then_inc(taken["o"], 1)
                dve.wait_ge(taken["o"], g + 1)
                link(dve.tensor_tensor(o_sq[:, :, :], o_sb[:, :, :], o_sb[:, :, :], ALU.mult))
                link(dve.tensor_reduce(o_var[:, :], o_sq[:, :, :], AX.X, ALU.add))
                dve.tensor_scalar(o_var[:, :], o_var[:, :], 1.0 / HK, EPS, ALU.mult, ALU.add).then_inc(o_var_ready, 1)

            def scale_o(g):
                dve.wait_ge(o_rstd_ready, g + 1)
                wait_past(dve, filled["ont"], g, 1, 0)
                dve.tensor_tensor(on[:, :, :], o_sb[:, :, :],
                                  o_rstd[:, :].unsqueeze(2).broadcast_to([P, TILES * H, HK]), ALU.mult)\
                   .then_inc(on_ready, 1)

            def norm_out(g):
                dve.wait_ge(taken["y"], g + 1)
                ln_stats(dve, c, lambda j: y[:, j, :], post, link).then_inc(post_var, 1)

            def add_out(g):
                dve.wait_ge(post_rstd, g + 1)
                for j in range(TILES):
                    ins = dve.tensor_scalar(y[:, j, :], y[:, j, :], post.meanvar[:, j, 0:1],
                                            post.rstd[:, j:j + 1], ALU.subtract, ALU.mult)
                link(ins)
                dve.tensor_tensor(group_of(c, g), group_of(c, g), y[:, :, :], ALU.add).then_inc(x_done, 1)

            dve.wait_ge(masks, 2)
            link(dve.memset(early[:, :], 0.0))
            link(dve.memset(between[:, :, :], 0.0))
            link(dve.memset(neg_half[:, :], -0.5))
            link(dve.memset(causal[0:CH, CH:P], 0.0))
            for i in range(2):
                link(dve.memset(early[CH * i:CH * i + CH // 2, CH * i:CH * (i + 1)], 1.0))
            flat = between[:, :, :].rearrange("p j i -> p (j i)")
            step = CHUNKS - 1 + 2
            link(dve.memset(flat[32:64, 0::step], 1.0 / NORM))
            link(dve.memset(flat[64:96, 0::step], 1.0 / NORM))
            link(dve.memset(flat[0:32, step - 1::step], 1.0 / NORM))
            link(dve.memset(flat[96:128, 1::step], 1.0 / NORM))
            link(dve.tensor_scalar(causal_q[:, :], causal[:, :], QSCALE, None, ALU.mult))
            link(dve.tensor_tensor(sum_from_mid[:, :], causal[:, :], early[:, :], ALU.subtract))
            dve.tensor_scalar(sum_from_mid[:, :], sum_from_mid[:, :], 1.0 / NORM, None, ALU.mult).then_inc(consts_ready, 1)
            dve.wait_ge(loaded, 16 * (LOADS - 1))
            dve.tensor_scalar(w_o[:, :], w_o[:, :], norm_w[:, 0:1], None, ALU.mult).then_inc(wo_ready, 1)
            dve.wait_ge(c.loaded_first, 16)
            first_steps(STEPS, run)

            def body(g, parity, ok):
                chain.turn(g)
                run_steps(STEPS, g, parity, ok, run)

            turns(dve, G, body)


def store_residual(c, out):
    with c.nc.semaphore("stored_all") as stored, c.nc.Block() as block:
        @block.sync
        def _(sp):
            sp.dma_start(out.rearrange("b (j p) d -> p (b j) d", p=P), c.x_res[:, :, :]).then_inc(stored, 16)
            sp.wait_ge(stored, 16)


def program(nc, x, out, ins, phases=(1, 2, 3, 4)):
    with ExitStack() as ctx:
        c = build_common(nc, ctx, x)
        ahead = Ahead(c, ctx, ins)
        if 1 in phases:
            gated_slots(c, ahead, *[ins["L0_attn_" + n] for n in ("Wq", "Wk", "Wv", "Wf", "g_norm_w", "Wo")])
        else:
            with nc.Block() as block:
                @block.sync
                def _(sp):
                    ahead.load(sp)
                    for transfers, loaded in ahead.groups:
                        sp.wait_ge(loaded, 16 * len(transfers))
        if 2 in phases:
            mixture_of_experts(c, ahead, ins["L0_ffn_w2"], ins["L0_ffn_sw2"])
        if 3 in phases:
            softmax_attention(c, ahead, (nc.dram_tensor("parts_scratch", [2, 2, 3, P, SEQ], BF16).ap(),
                                         nc.dram_tensor("max_scratch", [2, 3, 32, P], BF16).ap()))
        if 4 in phases:
            channel_mix(c, ahead, out)
        else:
            store_residual(c, out)


def kernel(**inputs):
    import numpy as np
    import concourse.bacc as bacc
    from concourse.bass_utils import run_bass_kernel_spmd

    nc = bacc.Bacc("TRN2", target_bir_lowering=False, num_devices=1)
    arrays, aps = {}, {}
    for name in inputs:
        a = np.ascontiguousarray(inputs[name])
        arrays["in_" + name] = a
        aps[name] = nc.dram_tensor("in_" + name, a.shape, mybir.dt.from_np(a.dtype), kind="ExternalInput").ap()
    x = aps.pop("L0_attn_x")
    out = nc.dram_tensor("out", x.shape, F32, kind="ExternalOutput").ap()
    program(nc, x, out, aps)
    return run_bass_kernel_spmd(nc, [arrays], core_ids=[0]).results[0]["out"]
```
